# Optimizing a Trainium2 kernel written in Bass

```python
import numpy as np
import jax
import jax.numpy as jnp

def _softmax(x, axis=-1):
    return jax.nn.softmax(x, axis=axis)

def _gelu(x):
    return jax.nn.gelu(x, approximate=True)

def _silu(x):
    return jax.nn.silu(x)

def _sigmoid(x):
    return jax.nn.sigmoid(x)

def _layernorm(x, axis=-1, eps=1e-05):
    m = jnp.mean(x, axis=axis, keepdims=True)
    v = jnp.var(x, axis=axis, keepdims=True)
    return (x - m) / jnp.sqrt(v + eps)

def _scatter_add(tgt, idx, src, axis=0):
    return tgt.at[idx].add(src)

def _segment_sum(src, seg, n):
    return jax.ops.segment_sum(src, seg, n)
kernel_name = 'mk_prb_d2_jaxref_r8_79e052'

def setup_inputs(seed: int=0):
    np.random.seed(seed)
    _w = jnp.asarray

    def _L0_attn_setup():
        import jax, jax.numpy as jnp
        import numpy as np
        D_INNER = 256
        D_STATE = 16
        DT_RANK = 128

        def _selective_ssm(x, A_log, D_param, x_proj_w, dt_proj_w, dt_proj_b):
            B, L, D = x.shape
            N = D_STATE
            x_dbl = jnp.einsum('bld,ed->ble', x, x_proj_w)
            dt, B_in, C_in = jnp.split(x_dbl, [DT_RANK, DT_RANK + N], axis=-1)
            delta = jax.nn.softplus(jnp.einsum('blr,dr->bld', dt, dt_proj_w) + dt_proj_b)
            A = -jnp.exp(A_log)
            xT = jnp.transpose(x, (1, 0, 2))
            dT = jnp.transpose(delta, (1, 0, 2))
            BT = jnp.transpose(B_in, (1, 0, 2))
            CT = jnp.transpose(C_in, (1, 0, 2))

            def step(h, inp):
                x_t, dt_t, B_t, C_t = inp
                dA = jnp.exp(dt_t[..., None] * A[None])
                dBx = dt_t[..., None] * B_t[:, None, :] * x_t[..., None]
                h = dA * h + dBx
                y_t = jnp.einsum('bdn,bn->bd', h, C_t) + D_param * x_t
                return (h, y_t)
            h0 = jnp.zeros((B, D, N), dtype=x.dtype)
            _, ys = jax.lax.scan(step, h0, (xT, dT, BT, CT))
            return jnp.transpose(ys, (1, 0, 2))
        key = jax.random.key(seed)
        k = jax.random.split(key, 6)
        B, L = (4, 512)
        x = jax.random.normal(k[0], (B, L, D_INNER), dtype=jnp.float32)
        A_log = jnp.log(jnp.broadcast_to(jnp.arange(1, D_STATE + 1, dtype=jnp.float32)[None, :], (D_INNER, D_STATE)))
        D_param = jnp.ones((D_INNER,), dtype=jnp.float32)
        fan_in = D_INNER
        bound = 1.0 / np.sqrt(fan_in)
        x_proj_w = jax.random.uniform(k[1], (DT_RANK + 2 * D_STATE, D_INNER), minval=-bound, maxval=bound, dtype=jnp.float32)
        bound2 = 1.0 / np.sqrt(DT_RANK)
        dt_proj_w = jax.random.uniform(k[2], (D_INNER, DT_RANK), minval=-bound2, maxval=bound2, dtype=jnp.float32)
        dt_init = jnp.exp(jax.random.uniform(k[3], (D_INNER,), dtype=jnp.float32) * (np.log(0.1) - np.log(0.001)) + np.log(0.001))
        dt_proj_b = jnp.log(jnp.exp(dt_init) - 1.0)
        return {'x': x, 'A_log': A_log, 'D_param': D_param, 'x_proj_w': x_proj_w, 'dt_proj_w': dt_proj_w, 'dt_proj_b': dt_proj_b}
    _L0_attn_in = _L0_attn_setup()

    def _L0_ffn_setup():
        import jax, jax.numpy as jnp
        import numpy as np
        B, S, H, I, E = (2, 256, 256, 176, 8)
        TOP_K = 2
        key = jax.random.key(seed)
        k0, k1, k2, k3, k4 = jax.random.split(key, 5)
        scale = float(np.sqrt(2.0 / (H + I)))
        return {'hidden_states': jax.random.normal(k0, (B, S, H), dtype=jnp.float32), 'router_w': jax.random.normal(k1, (E, H), dtype=jnp.float32) * H ** (-0.5), 'gate_w': jax.random.normal(k2, (E, I, H), dtype=jnp.float32) * scale, 'up_w': jax.random.normal(k3, (E, I, H), dtype=jnp.float32) * scale, 'down_w': jax.random.normal(k4, (E, H, I), dtype=jnp.float32) * scale}
    _L0_ffn_in = _L0_ffn_setup()

    def _L1_attn_setup():
        import jax, jax.numpy as jnp
        import numpy as np
        B, S, D_MODEL = (2, 256, 256)
        H, DS, DG, DV = (16, 64, 64, 128)
        ROPE_BASE = 10000.0
        NEG_INF = -1000000000.0

        def _rope(x, base=ROPE_BASE):
            d = x.shape[-1]
            half = d // 2
            inv_freq = 1.0 / base ** (jnp.arange(half, dtype=jnp.float32) / half)
            ang = jnp.arange(x.shape[1], dtype=jnp.float32)[:, None] * inv_freq
            cos = jnp.cos(ang)[None, :, None, :]
            sin = jnp.sin(ang)[None, :, None, :]
            x1, x2 = (x[..., :half], x[..., half:])
            return jnp.concatenate([x1 * cos - x2 * sin, x1 * sin + x2 * cos], axis=-1)
        key = jax.random.key(seed)
        ks = jax.random.split(key, 8)
        s = lambda fan_in: 1.0 / np.sqrt(fan_in)
        return {'x': jax.random.normal(ks[0], (B, S, D_MODEL), dtype=jnp.float32), 'wq_sem': jax.random.normal(ks[1], (D_MODEL, H * DS), dtype=jnp.float32) * s(D_MODEL), 'wk_sem': jax.random.normal(ks[2], (D_MODEL, H * DS), dtype=jnp.float32) * s(D_MODEL), 'wq_geo': jax.random.normal(ks[3], (D_MODEL, H * DG), dtype=jnp.float32) * s(D_MODEL), 'wk_geo': jax.random.normal(ks[4], (D_MODEL, H * DG), dtype=jnp.float32) * s(D_MODEL), 'wv': jax.random.normal(ks[5], (D_MODEL, H * DV), dtype=jnp.float32) * s(D_MODEL), 'wo': jax.random.normal(ks[6], (H * DV, D_MODEL), dtype=jnp.float32) * s(H * DV), 'gate_logit': jax.random.normal(ks[7], (H,), dtype=jnp.float32)}
    _L1_attn_in = _L1_attn_setup()

    def _L1_ffn_setup():
        import jax, jax.numpy as jnp
        import numpy as np
        TOP_K = 4
        key = jax.random.key(seed)
        ks = jax.random.split(key, 8)
        B, S, H = (1, 128, 256)
        E, I = (60, 176)
        I_SH = 704
        s = 0.02
        return {'hidden_states': jax.random.normal(ks[0], (B, S, H), jnp.float32), 'gate_w': jax.random.normal(ks[1], (E, H), jnp.float32) * s, 'shared_gate_w': jax.random.normal(ks[2], (1, H), jnp.float32) * s, 'w13': jax.random.normal(ks[3], (E, 2 * I, H), jnp.float32) * s, 'w2': jax.random.normal(ks[4], (E, H, I), jnp.float32) * s, 'se_gate_up_w': jax.random.normal(ks[5], (2 * I_SH, H), jnp.float32) * s, 'se_down_w': jax.random.normal(ks[6], (H, I_SH), jnp.float32) * s}
    _L1_ffn_in = _L1_ffn_setup()
    _d = {'L0_attn_x': _L0_attn_in['x'], 'L0_attn_A_log': _L0_attn_in['A_log'], 'L0_attn_D_param': _L0_attn_in['D_param'], 'L0_attn_x_proj_w': _L0_attn_in['x_proj_w'], 'L0_attn_dt_proj_w': _L0_attn_in['dt_proj_w'], 'L0_attn_dt_proj_b': _L0_attn_in['dt_proj_b'], 'L0_ffn_router_w': _L0_ffn_in['router_w'], 'L0_ffn_gate_w': _L0_ffn_in['gate_w'], 'L0_ffn_up_w': _L0_ffn_in['up_w'], 'L0_ffn_down_w': _L0_ffn_in['down_w'], 'L1_attn_wq_sem': _L1_attn_in['wq_sem'], 'L1_attn_wk_sem': _L1_attn_in['wk_sem'], 'L1_attn_wq_geo': _L1_attn_in['wq_geo'], 'L1_attn_wk_geo': _L1_attn_in['wk_geo'], 'L1_attn_wv': _L1_attn_in['wv'], 'L1_attn_wo': _L1_attn_in['wo'], 'L1_attn_gate_logit': _L1_attn_in['gate_logit'], 'L1_ffn_gate_w': _L1_ffn_in['gate_w'], 'L1_ffn_shared_gate_w': _L1_ffn_in['shared_gate_w'], 'L1_ffn_w13': _L1_ffn_in['w13'], 'L1_ffn_w2': _L1_ffn_in['w2'], 'L1_ffn_se_gate_up_w': _L1_ffn_in['se_gate_up_w'], 'L1_ffn_se_down_w': _L1_ffn_in['se_down_w']}
    _x0 = _d['L0_attn_x']
    _d['L0_attn_x'] = jax.random.normal(jax.random.fold_in(jax.random.key(seed), 1), (2, 1024, 256), dtype=_x0.dtype)
    del _x0
    return _d

def reference(L0_attn_x, L0_attn_A_log, L0_attn_D_param, L0_attn_x_proj_w, L0_attn_dt_proj_w, L0_attn_dt_proj_b, L0_ffn_router_w, L0_ffn_gate_w, L0_ffn_up_w, L0_ffn_down_w, L1_attn_wq_sem, L1_attn_wk_sem, L1_attn_wq_geo, L1_attn_wk_geo, L1_attn_wv, L1_attn_wo, L1_attn_gate_logit, L1_ffn_gate_w, L1_ffn_shared_gate_w, L1_ffn_w13, L1_ffn_w2, L1_ffn_se_gate_up_w, L1_ffn_se_down_w):

    def _L0_attn_ref(x, A_log, D_param, x_proj_w, dt_proj_w, dt_proj_b):
        import jax, jax.numpy as jnp
        import numpy as np
        D_INNER = 256
        D_STATE = 16
        DT_RANK = 128

        def _selective_ssm(x, A_log, D_param, x_proj_w, dt_proj_w, dt_proj_b):
            B, L, D = x.shape
            N = D_STATE
            x_dbl = jnp.einsum('bld,ed->ble', x, x_proj_w)
            dt, B_in, C_in = jnp.split(x_dbl, [DT_RANK, DT_RANK + N], axis=-1)
            delta = jax.nn.softplus(jnp.einsum('blr,dr->bld', dt, dt_proj_w) + dt_proj_b)
            A = -jnp.exp(A_log)
            xT = jnp.transpose(x, (1, 0, 2))
            dT = jnp.transpose(delta, (1, 0, 2))
            BT = jnp.transpose(B_in, (1, 0, 2))
            CT = jnp.transpose(C_in, (1, 0, 2))

            def step(h, inp):
                x_t, dt_t, B_t, C_t = inp
                dA = jnp.exp(dt_t[..., None] * A[None])
                dBx = dt_t[..., None] * B_t[:, None, :] * x_t[..., None]
                h = dA * h + dBx
                y_t = jnp.einsum('bdn,bn->bd', h, C_t) + D_param * x_t
                return (h, y_t)
            h0 = jnp.zeros((B, D, N), dtype=x.dtype)
            _, ys = jax.lax.scan(step, h0, (xT, dT, BT, CT))
            return jnp.transpose(ys, (1, 0, 2))
        return _selective_ssm(x, A_log, D_param, x_proj_w, dt_proj_w, dt_proj_b)

    def _L0_ffn_ref(hidden_states, router_w, gate_w, up_w, down_w):
        import jax, jax.numpy as jnp
        import numpy as np
        B, S, H, I, E = (2, 256, 256, 176, 8)
        TOP_K = 2
        b, s, h = hidden_states.shape
        e = router_w.shape[0]
        x = hidden_states.reshape(-1, h)
        logits = jnp.einsum('th,eh->te', x, router_w)
        top_vals, top_idx = jax.lax.top_k(logits, TOP_K)
        top_w = jax.nn.softmax(top_vals, axis=-1)
        expert = top_idx[:, 0]
        weight = top_w[:, 0]
        gate = jnp.einsum('th,eih->eti', x, gate_w)
        up = jnp.einsum('th,eih->eti', x, up_w)
        act = jax.nn.silu(gate) * up
        out_e = jnp.einsum('eti,ehi->eth', act, down_w)
        combine = jax.nn.one_hot(expert, e, dtype=x.dtype) * weight[:, None]
        out = jnp.einsum('eth,te->th', out_e, combine)
        return out.reshape(b, s, h)

    def _L1_attn_ref(x, wq_sem, wk_sem, wq_geo, wk_geo, wv, wo, gate_logit):
        import jax, jax.numpy as jnp
        import numpy as np
        B, S, D_MODEL = (2, 256, 256)
        H, DS, DG, DV = (16, 64, 64, 128)
        ROPE_BASE = 10000.0
        NEG_INF = -1000000000.0

        def _rope(x, base=ROPE_BASE):
            d = x.shape[-1]
            half = d // 2
            inv_freq = 1.0 / base ** (jnp.arange(half, dtype=jnp.float32) / half)
            ang = jnp.arange(x.shape[1], dtype=jnp.float32)[:, None] * inv_freq
            cos = jnp.cos(ang)[None, :, None, :]
            sin = jnp.sin(ang)[None, :, None, :]
            x1, x2 = (x[..., :half], x[..., half:])
            return jnp.concatenate([x1 * cos - x2 * sin, x1 * sin + x2 * cos], axis=-1)
        b, sl, _ = x.shape
        qs = (x @ wq_sem).reshape(b, sl, H, DS)
        ksem = (x @ wk_sem).reshape(b, sl, H, DS)
        qg = _rope((x @ wq_geo).reshape(b, sl, H, DG))
        kg = _rope((x @ wk_geo).reshape(b, sl, H, DG))
        v = (x @ wv).reshape(b, sl, H, DV)
        sem_scale = 1.0 / np.sqrt(DS)
        geo_scale = 1.0 / np.sqrt(DG)
        sem_scores = jnp.einsum('bqhd,bkhd->bhqk', qs, ksem) * sem_scale
        geo_scores = jnp.einsum('bqhd,bkhd->bhqk', qg, kg) * geo_scale
        g = jax.nn.sigmoid(gate_logit)[None, :, None, None]
        scores = g * sem_scores + (1.0 - g) * geo_scores
        causal = jnp.tril(jnp.ones((sl, sl), dtype=bool))
        scores = jnp.where(causal[None, None], scores, NEG_INF)
        attn = jax.nn.softmax(scores, axis=-1)
        out = jnp.einsum('bhqk,bkhd->bqhd', attn, v).reshape(b, sl, H * DV)
        return out @ wo

    def _L1_ffn_ref(hidden_states, gate_w, shared_gate_w, w13, w2, se_gate_up_w, se_down_w):
        import jax, jax.numpy as jnp
        import numpy as np
        TOP_K = 4
        orig_shape = hidden_states.shape
        E, H = gate_w.shape
        I = w2.shape[2]
        x = hidden_states.reshape(-1, H)
        M = x.shape[0]
        gu = x @ se_gate_up_w.T
        I_sh = se_down_w.shape[1]
        shared = jax.nn.silu(gu[:, :I_sh]) * gu[:, I_sh:] @ se_down_w.T
        shared = shared * jax.nn.sigmoid(x @ shared_gate_w.T)
        logits = x @ gate_w.T
        probs = jax.nn.softmax(logits.astype(jnp.float32), axis=-1)
        weights, sel = jax.lax.top_k(probs, TOP_K)
        cw = jnp.zeros((M, E), jnp.float32).at[jnp.arange(M)[:, None], sel].add(weights)

        def step(acc, ews):
            w13_e, w2_e, cw_e = ews
            gu_e = x @ w13_e.T
            h = jax.nn.silu(gu_e[:, :I]) * gu_e[:, I:]
            return (acc + cw_e[:, None] * (h @ w2_e.T), None)
        sparse, _ = jax.lax.scan(step, jnp.zeros((M, H), jnp.float32), (w13, w2, cw.T))
        return (shared + sparse).reshape(orig_shape)
    x = L0_attn_x
    xn = _layernorm(x, axis=-1)
    x = x + _L0_attn_ref(xn, L0_attn_A_log, L0_attn_D_param, L0_attn_x_proj_w, L0_attn_dt_proj_w, L0_attn_dt_proj_b) + _L0_ffn_ref(xn, L0_ffn_router_w, L0_ffn_gate_w, L0_ffn_up_w, L0_ffn_down_w)
    xn = _layernorm(x, axis=-1)
    x = x + _L1_attn_ref(xn, L1_attn_wq_sem, L1_attn_wk_sem, L1_attn_wq_geo, L1_attn_wk_geo, L1_attn_wv, L1_attn_wo, L1_attn_gate_logit) + _L1_ffn_ref(xn, L1_ffn_gate_w, L1_ffn_shared_gate_w, L1_ffn_w13, L1_ffn_w2, L1_ffn_se_gate_up_w, L1_ffn_se_down_w)
    return x

_drawn_inputs = setup_inputs


def setup_inputs(seed=0):
    import zlib

    import numpy as np

    out = dict(_drawn_inputs(seed))
    spreads = {'L0_attn_D_param': (1.0, 0.2)}
    factors = {'L0_attn_dt_proj_w': 3.974,
     'L1_attn_gate_logit': 33.864,
     'L1_ffn_gate_w': 8.0,
     'L1_ffn_shared_gate_w': 8.0,
     'L1_ffn_w13': 8.0,
     'L1_ffn_w2': 8.0,
     'L1_ffn_se_gate_up_w': 8.0,
     'L1_ffn_se_down_w': 8.0,
     'L1_attn_wq_sem': 8.0,
     'L1_attn_wk_sem': 8.0,
     'L1_attn_wq_geo': 8.0,
     'L1_attn_wk_geo': 8.0,
     'L1_attn_wv': 5.871,
     'L1_attn_wo': 5.811}
    for name, (base, spread) in spreads.items():
        noise = np.random.default_rng([zlib.crc32(name.encode()), seed]).standard_normal(out[name].shape)
        drawn = base * np.exp(spread * noise) if base else spread * noise
        out[name] = jnp.asarray(drawn.astype(out[name].dtype))
    for name, factor in factors.items():
        out[name] = (out[name] * factor).astype(out[name].dtype)
    return out
```

```python
from contextlib import ExitStack

import numpy as np

import concourse.bass as bass
from concourse import mybir

F32 = mybir.dt.float32
F32R = mybir.dt.float32r
BF16 = mybir.dt.bfloat16
I32 = mybir.dt.int32
U32 = mybir.dt.uint32
ALU = mybir.AluOpType
ACT = mybir.ActivationFunctionType
AX = mybir.AxisListType

P = 128
BATCH, SEQ, D = 2, 1024, 256
T = BATCH * SEQ
NT = T // P
DC = D // P
NG = 4
GT = NT // NG
EPS = 1e-5

STATES, RANK = 16, 128
XD = RANK + 2 * STATES

INNER = 176
IC = INNER // 2
E0, E1 = 8, 60
K1 = 4
SHARED = 4
TILES0 = T // P + E0
TILES1 = T * K1 // P + E1
ALL1 = TILES1 + SHARED * NT
RING = 4
GU_BANK, DN_BANK = (5, 3), (7, 2)

HEADS, QK = 16, 64


class Route:
    def __init__(self, tiles_n, slots, result, etab_dram, w13_dram, w2_dram, routed, n_weights):
        self.tiles_n, self.routed, self.n_weights = tiles_n, routed, n_weights
        self.slots, self.result, self.etab_dram = slots, result, etab_dram
        self.w13_dram, self.w2_dram = w13_dram, w2_dram


def log1p_coefficients(n):
    z = (np.cos(np.pi * (np.arange(64) + 0.5) / 64) + 1) / 18
    s = np.sqrt(z)
    return [float(2 * c) for c in np.polynomial.chebyshev.Chebyshev.fit(z, np.arctanh(s) / s, n - 1, domain=[0, 1 / 9])
            .convert(kind=np.polynomial.Polynomial).coef]


def build(nc, x_in, a_log, d_param, xproj, dtproj, dt_bias, router0, w13_0, w2_0,
          router1, w13_1, w2_1, wqkv, wo_h, gate_logit, rope, out, only0=False):
    ctx = ExitStack()
    with ctx:
        def sb(name, shape, dt=F32):
            return ctx.enter_context(nc.sbuf_tensor(name, shape, dt))

        def sem(name):
            return ctx.enter_context(nc.semaphore(name))

        def dram(name, shape, dt=F32):
            return nc.dram_tensor(name, shape, dt).ap()

        ps = ctx.enter_context(nc.psum_tensor("ps", [P, 8, 512], F32))

        bc_rows = dram("bc_rows", [2 * STATES, T])
        sorted1 = dram("sorted1", [TILES1 * P, D])
        result1 = dram("result1", [TILES1 * P, D])
        etab1 = dram("etab1", [P, 1], I32)
        sorted0 = dram("sorted0", [TILES0 * P, D])
        result0 = dram("result0", [TILES0 * P, D])
        etab0 = dram("etab0", [P, 1], I32)
        xr = sb("xr", [P, NT, D])
        xn = sb("xn", [P, NT, D])
        ident = sb("ident", [P, P])
        ident_b = sb("ident_b", [P, P], BF16)
        before = sb("before", [P, P], BF16)
        ones_b = sb("ones_b", [P, P], BF16)
        zero_b = sb("zero_b", [P, P], BF16)
        iota_e = sb("iota_e", [P, E1])
        iota_p = sb("iota_p", [P, 1])
        neg_half = sb("neg_half", [P, NT])
        stat = sb("stat", [P, 4, NT])

        base0 = ExitStack()

        def sb0(name, shape, dt=F32):
            return base0.enter_context(nc.sbuf_tensor(name, shape, dt))

        zeros = sb0("zeros", [P, 2048])
        xnT = sb0("xnT", [P, DC, T])
        delta = sb0("delta", [P, DC, T])
        dx = sb0("dx", [P, DC, T])
        xpw = sb0("xpw", [P, DC, XD])
        dtw = sb0("dtw", [P, D])
        dtb = sb0("dtb", [P, DC])
        alog = sb0("alog", [P, DC, STATES])
        aneg = sb0("aneg", [P, DC, STATES])
        dpar = sb0("dpar", [P, DC])
        rw0 = sb0("rw0", [P, DC, E0])
        decay = sb0("decay", [P, 2, DC, SEQ])
        state = sb0("state", [P, 2, DC, SEQ])
        brow = sb0("brow", [P, 2, SEQ])
        crow = sb0("crow", [P, 2, SEQ])
        sq = state[:, 0].rearrange("p c t -> p (c t)")
        sp_x = decay[:, 0].rearrange("p c t -> p (c t)")
        sp_e = decay[:, 1].rearrange("p c t -> p (c t)")
        sp_s = state[:, 0].rearrange("p c t -> p (c t)")
        sp_z = state[:, 1].rearrange("p c t -> p (c t)")
        dtT = brow[:, :, :].rearrange("p a t -> p (a t)")
        bcT = crow[0:2 * STATES, :, :].rearrange("p a t -> p (a t)")

        def ring_buffers(r, n, alloc):
            r.w13 = alloc(f'w13r{n}', [P, RING, DC, 2 * INNER])
            r.w2 = alloc(f'w2r{n}', [IC, RING, 2, D])
            r.xs = alloc(f'xs{n}', [P, RING, D])
            r.xt = alloc(f'xt{n}', [P, 2, D])
            r.th = alloc(f'th{n}', [P, 2, INNER])
            r.ga = alloc(f'ga{n}', [P, 2, INNER])
            r.hh = alloc(f'hh{n}', [P, 2, INNER])
            r.ht = alloc(f'ht{n}', [IC, 2, 2, P])
            r.yy = alloc(f'yy{n}', [P, RING, D])
            r.got = alloc(f'got{n}', [P, 4, D])

        def route_buffers(r, n, e, k, alloc, el, keep_alloc):
            r.E = e
            r.K = k
            r.name = n
            r.EL = el
            r.logit = alloc(f'logit{n}', [P, NT, el])
            r.top = alloc(f'top{n}', [P, NT, 8])
            r.idx = alloc(f'idx{n}', [P, NT, 8], U32)
            r.idxf = alloc(f'idxf{n}', [P, NT, 8])
            r.hot = alloc(f'hot{n}', [P, k, e, NT], BF16)
            r.m = alloc(f'm{n}', [P, e, NT], BF16)
            r.keep = alloc(f'keep{n}', [P, e, NT], BF16)
            r.cum = alloc(f'cum{n}', [P, e, NT], BF16)
            r.cumx = alloc(f'cumx{n}', [P, e, NT], BF16)
            r.rank = alloc(f'rank{n}', [P, e, NT])
            r.prod = alloc(f'prod{n}', [P, e, NT])
            r.cnti = alloc(f'cnti{n}', [P, e], I32)
            r.tiles = alloc(f'tiles{n}', [P, e])
            r.upto = alloc(f'upto{n}', [P, e])
            r.base = alloc(f'base{n}', [P, e])
            r.slotf = alloc(f'slotf{n}', [P, k, NT])
            r.slot = keep_alloc(f'slot{n}', [P, k, NT], U32)
            r.weight = keep_alloc(f'weight{n}', [P, NT, 8])
            r.ecol = alloc(f'ecol{n}', [P, 2])
            r.ecoli = keep_alloc(f'ecoli{n}', [P, 1], I32)
            r.ecmp = alloc(f'ecmp{n}', [P, e])
            r.logits_ready = sem(f'logits_ready{n}')
            r.step = sem(f'route_step{n}')
            r.ranks_ready = sem(f'ranks_ready{n}')
            r.m_ready = sem(f'm_ready{n}')
            r.slots_ready = sem(f'slots_ready{n}')
            r.scattered = sem(f'scattered{n}')
            r.tiles_known = sem(f'tiles_known{n}')
            r.table_stored = sem(f'table_stored{n}')
            r.table_loaded = sem(f'table_loaded{n}')
            r.zeroed = sem(f'zeroed{n}')
            r.etab = keep_alloc(f'etabrow{n}', [1, 192], I32)
            r.x_loaded = [sem(f'tokens_loaded{n}_{q}') for q in range(RING)]
            r.w13_loaded = [sem(f'w13_loaded{n}_{q}') for q in range(RING)]
            r.w2_loaded = [sem(f'w2_loaded{n}_{q}') for q in range(RING)]
            r.shared_added = sem(f'shared_added{n}')
            r.xt_ready = sem(f'xt_ready{n}')
            r.xt_copied = sem(f'xt_copied{n}')
            r.gu_ready = sem(f'gu_ready{n}')
            r.tanh_ready = sem(f'tanh_ready{n}')
            r.act_step = sem(f'gated{n}')
            r.h_done = sem(f'h_done{n}')
            r.ht_ready = sem(f'ht_ready{n}')
            r.ht_copied = sem(f'ht_copied{n}')
            r.dn_done = sem(f'dn_done{n}')
            r.y_copied = sem(f'y_copied{n}')
            r.stored = [sem(f'y_stored{n}_{q}') for q in range(RING)]
            r.gathered = [sem(f'gathered{n}_{q}') for q in range(4)]
            r.added = sem(f'added{n}')

        R0 = Route(TILES0, sorted0, result0, etab0, w13_0, w2_0, TILES0, E0)
        route_buffers(R0, 0, E0, 1, sb0, E0, sb0)
        ring_buffers(R0, 0, sb0)

        base0.close()

        def sbk(name, shape, dt=F32):
            return ctx1.enter_context(nc.sbuf_tensor(name, shape, dt))
        ctx1 = ExitStack()
        xnr = sbk("xnr", [P, DC, T], F32R)
        xnl = sbk("xnl", [P, DC, T], F32R)
        gsc = sbk("gsc", [P, 2, HEADS])
        rowsum = sbk("rowsum", [P, 2, 8])
        rinv = sbk("rinv", [P, 2, 8])
        negmax = sbk("negmax", [P, 2, 8])
        rw1 = sbk("rw1", [P, DC, E1 + 1])
        keep1 = {}

        def alloc_keep1(name, shape, dt=F32):
            return sbk(name, shape, dt)
        kslot = alloc_keep1

        att = ExitStack()

        def sba(name, shape, dt=F32):
            return att.enter_context(nc.sbuf_tensor(name, shape, dt))
        slot_w = kslot("slot1", [P, K1, NT], U32)
        weight_w = kslot("weight1", [P, NT, 8])
        ecoli_w = kslot("ecoli1", [P, 1], I32)
        etab_w = kslot("etabrow1", [1, 192], I32)
        kept = {"slot1": slot_w, "weight1": weight_w, "ecoli1": ecoli_w, "etabrow1": etab_w}
        wraw = sba("wraw", [P, 3, DC, P])
        wr = sba("wr", [P, 3, DC, P], F32R)
        wl = sba("wl", [P, 3, DC, P], F32R)
        woraw = sba("woraw", [P, D])
        wor = sba("wor", [P, D], F32R)
        wol = sba("wol", [P, D], F32R)
        rope_t = sba("rope_t", [P, 2, SEQ])
        qkr = sba("qkr", [P, 2, 2, SEQ], F32R)
        qkl = sba("qkl", [P, 2, 2, SEQ], F32R)
        vr = sba("vr", [P, 2, 8, P], F32R)
        vl = sba("vl", [P, 2, 8, P], F32R)
        otr = sba("otr", [P, 512], F32R)
        otl = sba("otl", [P, 512], F32R)
        t1 = sba("t1", [P, 2, 512])
        sw = sba("sw", [P, 2, 512])
        maskb = sba("maskb", [P, P], BF16)
        over = ExitStack()

        def sbo(name, shape, dt=F32):
            return over.enter_context(nc.sbuf_tensor(name, shape, dt))
        pb = sbo("pb", [P, 2, SEQ])
        ptr = sbo("ptr", [P, 8, 512], F32R)
        ptl = sbo("ptl", [P, 8, 512], F32R)
        over.close()
        over2 = ExitStack()
        xnT1 = over2.enter_context(nc.sbuf_tensor("xnT1", [P, DC, T], F32))
        R1 = Route(ALL1, sorted1, result1, etab1, w13_1, w2_1, TILES1, E1 + SHARED)
        route_buffers(R1, 1, E1, K1, lambda n, sh, dt=F32: over2.enter_context(nc.sbuf_tensor(n, sh, dt)), E1 + 1,
                            lambda n, sh, dt=F32: kept[n])
        over2.close()
        att.close()
        over3 = ExitStack()
        ring_buffers(R1, 1, lambda n, sh, dt=F32: over3.enter_context(nc.sbuf_tensor(n, sh, dt)))
        over3.close()
        ctx1.close()

        s_x = [sem(f"x_loaded{g}") for g in range(NG)]
        s_par = sem("params_loaded")
        s_const = sem("consts_made")
        s_ln = sem("ln_step")
        s_sq = sem("squares_ready")
        s_var = sem("variance_ready")
        s_rstd = sem("rstd_ready")
        s_cen = sem("centred")
        s_xn = sem("xn_ready")
        s_xnT_ps = sem("xnT_in_psum")
        s_xnT = sem("xnT_ready")
        s_xd = sem("xdbl_in_psum")
        s_xdc = sem("xdbl_copied")
        s_bc = sem("bc_rows_stored")
        s_dp = sem("dt_in_psum")
        s_dpc = sem("dt_biased")
        s_sp = sem("softplus_step")
        s_spa = sem("softplus_act_step")
        s_delta = sem("delta_ready")
        s_row = [sem(f"rows_loaded{r}") for r in range(2)]
        s_dec = sem("decay_ready")
        s_dbx = sem("input_term_ready")
        s_scan = sem("scanned")
        s_hc = sem("hc_ready")
        s_ysum = sem("y_summed")
        s_aneg = sem("a_ready")
        s_yT = sem("yT_ready")
        s_yT_ps = sem("y_rows_in_psum")
        s_yadd = sem("y_rows_added")
        s_out = sem("out_stored")

        s_mask = sem("mask_made")
        s_par1 = sem("params1_loaded")
        s_gate = sem("gate_step")
        s_gact = sem("gate_exp")
        s_xnT1_ps = sem("xn1T_in_psum")
        s_xnT1 = sem("xn1T_copied")
        s_split = sem("xn1_split")
        s_wraw = sem("head_weights_loaded")
        s_wsc = sem("head_weights_scaled")
        s_ws = sem("head_weights_split")
        s_wor = sem("wo_loaded")
        s_wos = sem("wo_split")
        s_rnd = sem("weights_rounded")
        s_S = sem("scores_ready")
        s_max = sem("max_ready")
        s_exp = sem("exp_ready")
        s_T = sem("probs_transposed")
        s_pr = sem("probs_rounded")
        s_pl = sem("probs_split")
        s_b6 = sem("bank6_filled")
        s_a6 = sem("bank6_rounded")
        s_e6 = sem("bank6_taken")
        s_b7 = sem("bank7_filled")
        s_a7 = sem("bank7_rounded")
        s_e7 = sem("bank7_taken")
        s_t2 = sem("rotated")
        s_rot = sem("rotation_added")
        s_qr = sem("qk_rounded")
        s_ql = sem("qk_split")
        s_rinv = sem("sums_inverted")
        s_w1 = sem("weights1_step")
        s_w1a = sem("weights1_exp")

        COEF = log1p_coefficients(5)

        def w(eng, s, value):
            if not isinstance(value, int) or value > 0:
                eng.wait_ge(s, value)

        def route_dve(v, r):
            n = [0]

            def step(ins):
                n[0] += 1
                ins.then_inc(r.step, 1)
                v.wait_ge(r.step, n[0])

            v.wait_ge(r.logits_ready, 1)
            for i in range(NT):
                last = v.tensor_copy(r.logit[:, i, :], ps[:, 4 + i // 8, (i % 8) * r.EL:(i % 8 + 1) * r.EL])
            step(last)
            for i in range(NT):
                last = v.max(r.top[:, i, :], r.logit[:, i, 0:r.E])
            step(last)
            for i in range(NT):
                last = v.max_index(r.idx[:, i, :], r.top[:, i, :], r.logit[:, i, 0:r.E])
            step(last)
            step(v.tensor_copy(r.idxf[:], r.idx[:]))
            for k in range(r.K):
                last = v.tensor_tensor(r.hot[:, k], iota_e[:, 0:r.E].unsqueeze(2).to_broadcast([P, r.E, NT]),
                                       r.idxf[:, :, k].unsqueeze(1).to_broadcast([P, r.E, NT]), ALU.is_equal)
            step(last)
            if r.K == 1:
                step(v.tensor_copy(r.m[:], r.hot[:, 0]))
            else:
                step(v.tensor_tensor(r.m[:], r.hot[:, 0], r.hot[:, 1], ALU.add))
                for k in range(2, r.K):
                    step(v.tensor_tensor(r.m[:], r.m[:], r.hot[:, k], ALU.add))
            step(v.memset(r.keep[:], 1.0))
            step(v.memset(r.keep[:, :, 0:1], 0.0))
            step(v.tensor_tensor_scan(r.cum[:].rearrange("p e i -> p (e i)"), r.keep[:].rearrange("p e i -> p (e i)"),
                                      r.m[:].rearrange("p e i -> p (e i)"), 0.0, ALU.mult, ALU.add))
            v.tensor_tensor(r.cumx[:], r.cum[:], r.m[:], ALU.subtract).then_inc(r.m_ready, 1)
            v.wait_ge(r.ranks_ready, 1)
            step(v.tensor_scalar(r.cnti[:], ps[:, 6, 0:r.E], float(P - 1), None, ALU.add))
            step(v.tensor_scalar(r.cnti[:], r.cnti[:], 7, None, ALU.arith_shift_right))
            step(v.tensor_copy(r.tiles[:], r.cnti[:]))
            step(v.tensor_tensor_scan(r.upto[:], r.ecmp[:], r.tiles[:], 0.0, ALU.mult, ALU.add))
            step(v.tensor_tensor(r.base[:], r.upto[:], r.tiles[:], ALU.subtract))
            step(v.tensor_scalar(r.base[:], r.base[:], float(P), None, ALU.mult))
            half = r.E // 2
            for c in range(2):
                last = v.tensor_tensor(r.rank[:, c * half:(c + 1) * half],
                                       ps[:, 4 + c, 0:half * NT].rearrange("p (e i) -> p e i", i=NT),
                                       r.base[:, c * half:(c + 1) * half].unsqueeze(2).to_broadcast([P, half, NT]), ALU.add)
            step(last)
            for k in range(r.K):
                step(v.tensor_tensor(r.prod[:], r.rank[:], r.hot[:, k], ALU.mult))
                step(v.tensor_reduce(r.slotf[:, k, :], r.prod[:].rearrange("p e i -> p i e"), AX.X, ALU.add))
            v.tensor_copy(r.slot[:], r.slotf[:]).then_inc(r.slots_ready, 1)
            step(v.tensor_scalar(r.ecmp[:], r.upto[:], iota_p[:, 0:1], None, ALU.is_le))
            step(v.tensor_reduce(r.ecol[:, 0:1], r.ecmp[:], AX.X, ALU.add))
            step(v.tensor_scalar(r.ecol[:, 1:2], r.ecol[:, 0:1], float(r.E - 1), None, ALU.min))
            v.tensor_copy(r.ecoli[:], r.ecol[:, 1:2]).then_inc(r.tiles_known, 1)
            return step

        def route_pe(pe, r):
            pe.wait_ge(r.m_ready, 1)
            half = r.E // 2
            for c in range(2):
                o = ps[:, 4 + c, 0:half * NT]
                mm = r.m[:, c * half:(c + 1) * half].rearrange("p e i -> p (e i)")
                cx = r.cumx[:, c * half:(c + 1) * half].rearrange("p e i -> p (e i)")
                pe.matmul(o, before[:], mm, start=True, stop=False)
                pe.matmul(o, ones_b[:], cx, start=False, stop=True)
            pe.matmul(ps[:, 6, 0:r.E], ones_b[:], r.cum[:, :, NT - 1], start=True, stop=True).then_inc(r.ranks_ready, 1)

        def route_pool(g, r):
            g.wait_ge(r.zeroed, 16 * r.zero_dmas)
            g.wait_ge(r.slots_ready, 1)
            for k in range(r.K):
                for i in range(NT):
                    g.indirect_dma_start(r.slots, bass.IndirectOffsetOnAxis(ap=r.slot[:, k, i:i + 1], axis=0),
                                         xn[:, i, :], None).then_inc(r.scattered, 16)

        def route_sp(sp, r):
            sp.wait_ge(r.tiles_known, 1)
            sp.dma_start(r.etab_dram, r.ecoli[:]).then_inc(r.table_stored, 16)
            sp.wait_ge(r.table_stored, 16)
            sp.dma_start(r.etab[0:1, 0:r.routed], r.etab_dram[0:r.routed, :].rearrange("p o -> o p")).then_inc(r.table_loaded, 16)
            sp.wait_ge(r.table_loaded, 16)
            sp.wait_ge(r.scattered, 16 * NT * r.K)

        def zero_fill(sp, r):
            rows = 1024
            total = r.routed * P
            r.zero_dmas = -(-total // rows)
            for q in range(r.zero_dmas):
                n = min(rows, total - q * rows)
                sp.dma_start(r.slots[q * rows:q * rows + n, :].rearrange("(p a) d -> p (a d)", p=P),
                             zeros[:, 0:n * D // P]).then_inc(r.zeroed, 16)

        def tile_steps(eng, r, fn):
            first_shared, end = r.routed // RING, r.tiles_n // RING

            def out(i):
                for q in range(RING):
                    def kind(a, s=i * RING + q):
                        return None if s < a or s - a >= r.tiles_n else 'routed' if s - a < r.routed else 'shared'
                    fn(i, q, kind)

            def loop(lo, hi, what):
                with eng.Fori(lo, hi) as i:
                    for q in range(RING):
                        fn(i, q, lambda a: what)
            out(0)
            out(1)
            loop(2, first_shared, 'routed')
            if end > first_shared:
                out(first_shared)
                out(first_shared + 1)
                loop(first_shared + 2, end, 'shared')
            out(end)
            out(end + 1)

        def experts_sp(sp, r):
            def fn(i, q, kind):
                s = i * RING + q
                if kind(0):
                    if kind(0) == 'routed':
                        e = sp.value_load(r.etab[0:1, bass.ds(s, 1)], min_val=0, max_val=r.n_weights - 1)
                    w(sp, r.gu_ready, s - 3)
                    if kind(0) == 'routed':
                        sp.dma_start(r.xs[:, q], r.slots[bass.ds(s * P, P), :]).then_inc(r.x_loaded[q], 16)
                        sp.dma_start(r.w13[:, q], r.w13_dram[bass.ds(e, 1)].rearrange("o p c n -> (o p) c n")).then_inc(r.w13_loaded[q], 16)
                    else:
                        token_tile = i - r.routed // RING
                        sp.dma_start(r.xs[:, q], xn[:, bass.ds(token_tile, 1), :].rearrange("p o d -> p (o d)")).then_inc(r.x_loaded[q], 16)
                        if isinstance(i, int) and s < r.routed + SHARED:
                            sp.dma_start(r.w13[:, q], r.w13_dram[r.E + q]).then_inc(r.w13_loaded[q], 16)
                b = (q - 2) % RING
                if kind(2) == 'routed':
                    e = sp.value_load(r.etab[0:1, bass.ds(s - 2, 1)], min_val=0, max_val=r.n_weights - 1)
                    w(sp, r.dn_done, s - 5)
                    sp.dma_start(r.w2[:, b], r.w2_dram[bass.ds(e, 1)].rearrange("o p c n -> (o p) c n")).then_inc(r.w2_loaded[b], 16)
                elif kind(2) == 'shared' and isinstance(i, int) and s - 2 < r.routed + SHARED:
                    sp.wait_ge(r.dn_done, s - 5)
                    sp.dma_start(r.w2[:, b], r.w2_dram[r.E + b]).then_inc(r.w2_loaded[b], 16)
                if kind(7) == 'routed':
                    b = (q - 7) % RING
                    sp.wait_ge(r.y_copied, s - 6)
                    sp.dma_start(r.result[bass.ds((s - 7) * P, P), :], r.yy[:, b]).then_inc(r.stored[b], 16)
            tile_steps(sp, r, fn)

        def experts_pe(pe, r):
            uses = r.routed // RING

            def fn(i, q, kind):
                s = i * RING + q
                if kind(0):
                    pe.wait_ge(r.x_loaded[q], (i + 1) * 16)
                    w(pe, r.xt_copied, s)
                    for c in range(DC):
                        last = pe.transpose(ps[:, 4, c * P:(c + 1) * P], r.xs[:, q, c * P:(c + 1) * P], ident[:])
                    last.then_inc(r.xt_ready, 1)
                if kind(1):
                    b = (q - 1) % RING
                    turn = i + (q - 1) // RING
                    if kind(1) == 'routed' or isinstance(i, int) and turn == uses:
                        pe.wait_ge(r.w13_loaded[b], (turn + 1) * 16)
                    pe.wait_ge(r.xt_copied, s)
                    w(pe, r.h_done, s - 2)
                    for c in range(DC):
                        last = pe.matmul(ps[:, GU_BANK[b % 2], 0:2 * INNER], r.xt[:, b % 2, c * P:(c + 1) * P], r.w13[:, b, c],
                                         start=c == 0, stop=c == DC - 1)
                    last.then_inc(r.gu_ready, 1)
                if kind(2):
                    b = (q - 2) % RING
                    pe.wait_ge(r.h_done, s - 1)
                    w(pe, r.ht_copied, s - 2)
                    for c in range(2):
                        last = pe.transpose(ps[0:IC, 6, c * P:(c + 1) * P], r.hh[:, b % 2, c * IC:(c + 1) * IC], ident[:])
                    last.then_inc(r.ht_ready, 1)
                if kind(3):
                    b = (q - 3) % RING
                    turn = i + (q - 3) // RING
                    pe.wait_ge(r.ht_copied, s - 2)
                    if kind(3) == 'routed':
                        pe.wait_ge(r.w2_loaded[b], (turn + 1) * 16)
                        w(pe, r.y_copied, s - 4)
                        bank, begins, ends = DN_BANK[b % 2], True, True
                    else:
                        if isinstance(i, int) and turn == uses:
                            pe.wait_ge(r.w2_loaded[b], (turn + 1) * 16)
                        if b == 0:
                            if isinstance(i, int) and turn == uses:
                                pe.wait_ge(r.y_copied, r.routed)
                            else:
                                pe.wait_ge(r.shared_added, turn - uses)
                        bank, begins, ends = DN_BANK[0], b == 0, b == SHARED - 1
                    for c in range(2):
                        last = pe.matmul(ps[:, bank, 0:D], r.ht[:, b % 2, c], r.w2[:, b, c],
                                         start=begins and c == 0, stop=ends and c == 1)
                    last.then_inc(r.dn_done, 1)
            tile_steps(pe, r, fn)

        def experts_act(act, r):
            def fn(i, q, kind):
                s = i * RING + q
                if kind(0):
                    act.wait_ge(r.xt_ready, s + 1)
                    w(act, r.gu_ready, s - 1)
                    act.copy(r.xt[:, q % 2], ps[:, 4, 0:D]).then_inc(r.xt_copied, 1)
                if kind(1):
                    b = (q - 1) % 2
                    act.wait_ge(r.gu_ready, s)
                    w(act, r.act_step, s - 2)
                    act.activation(r.th[:, b], ps[:, GU_BANK[b], 0:INNER], ACT.Tanh, scale=0.5).then_inc(r.tanh_ready, 1)
                if kind(3) == 'routed':
                    b = (q - 3) % RING
                    act.wait_ge(r.dn_done, s - 2)
                    w(act, r.stored[b], (i + (q - 3) // RING) * 16)
                    act.copy(r.yy[:, b], ps[:, DN_BANK[b % 2], 0:D]).then_inc(r.y_copied, 1)
            tile_steps(act, r, fn)

        def experts_dve(v, r):
            def add_result(i, k):
                n = i * r.K + k
                v.wait_ge(r.gathered[k], 16 * (i + 1))
                w(v, r.added, n)
                if k == 0:
                    v.wait_ge(r.shared_added, i + 1)
                xi = xr[:, bass.ds(i, 1), :].rearrange("p o d -> p (o d)")
                v.scalar_tensor_tensor(xi, r.got[:, k, :], r.weight[:, bass.ds(i, 1), k], xi, ALU.mult, ALU.add).then_inc(r.added, 1)

            def fn(i, q, kind):
                s = i * RING + q
                if kind(1):
                    b = (q - 1) % 2
                    v.wait_ge(r.tanh_ready, s)
                    v.scalar_tensor_tensor(r.ga[:, b], r.th[:, b], 1.0, ps[:, GU_BANK[b], 0:INNER], ALU.add, ALU.mult).then_inc(r.act_step, 1)
                    v.wait_ge(r.act_step, s)
                    w(v, r.ht_ready, s - 2)
                    v.scalar_tensor_tensor(r.hh[:, b], r.ga[:, b], 0.5, ps[:, GU_BANK[b], INNER:2 * INNER], ALU.mult, ALU.mult).then_inc(r.h_done, 1)
                if kind(2):
                    b = (q - 2) % 2
                    v.wait_ge(r.ht_ready, s - 1)
                    w(v, r.dn_done, s - 3)
                    v.tensor_copy(r.ht[:, b].rearrange("p c t -> p (c t)"), ps[0:IC, 6, 0:2 * P]).then_inc(r.ht_copied, 1)
                if kind(3) == 'shared' and q == 2:
                    token_tile = i - 1 - r.routed // RING
                    v.wait_ge(r.dn_done, s - 2)
                    xi = xr[:, bass.ds(token_tile, 1), :].rearrange("p o d -> p (o d)")
                    v.scalar_tensor_tensor(xi, ps[:, DN_BANK[0], 0:D], r.weight[:, bass.ds(token_tile, 1), r.K], xi,
                                           ALU.mult, ALU.add).then_inc(r.shared_added, 1)
                if r.tiles_n > r.routed and (not isinstance(i, int) and kind(0) == 'shared' or isinstance(i, int) and i >= r.tiles_n // RING):
                    add_result(i - 2 - r.routed // RING, q)
            tile_steps(v, r, fn)

        def gather_pool(g, r):
            for q in range(RING):
                g.wait_ge(r.stored[q], 16 * r.routed // RING)
            n = 0
            for i in range(NT):
                for k in range(r.K):
                    if n >= 4:
                        g.wait_ge(r.added, n - 3)
                    g.indirect_dma_start(r.got[:, n % 4, :], None, r.result[:, :],
                                         bass.IndirectOffsetOnAxis(ap=r.slot[:, k, i:i + 1], axis=0)).then_inc(r.gathered[n % 4], 16)
                    n += 1

        def gather_dve(v, r):
            n = 0
            for i in range(NT):
                for k in range(r.K):
                    v.wait_ge(r.gathered[n % 4], 16 * (n // 4 + 1))
                    if k > 0:
                        v.wait_ge(r.added, n)
                    v.scalar_tensor_tensor(xr[:, i, :], r.got[:, n % 4, :], r.weight[:, i, k:k + 1], xr[:, i, :],
                                           ALU.mult, ALU.add).then_inc(r.added, 1)
                    n += 1

        ITS = BATCH * HEADS
        P_RING = 2

        def chunk_of(qt):
            return qt if qt < 4 else 4 + 2 * (qt - 4)

        def chunks(qt):
            return [(chunk_of(qt) + j // 4, j, min(j + 4, qt + 1)) for j in range(0, qt + 1, 4)]

        LAST7 = 5 + 8 * (ITS - 1)

        def use7(it, n, last=False):
            if last:
                return LAST7 + {'o2': 1, 'o0': 2, 'end': 3}[n]
            return 5 + 8 * it + {'o2': 1, 0: 2, 1: 3, 2: 4, 3: 5, 4: 6, 'o0': 7, 5: 8}[n]

        def use6(it, n):
            return 4 * it + {'o3': 0, 'h0': 1, 'o1': 2, 'h1': 3}[n]

        def heads_loop(eng, body):
            for b in range(BATCH):
                body(0, b, False)
            with eng.Fori(1, HEADS - 1) as h:
                for b in range(BATCH):
                    body(h, b, False)
            for b in range(BATCH):
                body(HEADS - 1, b, b == BATCH - 1)

        def three(pe, out_ap, a_r, a_l, b_r, b_l, start, stop):
            pe.matmul(out_ap, a_r, b_r, start=start, stop=False)
            pe.matmul(out_ap, a_l, b_r, start=False, stop=False)
            return pe.matmul(out_ap, a_r, b_l, start=False, stop=stop)

        def att_pe(pe):
            def scores(it, qt, buf, nxt):
                n = 8 * it + qt
                w(pe, s_exp, n - 1)
                kb = buf
                qn = qt % 8
                if qn == 0:
                    w(pe, s_ql, 4 * (it + (1 if nxt else 0)) + 4)
                bank = 2 * (qt % 2)
                for c in range(0, qn + 1, 4):
                    cols = min(4, qn + 1 - c) * P
                    o = ps[:, bank + c // 4, 0:cols]
                    qs = slice(qn * P, (qn + 1) * P)
                    ks = slice(c * P, c * P + cols)
                    last = three(pe, o, qkr[:, kb, 0, qs], qkl[:, kb, 0, qs], qkr[:, kb, 1, ks], qkl[:, kb, 1, ks],
                                 True, qn // 4 != c // 4)
                    if qn // 4 == c // 4:
                        last = pe.matmul(ps[:, bank + c // 4, (qn - c) * P:(qn - c + 1) * P], ident_b[:], maskb[:], start=False, stop=True)
                last.then_inc(s_S, 1)

            def piece(it, b, p, target_b, count):
                w(pe, s_e7, count - 1)
                tok = target_b * SEQ
                if p < 4:
                    wi, half = p // 2, p % 2
                    sl = slice(tok + half * 512, tok + half * 512 + 512)
                    for c in range(DC):
                        last = three(pe, ps[:, 7, :], wr[:, wi, c], wl[:, wi, c], xnr[:, c, sl], xnl[:, c, sl], c == 0, c == DC - 1)
                else:
                    for i in range(4):
                        sl = slice(tok + ((p - 4) * 4 + i) * P, tok + ((p - 4) * 4 + i + 1) * P)
                        for c in range(DC):
                            last = three(pe, ps[:, 7, i * P:(i + 1) * P], xnr[:, c, sl], xnl[:, c, sl], wr[:, 2, c], wl[:, 2, c], c == 0, c == DC - 1)
                last.then_inc(s_b7, 1)

            def transposes(it, qt):
                w(pe, s_exp, 8 * it + qt + 1)
                for ci, j0, j1 in chunks(qt):
                    w(pe, s_pl, 12 * it + ci - 1)
                    for j in range(j0, j1):
                        last = pe.transpose(ps[:, 4 + ci % 2, (j - j0) * P:(j - j0 + 1) * P], pb[:, qt % 2, j * P:(j + 1) * P], ident[:])
                    last.then_inc(s_T, 1)

            def output(it, buf, g):
                w(pe, s_pl, 12 * it + (4 if g == 0 else 12))
                u = use6(it, 'h0' if g == 0 else 'h1')
                w(pe, s_e6, u - 1)
                for j in range(4 * g + 4):
                    c0 = max(0, j - 4 * g) * P
                    last = three(pe, ps[:, 6, c0:512], vr[:, buf, j], vl[:, buf, j], ptr[:, j, c0:512], ptl[:, j, c0:512], j == 0, j == 4 * g + 3)
                last.then_inc(s_b6, 1)

            def project_out(h, it, which, bank, count, s_fill, s_taken, taken6):
                w(pe, s_e6, taken6)
                w(pe, s_taken, count - 1)
                for a in range(2):
                    sl = slice((2 * (which % 2) + a) * P, (2 * (which % 2) + a + 1) * P)
                    last = three(pe, ps[:, bank, a * D:(a + 1) * D], otr[:, sl], otl[:, sl], wor[:], wol[:], True, True)
                last.then_inc(s_fill, 1)

            pe.wait_ge(s_split, 2 * NG)
            pe.wait_ge(s_ws, 1)
            for p in range(6):
                piece(0, 0, p, 0, p + 1)
            pe.wait_ge(s_mask, 1)
            pe.wait_ge(s_e7, 6)
            scores(0, 0, 0, False)

            def body(h, b, last):
                it = 2 * h + b
                for qt in range(8):
                    if qt < 7:
                        scores(it, qt + 1, b, False)
                    elif not last:
                        pe.wait_ge(s_e7, use7(it, 5))
                        scores(it, 8, 1 - b, True)
                    if qt > 0 and qt < 6 and not last:
                        piece(it, b, qt, 1 - b, use7(it, qt))
                    transposes(it, qt)
                    if qt == 0:
                        if not (isinstance(it, int) and it == 0):
                            project_out(h, it, 2, 7, use7(it, 'o2', last), s_b7, s_e7, use6(it, 'o3') - 1)
                            project_out(h, it, 3, 6, use6(it, 'o3'), s_b6, s_e6, use6(it, 'o3') - 1)
                        if not last:
                            if b == BATCH - 1:
                                pe.wait_ge(s_ws, h + 2)
                            piece(it, b, 0, 1 - b, use7(it, 0))
                    if qt == 3:
                        output(it, b, 0)
                    if qt == 4:
                        if b == 0:
                            pe.wait_ge(s_wos, h + 1)
                        project_out(h, it, 0, 7, use7(it, 'o0', last), s_b7, s_e7, use6(it, 'h0'))
                        project_out(h, it, 1, 6, use6(it, 'o1'), s_b6, s_e6, use6(it, 'h0'))
                    if qt == 7:
                        output(it, b, 1)
            heads_loop(pe, body)
            project_out(HEADS, ITS, 2, 7, use7(0, 'end', True), s_b7, s_e7, use6(ITS, 'o3') - 1)
            project_out(HEADS, ITS, 3, 6, use6(ITS, 'o3'), s_b6, s_e6, use6(ITS, 'o3') - 1)

        def att_act(act):
            def exps(it, qt):
                n = 8 * it + qt
                qn, par = qt % 8, qt // 8
                w(act, s_max, n + 1)
                w(act, s_T, 12 * it + (chunk_of(qt - 2) + len(chunks(qt - 2)) if qt >= 2 else -(2, 0)[qt]))
                return qn, n

            def piece(it, p, buf, count, pieces_before):
                act.wait_ge(s_b7, count)
                if p < 4:
                    w(act, s_rot, pieces_before - 1)
                    act.copy(sw[64:96, p % 2, :], ps[96:128, 7, :])
                    act.copy(sw[96:128, p % 2, :], ps[64:96, 7, :]).then_inc(s_a7, 1)
                else:
                    act.copy(vr[:, buf, (p - 4) * 4:(p - 3) * 4, :].rearrange("p i d -> p (i d)"), ps[:, 7, :]).then_inc(s_a7, 1)

            def rounded(it, p, buf, pieces_before):
                act.wait_ge(s_rot, pieces_before + 1)
                act.copy(qkr[:, buf, p // 2, (p % 2) * 512:(p % 2 + 1) * 512], t1[:, p % 2, :]).then_inc(s_qr, 1)

            def exp_tile(it, qt, b):
                qn, n = exps(it, qt)
                par = b if qt < 8 else 1 - b
                cols = (qn + 1) * P
                bank = 2 * (qt % 2)
                act.activation(pb[:, qt % 2, 0:cols], ps[:, bank:bank + 2, :].rearrange("p a n -> p (a n)")[:, 0:cols], ACT.Exp,
                               bias=negmax[:, par, qn:qn + 1], accum_out=rowsum[:, par, qn:qn + 1]).then_inc(s_exp, 1)

            for p in range(6):
                piece(-1, p, 0, p + 1, p)
                if p < 4:
                    rounded(-1, p, 0, p)
            exp_tile(0, 0, 0)

            def body(h, b, last):
                it = 2 * h + b
                for qt in range(8):
                    if qt < 7 or not last:
                        exp_tile(it, qt + 1, b)
                    if qt > 0 and qt < 6 and not last:
                        piece(it, qt, 1 - b, use7(it, qt), 4 * (it + 1) + qt)
                    if 2 <= qt < 5 and not last:
                        rounded(it, qt - 1, 1 - b, 4 * (it + 1) + qt - 1)
                    for ci, j0, j1 in chunks(qt):
                        act.wait_ge(s_T, 12 * it + ci + 1)
                        if ci == 0:
                            w(act, s_b6, use6(it, 'h1') - 4)
                        if ci == 4:
                            act.wait_ge(s_b6, use6(it, 'h0'))
                        cols = slice((qt % 4) * P, (qt % 4 + 1) * P)
                        act.copy(ptr[:, j0:j1, cols], ps[:, 4 + ci % 2, 0:(j1 - j0) * P].rearrange("p (j q) -> p j q", q=P)).then_inc(s_pr, 1)
                    if qt == 0 and not last:
                        piece(it, 0, 1 - b, use7(it, 0), 4 * (it + 1))
                    if qt == 1 and not last:
                        rounded(it, 0, 1 - b, 4 * (it + 1))
                    if qt in (3, 7):
                        g = qt // 4
                        act.wait_ge(s_b6, use6(it, f'h{g}'))
                        if g == 0:
                            w(act, s_b6, use6(it, 'o3'))
                        act.copy(otr[:], ps[:, 6, :]).then_inc(s_a6, 1)
            heads_loop(act, body)

        def att_dve(v):
            def max_tile(it, qt, b):
                qn = qt % 8
                par = b if qt < 8 else 1 - b
                cols = (qn + 1) * P
                bank = 2 * (qt % 2)
                v.wait_ge(s_S, 8 * it + qt + 1)
                v.tensor_reduce(negmax[:, par, qn:qn + 1], ps[:, bank:bank + 2, :].rearrange("p a n -> p (a n)")[:, 0:cols], AX.X, ALU.max,
                                negate=True).then_inc(s_max, 1)

            def piece(it, p, buf, count):
                v.wait_ge(s_a7, count_a7(it, p))
                if p < 4:
                    w(v, s_ql, 4 * (it + 1) + p - 1)
                    v.tensor_tensor(t1[:, p % 2, :], ps[:, 7, :], rope_t[:, 0, (p % 2) * 512:(p % 2 + 1) * 512], ALU.mult).then_inc(s_e7, 1)
                else:
                    v.tensor_tensor(vl[:, buf, (p - 4) * 4:(p - 3) * 4, :].rearrange("p i d -> p (i d)"), ps[:, 7, :],
                                    vr[:, buf, (p - 4) * 4:(p - 3) * 4, :].rearrange("p i d -> p (i d)").bitcast(F32), ALU.subtract).then_inc(s_e7, 1)

            def count_a7(it, p):
                return 6 * (it + 1) + p + 1

            def rest(it, p, buf):
                n = 4 * (it + 1) + p
                v.wait_ge(s_qr, n + 1)
                o = (slice(None), buf, p // 2, slice((p % 2) * 512, (p % 2 + 1) * 512))
                v.tensor_tensor(qkl[o], t1[:, p % 2, :], qkr[o].bitcast(F32), ALU.subtract).then_inc(s_ql, 1)

            def add_out(it, which, bank, b_out, count, s_fill, s_taken):
                v.wait_ge(s_fill, count)
                for a in range(2):
                    qn = 2 * which + a
                    i = b_out * 8 + qn
                    last = v.scalar_tensor_tensor(xr[:, i, :], ps[:, bank, a * D:(a + 1) * D], rinv[:, b_out, qn:qn + 1], xr[:, i, :], ALU.mult, ALU.add)
                last.then_inc(s_taken, 1)

            def split_qkv(h):
                v.wait_ge(s_wraw, (h + 1) * 16)
                for part in range(2):
                    sl = slice(part * QK, (part + 1) * QK)
                    last = v.tensor_scalar(wraw[:, 0, :, sl], wraw[:, 0, :, sl], gsc[:, part, bass.ds(h, 1)], None, ALU.mult)
                last.then_inc(s_wsc, 1)
                v.wait_ge(s_wsc, h + 1)
                v.tensor_copy(wr[:], wraw[:]).then_inc(s_rnd, 1)
                v.wait_ge(s_rnd, 2 * h + 1)
                v.tensor_tensor(wl[:], wraw[:], wr[:].bitcast(F32), ALU.subtract).then_inc(s_ws, 1)

            def split_wo(h):
                v.wait_ge(s_wor, (h + 1) * 16)
                v.tensor_copy(wor[:], woraw[:]).then_inc(s_rnd, 1)
                v.wait_ge(s_rnd, 2 * h + 2)
                v.tensor_tensor(wol[:], woraw[:], wor[:].bitcast(F32), ALU.subtract).then_inc(s_wos, 1)

            v.wait_ge(s_par1, 64)
            split_qkv(0)
            for p in range(6):
                piece(-1, p, 0, p + 1)
                if p < 4:
                    rest(-1, p, 0)
            max_tile(0, 0, 0)

            def body(h, b, last):
                it = 2 * h + b
                for qt in range(8):
                    if qt < 7 or not last:
                        max_tile(it, qt + 1, b)
                    if qt > 0 and qt < 6 and not last:
                        piece(it, qt, 1 - b, use7(it, qt))
                    if 2 <= qt < 5 and not last:
                        rest(it, qt - 1, 1 - b)
                    for ci, j0, j1 in chunks(qt):
                        v.wait_ge(s_pr, 12 * it + ci + 1)
                        cols = slice((qt % 4) * P, (qt % 4 + 1) * P)
                        v.tensor_tensor(ptl[:, j0:j1, cols], ps[:, 4 + ci % 2, 0:(j1 - j0) * P].rearrange("p (j q) -> p j q", q=P),
                                        ptr[:, j0:j1, cols].bitcast(F32), ALU.subtract).then_inc(s_pl, 1)
                    if qt == 0:
                        if not (isinstance(it, int) and it == 0):
                            add_out(it, 2, 7, 1 - b, use7(it, 'o2', last), s_b7, s_e7)
                            add_out(it, 3, 6, 1 - b, use6(it, 'o3'), s_b6, s_e6)
                        if not last:
                            piece(it, 0, 1 - b, use7(it, 0))
                    if qt == 1 and not last:
                        rest(it, 0, 1 - b)
                    if qt == 2 and b == 0:
                        split_wo(h)
                    if qt == 6 and b == 0 and not (isinstance(h, int) and h == HEADS - 1):
                        v.wait_ge(s_b7, use7(it, 5))
                        split_qkv(h + 1)
                    if qt in (3, 7):
                        g = qt // 4
                        v.wait_ge(s_a6, 2 * it + g + 1)
                        v.tensor_tensor(otl[:], ps[:, 6, :], otr[:].bitcast(F32), ALU.subtract).then_inc(s_e6, 1)
                        v.wait_ge(s_exp, 8 * it + qt + 1)
                        v.reciprocal(rinv[:, b, 4 * g:4 * g + 4], rowsum[:, b, 4 * g:4 * g + 4]).then_inc(s_rinv, 1)
                        v.wait_ge(s_rinv, 2 * it + g + 1)
                    if qt == 4:
                        add_out(it, 0, 7, b, use7(it, 'o0', last), s_b7, s_e7)
                        add_out(it, 1, 6, b, use6(it, 'o1'), s_b6, s_e6)
            heads_loop(v, body)
            add_out(ITS, 2, 7, 1, use7(0, 'end', True), s_b7, s_e7)
            add_out(ITS, 3, 6, 1, use6(ITS, 'o3'), s_b6, s_e6)

        def att_pool(g):
            def rotate(n, p):
                g.wait_ge(s_a7, 6 * (n // 4) + p + 1 if isinstance(n, int) else 6 * n[1] + p + 1)
                cnt = n if isinstance(n, int) else 4 * n[1] + p
                half = p % 2
                g.tensor_tensor(sw[64:128, half, :], sw[64:128, half, :], rope_t[64:128, 1, half * 512:(half + 1) * 512], ALU.mult).then_inc(s_t2, 1)
                g.wait_ge(s_t2, cnt + 1)
                g.wait_ge(s_e7, e7_of(n, p))
                g.tensor_tensor(t1[64:128, half, :], t1[64:128, half, :], sw[64:128, half, :], ALU.add).then_inc(s_rot, 1)

            def e7_of(n, p):
                return p + 1 if isinstance(n, int) else use7(n[1] - 1, p)
            g.wait_ge(s_par1, 64)
            for p in range(4):
                rotate(p, p)
            with g.Fori(1, ITS) as it:
                for p in range(4):
                    rotate((0, it), p)

        def att_sp(sp):
            for h in (0,):
                sp.dma_start(wraw[:], wqkv[0]).then_inc(s_wraw, 16)
                sp.dma_start(woraw[:], wo_h[0]).then_inc(s_wor, 16)
            with sp.Fori(1, HEADS) as h:
                sp.wait_ge(s_ws, h)
                sp.dma_start(wraw[:], wqkv[bass.ds(h, 1)].rearrange("o p a c n -> (o p) a c n")).then_inc(s_wraw, 16)
                sp.wait_ge(s_wos, h)
                sp.dma_start(woraw[:], wo_h[bass.ds(h, 1)].rearrange("o p n -> (o p) n")).then_inc(s_wor, 16)

        block = ctx.enter_context(nc.Block())

        @block.sync
        def _(sp):
            for g in range(NG):
                sp.dma_start(xr[:, g * GT:(g + 1) * GT, :],
                             x_in[g * GT * P:(g + 1) * GT * P, :].rearrange("(i p) d -> p i d", p=P)).then_inc(s_x[g], 16)
            sp.dma_start(xpw[:], xproj).then_inc(s_par, 16)
            sp.dma_start(dtw[:], dtproj).then_inc(s_par, 16)
            sp.dma_start(dtb[:], dt_bias).then_inc(s_par, 16)
            sp.dma_start(alog[:], a_log).then_inc(s_par, 16)
            sp.dma_start(dpar[:], d_param).then_inc(s_par, 16)
            sp.dma_start(rw0[:], router0).then_inc(s_par, 16)
            sp.wait_ge(s_const, 1)
            zero_fill(sp, R0)
            zero_fill(sp, R1)
            sp.wait_ge(s_xdc, 8)
            sp.dma_start(bc_rows, bcT).then_inc(s_bc, 16)
            route_sp(sp, R0)
            sp.wait_ge(s_bc, 16)
            sp.wait_ge(s_dp, 8)
            for b in range(BATCH):
                with sp.Fori(0, STATES // 2) as j:
                    for q in range(2):
                        it = b * STATES + j * 2 + q
                        sp.wait_ge(s_hc, it + 1)
                        for rows, off in ((brow, 0), (crow, STATES)):
                            sp.dma_start(rows[:, q, :], bc_rows[bass.ds(j * 2 + q + off, 1), b * SEQ:(b + 1) * SEQ]
                                         .to_broadcast([P, SEQ])).then_inc(s_row[q], 16)
            experts_sp(sp, R0)
            if not only0:
                sp.wait_ge(s_xn, 2 * NG)
                sp.dma_start(rw1[:], router1).then_inc(s_par1, 16)
                sp.dma_start(rope_t[:], rope).then_inc(s_par1, 16)
                sp.dma_start(gsc[:, 0, :], gate_logit.to_broadcast([P, HEADS])).then_inc(s_par1, 16)
                sp.dma_start(gsc[:, 1, :], gate_logit.to_broadcast([P, HEADS])).then_inc(s_par1, 16)
                att_sp(sp)
                route_sp(sp, R1)
                sp.wait_ge(s_e6, use6(ITS, 'o3'))
                sp.wait_ge(s_e7, use7(0, 'end', True))
                experts_sp(sp, R1)
                for q in range(NG):
                    sp.wait_ge(R1.shared_added, (q + 1) * GT)
                    sp.wait_ge(R1.added, (q + 1) * GT * K1)
                    sp.dma_start(out[q * GT * P:(q + 1) * GT * P, :].rearrange("(i p) d -> p i d", p=P),
                                 xr[:, q * GT:(q + 1) * GT, :]).then_inc(s_out, 16)
                sp.wait_ge(s_out, 16 * NG)
                for q in range(RING):
                    sp.wait_ge(R1.stored[q], 16 * R1.routed // RING)
                sp.wait_ge(R1.zeroed, 16 * R1.zero_dmas)
            if only0:
                sp.wait_ge(R0.added, NT)
                sp.dma_start(out.rearrange("(i p) d -> p i d", p=P), xr[:]).then_inc(s_out, 16)
                sp.wait_ge(s_out, 16)
            for q in range(RING):
                sp.wait_ge(R0.stored[q], 16 * R0.tiles_n // RING)
            sp.wait_ge(R0.zeroed, 16 * R0.zero_dmas)

        @block.gpsimd
        def _(g):
            n = [0]

            def step(ins):
                n[0] += 1
                ins.then_inc(s_const, 1)
                g.wait_ge(s_const, n[0])
            step(g.memset(zeros[:], 0.0))
            step(g.memset(neg_half[:], -0.5))
            step(g.memset(zero_b[:], 0.0))
            step(g.memset(ones_b[:], 1.0))
            step(g.memset(ident[:], 0.0))
            step(g.affine_select(out=ident[:], in_=ident[:], compare_op=ALU.not_equal, fill=1.0, base=0,
                                 pattern=[[-1, P]], channel_multiplier=1))
            step(g.tensor_copy(ident_b[:], ident[:]))
            step(g.affine_select(out=before[:], in_=ones_b[:], compare_op=ALU.is_gt, fill=0.0, base=0,
                                 pattern=[[1, P]], channel_multiplier=-1))
            step(g.iota(iota_e[:], [[1, E1]], base=0, channel_multiplier=0, allow_small_or_imprecise_dtypes=True))
            step(g.iota(iota_p[:], [[1, 1]], base=0, channel_multiplier=1, allow_small_or_imprecise_dtypes=True))
            for q in range(NG):
                g.wait_ge(s_var, q + 1)
                g.tensor_tensor(stat[:, 3, q * GT:(q + 1) * GT], stat[:, 2, q * GT:(q + 1) * GT],
                                neg_half[:, q * GT:(q + 1) * GT], ALU.pow).then_inc(s_rstd, 1)
            route_pool(g, R0)
            gather_pool(g, R0)
            if only0:
                return
            for q in range(NG):
                g.wait_ge(s_var, NG + q + 1)
                g.tensor_tensor(stat[:, 3, q * GT:(q + 1) * GT], stat[:, 2, q * GT:(q + 1) * GT],
                                neg_half[:, q * GT:(q + 1) * GT], ALU.pow).then_inc(s_rstd, 1)
            g.wait_ge(s_xn, 2 * NG)
            g.affine_select(out=maskb[:], in_=zero_b[:], compare_op=ALU.is_ge, fill=-1e9, base=0,
                            pattern=[[-1, P]], channel_multiplier=1).then_inc(s_mask, 1)
            g.wait_ge(s_mask, 1)
            route_pool(g, R1)
            g.wait_ge(R1.scattered, 16 * NT * K1)
            att_pool(g)
            gather_pool(g, R1)

        N_CONST = 10

        @block.vector
        def _(v):
            def ln(first):
                for q in range(NG):
                    sl = slice(q * GT, (q + 1) * GT)
                    st = first + 5 * q

                    def step(ins, m):
                        ins.then_inc(s_ln, 1)
                        v.wait_ge(s_ln, st + m)
                    if first == 0:
                        v.wait_ge(s_x[q], 16)
                    else:
                        v.wait_ge(R0.added, GT * (q + 1))
                    step(v.tensor_reduce(stat[:, 0, sl], xr[:, sl, :], AX.X, ALU.add), 1)
                    step(v.tensor_scalar(stat[:, 1, sl], stat[:, 0, sl], -1.0 / D, None, ALU.mult), 2)
                    step(v.tensor_tensor(xn[:, sl, :], xr[:, sl, :], stat[:, 1, sl].unsqueeze(2).to_broadcast([P, GT, D]), ALU.add), 3)
                    s3 = (sw[:].rearrange("p a n -> p (a n)") if first else sq[:, 0:GT * D]).rearrange("p (i d) -> p i d", d=D)
                    step(v.tensor_tensor(s3, xn[:, sl, :], xn[:, sl, :], ALU.mult), 4)
                    step(v.tensor_reduce(stat[:, 0, sl], s3, AX.X, ALU.add), 5)
                    v.tensor_scalar(stat[:, 2, sl], stat[:, 0, sl], 1.0 / D, EPS, ALU.mult, ALU.add).then_inc(s_var, 1)
                    v.wait_ge(s_rstd, first // (5 * NG) * NG + q + 1)
                    v.tensor_tensor(xn[:, sl, :], xn[:, sl, :], stat[:, 3, sl].unsqueeze(2).to_broadcast([P, GT, D]), ALU.mult)\
                        .then_inc(s_xn, 1)
            ln(0)
            for q in range(NG):
                v.wait_ge(s_xnT_ps, q + 1)
                for c in range(DC):
                    last = v.tensor_copy(xnT[:, c, q * 512:(q + 1) * 512], ps[:, (q % 2) * 2 + c, :])
                last.then_inc(s_xnT, 1)
            v.wait_ge(s_const, N_CONST)
            v.memset(R0.ecmp[:], 1.0)
            step = route_dve(v, R0)
            v.tensor_tensor(R0.weight[:, :, 0], R0.top[:, :, 1], R0.top[:, :, 0], ALU.subtract).then_inc(s_spa, 1)
            v.wait_ge(s_spa, 2)
            v.tensor_scalar(R0.weight[:, :, 0], R0.weight[:, :, 1], 1.0, None, ALU.add).then_inc(s_spa, 1)
            v.wait_ge(s_spa, 3)
            v.reciprocal(R0.weight[:, :, 0], R0.weight[:, :, 0]).then_inc(s_spa, 1)
            v.wait_ge(s_spa, 4)

            for b in range(BATCH):
                m = [10 * b]

                def sstep(ins):
                    m[0] += 1
                    ins.then_inc(s_sp, 1)
                    v.wait_ge(s_sp, m[0])
                dl = delta[:, :, b * SEQ:(b + 1) * SEQ]

                def two(a):
                    return a.rearrange("p (c t) -> p c t", c=DC)
                v.wait_ge(s_spa, 4 + b + 1)
                sstep(v.tensor_scalar(sp_z, sp_e, 2.0, None, ALU.add))
                sstep(v.reciprocal(sp_z, sp_z))
                sstep(v.tensor_tensor(sp_s, sp_e, sp_z, ALU.mult))
                sstep(v.tensor_tensor(sp_z, sp_s, sp_s, ALU.mult))
                sstep(v.tensor_scalar(sp_e, sp_z, COEF[4], COEF[3], ALU.mult, ALU.add))
                sstep(v.tensor_tensor(sp_e, sp_e, sp_z, ALU.mult))
                sstep(v.scalar_tensor_tensor(sp_e, sp_e, COEF[2], sp_z, ALU.add, ALU.mult))
                sstep(v.scalar_tensor_tensor(sp_e, sp_e, COEF[1], sp_z, ALU.add, ALU.mult))
                sstep(v.scalar_tensor_tensor(sp_e, sp_e, COEF[0], sp_s, ALU.add, ALU.mult))
                sstep(v.scalar_tensor_tensor(dl, two(sp_x), 0.0, two(sp_e), ALU.max, ALU.add))
                v.tensor_tensor(dx[:, :, b * SEQ:(b + 1) * SEQ], dl, xnT[:, :, b * SEQ:(b + 1) * SEQ], ALU.mult).then_inc(s_delta, 1)
            v.wait_ge(s_delta, 2)
            for q in range(2):
                last = v.memset(decay[:, q, :, 0:1], 0.0)
            last.then_inc(s_hc, 2)
            for b in range(BATCH):
                with v.Fori(0, STATES // 2) as j:
                    for q in range(2):
                        it = b * STATES + j * 2 + q
                        flat = state[:, q].rearrange("p c t -> p (c t)")
                        v.wait_ge(s_row[q], (b * (STATES // 2) + j + 1) * 32)
                        v.wait_ge(s_ysum, it + 1)
                        v.tensor_tensor(state[:, q], dx[:, :, b * SEQ:(b + 1) * SEQ],
                                        brow[:, q, :].unsqueeze(1).to_broadcast([P, DC, SEQ]), ALU.mult).then_inc(s_dbx, 1)
                        v.wait_ge(s_dbx, it + 1)
                        v.wait_ge(s_dec, it + 1)
                        v.tensor_tensor_scan(flat, decay[:, q].rearrange("p c t -> p (c t)"), flat, 0.0,
                                             ALU.mult, ALU.add).then_inc(s_scan, 1)
                        v.wait_ge(s_scan, it + 1)
                        v.tensor_tensor(state[:, q], state[:, q],
                                        crow[:, q, :].unsqueeze(1).to_broadcast([P, DC, SEQ]), ALU.mult).then_inc(s_hc, 1)
                v.wait_ge(s_ysum, 2 + (b + 1) * STATES)
                v.wait_ge(s_dec, (b + 1) * STATES)
                for c in range(DC):
                    last = v.scalar_tensor_tensor(delta[:, c, b * SEQ:(b + 1) * SEQ], xnT[:, c, b * SEQ:(b + 1) * SEQ],
                                                  dpar[:, c:c + 1], ps[:, 2 * c:2 * c + 2, :].rearrange("p a t -> p (a t)"), ALU.mult, ALU.add)
                last.then_inc(s_yT, 1)
            for i in range(NT // 2):
                v.wait_ge(s_yT_ps, i + 1)
                v.tensor_tensor(xr[:, 2 * i:2 * i + 2, :], xr[:, 2 * i:2 * i + 2, :],
                                ps[:, i % 2, :].rearrange("p (a d) -> p a d", a=2), ALU.add).then_inc(s_yadd, 1)
            experts_dve(v, R0)
            v.wait_ge(s_yadd, NT // 2)
            gather_dve(v, R0)
            if only0:
                return
            v.wait_ge(R1.zeroed, 16 * R1.zero_dmas)
            ln(5 * NG)
            for q in range(NG):
                sl = slice(q * 512, (q + 1) * 512)
                v.wait_ge(s_xnT1, q + 1)
                v.tensor_copy(xnr[:, :, sl], xnT1[:, :, sl]).then_inc(s_split, 1)
                v.wait_ge(s_split, 2 * q + 1)
                v.tensor_tensor(xnl[:, :, sl], xnT1[:, :, sl], xnr[:, :, sl].bitcast(F32), ALU.subtract).then_inc(s_split, 1)
            gs = [0]

            def gstep(ins):
                gs[0] += 1
                ins.then_inc(s_gate, 1)
                v.wait_ge(s_gate, gs[0])
            v.wait_ge(s_gact, 1)
            gstep(v.tensor_scalar(gsc[:], gsc[:], 1.0, None, ALU.add))
            gstep(v.reciprocal(gsc[:], gsc[:]))
            gstep(v.tensor_scalar(gsc[:, 1, :], gsc[:, 1, :], -1.0, 1.0, ALU.mult, ALU.add))
            gstep(v.tensor_scalar(gsc[:], gsc[:], QK ** -0.5, None, ALU.mult))
            v.memset(R1.ecmp[:], 1.0)
            step = route_dve(v, R1)
            soft = R1.rank[:].rearrange("p e i -> p (e i)").rearrange("p (i e) -> p i e", e=E1)
            top0 = R1.top[:, :, 0:1]
            v.tensor_tensor(soft, R1.logit[:, :, 0:E1], top0.to_broadcast([P, NT, E1]), ALU.subtract).then_inc(s_w1, 1)
            v.tensor_tensor(R1.weight[:, :, 0:K1], R1.top[:, :, 0:K1], top0.to_broadcast([P, NT, K1]), ALU.subtract).then_inc(s_w1, 1)
            v.memset(R1.weight[:, :, K1:], 0.0).then_inc(s_w1, 1)
            v.wait_ge(s_w1a, 3)
            v.tensor_reduce(R1.weight[:, :, 5], soft, AX.X, ALU.add).then_inc(s_w1, 1)
            v.tensor_scalar(R1.weight[:, :, K1], R1.weight[:, :, K1], 1.0, None, ALU.add).then_inc(s_w1, 1)
            v.wait_ge(s_w1, 5)
            v.reciprocal(R1.weight[:, :, K1:6], R1.weight[:, :, K1:6]).then_inc(s_w1, 1)
            v.wait_ge(s_w1, 6)
            v.tensor_tensor(R1.weight[:, :, 0:K1], R1.weight[:, :, 0:K1], R1.weight[:, :, 5:6].to_broadcast([P, NT, K1]), ALU.mult).then_inc(s_w1, 1)
            v.wait_ge(s_w1, 7)
            att_dve(v)
            v.wait_ge(s_e6, use6(ITS, 'o3'))
            v.wait_ge(s_e7, use7(0, 'end', True))
            experts_dve(v, R1)

        @block.scalar
        def _(act):
            act.wait_ge(s_par, 96)
            act.activation(alog[:], alog[:], ACT.Exp).then_inc(s_aneg, 1)
            act.wait_ge(s_aneg, 1)
            act.mul(aneg[:], alog[:], -1.0).then_inc(s_aneg, 1)
            for q in range(4):
                act.wait_ge(s_xd, 2 * q + 1)
                act.copy(dtT[:, q * 512:(q + 1) * 512], ps[:, (2 * q) % 4, :]).then_inc(s_xdc, 1)
                act.wait_ge(s_xd, 2 * q + 2)
                act.copy(bcT[:, q * 512:(q + 1) * 512], ps[0:2 * STATES, (2 * q + 1) % 4, :]).then_inc(s_xdc, 1)
            act.wait_ge(s_spa, 1)
            act.activation(R0.weight[:, :, 1], R0.weight[:, :, 0], ACT.Exp).then_inc(s_spa, 1)
            for b in range(BATCH):
                if b:
                    act.wait_ge(s_sp, 10)
                for c in range(DC):
                    for q in range(2):
                        m = b * 4 + c * 2 + q
                        act.wait_ge(s_dp, m + 1)
                        act.activation(sp_x[:, c * SEQ + q * 512:c * SEQ + (q + 1) * 512], ps[:, m % 4, :], ACT.Identity,
                                       bias=dtb[:, c:c + 1]).then_inc(s_dpc, 1)
                act.wait_ge(s_dpc, 5 * (b + 1) - 1)
                act.activation(sp_e, sp_x, ACT.Abs).then_inc(s_dpc, 1)
                act.wait_ge(s_dpc, 5 * (b + 1))
                act.wait_ge(s_spa, 4 + b)
                act.activation(sp_e, sp_e, ACT.Exp, scale=-1.0).then_inc(s_spa, 1)
            act.wait_ge(s_delta, 2)
            act.wait_ge(s_aneg, 2)
            for b in range(BATCH):
                with act.Fori(0, STATES // 2) as j:
                    for q in range(2):
                        it = b * STATES + j * 2 + q
                        act.wait_ge(s_hc, it + 1)
                        for c in range(DC):
                            last = act.activation(decay[:, q, c, 1:SEQ], delta[:, c, b * SEQ + 1:(b + 1) * SEQ], ACT.Exp,
                                                  scale=aneg[:, c, bass.ds(j * 2 + q, 1)])
                        last.then_inc(s_dec, 1)
            experts_act(act, R0)
            if only0:
                return
            for q in range(NG):
                act.wait_ge(s_xnT1_ps, q + 1)
                for c in range(DC):
                    last = act.copy(xnT1[:, c, q * 512:(q + 1) * 512], ps[:, (q % 2) * 2 + c, :])
                last.then_inc(s_xnT1, 1)
            act.wait_ge(s_par1, 64)
            act.activation(gsc[:], gsc[:], ACT.Exp, scale=-1.0).then_inc(s_gact, 1)
            act.wait_ge(s_w1, 3)
            act.activation(R1.rank[:], R1.rank[:], ACT.Exp).then_inc(s_w1a, 1)
            act.activation(R1.weight[:, :, 0:K1], R1.weight[:, :, 0:K1], ACT.Exp).then_inc(s_w1a, 1)
            act.activation(R1.weight[:, :, K1], R1.logit[:, :, E1], ACT.Exp, scale=-1.0).then_inc(s_w1a, 1)
            att_act(act)
            experts_act(act, R1)

        @block.tensor
        def _(pe):
            pe.wait_ge(s_const, N_CONST)
            for q in range(NG):
                pe.wait_ge(s_xn, q + 1)
                if q >= 2:
                    pe.wait_ge(s_xnT, q - 1)
                for c in range(DC):
                    for i in range(GT):
                        last = pe.transpose(ps[:, (q % 2) * 2 + c, i * P:(i + 1) * P], xn[:, q * GT + i, c * P:(c + 1) * P], ident[:])
                last.then_inc(s_xnT_ps, 1)
            pe.wait_ge(s_xnT, NG)
            pe.wait_ge(s_par, 96)
            for i in range(NT):
                for c in range(DC):
                    last = pe.matmul(ps[:, 4 + i // 8, (i % 8) * E0:(i % 8 + 1) * E0], xnT[:, c, i * P:(i + 1) * P],
                                     rw0[:, c, :], start=c == 0, stop=c == DC - 1)
            last.then_inc(R0.logits_ready, 1)
            for q in range(4):
                for w in range(2):
                    n = 2 * q + w
                    if n >= 4:
                        pe.wait_ge(s_xdc, n - 3)
                    rows = P if w == 0 else 2 * STATES
                    for c in range(DC):
                        last = pe.matmul(ps[0:rows, n % 4, :], xpw[:, c, w * P:w * P + rows], xnT[:, c, q * 512:(q + 1) * 512],
                                         start=c == 0, stop=c == DC - 1)
                    last.then_inc(s_xd, 1)
            pe.wait_ge(s_xdc, 8)
            for b in range(BATCH):
                for c in range(DC):
                    for q in range(2):
                        m = b * 4 + c * 2 + q
                        if m >= 4:
                            pe.wait_ge(s_dpc, m - 3)
                        pe.matmul(ps[:, m % 4, :], dtw[:, c * P:(c + 1) * P], dtT[:, b * SEQ + q * 512:b * SEQ + (q + 1) * 512],
                                  start=True, stop=True).then_inc(s_dp, 1)
                if b == 0:
                    route_pe(pe, R0)
            pe.wait_ge(s_dpc, 10)
            for q in range(4):
                last = pe.matmul(ps[:, q, :], ident[:], zeros[:, 0:512], start=True, stop=False, skip_group_check=True)
            last.then_inc(s_ysum, 2)
            for b in range(BATCH):
                if b:
                    pe.wait_ge(s_yT, b)
                    for q in range(4):
                        last = pe.matmul(ps[:, q, :], ident[:], zeros[:, 0:512], start=True, stop=False, skip_group_check=True)
                with pe.Fori(0, STATES // 2) as j:
                    for q in range(2):
                        pe.wait_ge(s_hc, 2 + b * STATES + j * 2 + q + 1)
                        for c in range(DC):
                            for h in range(2):
                                last = pe.matmul(ps[:, 2 * c + h, :], ident[:], state[:, q, c, h * 512:(h + 1) * 512],
                                                 start=False, stop=True, skip_group_check=True)
                        last.then_inc(s_ysum, 1)
            pe.wait_ge(s_yT, 2)
            for i in range(NT // 2):
                if i >= 2:
                    pe.wait_ge(s_yadd, i - 1)
                for a in range(2):
                    for c in range(DC):
                        tt = 2 * i + a
                        last = pe.transpose(ps[:, i % 2, a * D + c * P:a * D + (c + 1) * P], delta[:, c, tt * P:(tt + 1) * P], ident[:])
                last.then_inc(s_yT_ps, 1)
            experts_pe(pe, R0)
            if only0:
                return
            for q in range(NG):
                pe.wait_ge(s_xn, NG + q + 1)
                if q >= 2:
                    pe.wait_ge(s_xnT1, q - 1)
                for c in range(DC):
                    for i in range(GT):
                        last = pe.transpose(ps[:, (q % 2) * 2 + c, i * P:(i + 1) * P], xn[:, q * GT + i, c * P:(c + 1) * P], ident[:])
                last.then_inc(s_xnT1_ps, 1)
            pe.wait_ge(s_xnT1, NG)
            pe.wait_ge(s_par1, 64)
            for i in range(NT):
                for c in range(DC):
                    last = pe.matmul(ps[:, 4 + i // 8, (i % 8) * (E1 + 1):(i % 8 + 1) * (E1 + 1)], xnT1[:, c, i * P:(i + 1) * P],
                                     rw1[:, c, :], start=c == 0, stop=c == DC - 1)
            last.then_inc(R1.logits_ready, 1)
            route_pe(pe, R1)
            att_pe(pe)
            experts_pe(pe, R1)


def layouts(v):
    c = np.ascontiguousarray

    def feat(w):
        return c(w.reshape(DC, P, -1).transpose(1, 0, 2))

    def w13_of(gate, up):
        w = np.concatenate([gate, up], axis=1).transpose(0, 2, 1)
        return c(w.reshape(-1, DC, P, 2 * INNER).transpose(0, 2, 1, 3))

    def w2_of(w):
        return c(w.transpose(0, 2, 1).reshape(-1, 2, IC, D).transpose(0, 2, 1, 3))

    se_g, se_u = v['L1_ffn_se_gate_up_w'][:SHARED * INNER], v['L1_ffn_se_gate_up_w'][SHARED * INNER:]
    w13l1 = np.concatenate([v['L1_ffn_w13'], np.concatenate([se_g.reshape(SHARED, INNER, D), se_u.reshape(SHARED, INNER, D)], axis=1)])
    w2l1 = np.concatenate([v['L1_ffn_w2'], v['L1_ffn_se_down_w'].reshape(D, SHARED, INNER).transpose(1, 0, 2)])

    def heads(w, n):
        return w.reshape(DC, P, HEADS, n).transpose(2, 1, 0, 3)
    q = np.concatenate([heads(v['L1_attn_wq_sem'], QK), heads(v['L1_attn_wq_geo'], QK)], axis=3)
    k = np.concatenate([heads(v['L1_attn_wk_sem'], QK), heads(v['L1_attn_wk_geo'], QK)], axis=3)
    wv = heads(v['L1_attn_wv'], P)
    half = QK // 2
    inv = (1.0 / 10000.0 ** (np.arange(half, dtype=np.float32) / np.float32(half))).astype(np.float32)
    ang = inv[:, None] * np.arange(SEQ, dtype=np.float32)[None]
    cos, sin = np.cos(ang).astype(np.float32), np.sin(ang).astype(np.float32)
    rope = np.stack([np.concatenate([np.ones((QK, SEQ), np.float32), cos, cos]),
                     np.concatenate([np.zeros((QK, SEQ), np.float32), -sin, sin])], axis=1)
    return {
        'x': c(v['L0_attn_x'].reshape(T, D)), 'a_log': feat(v['L0_attn_A_log']), 'd_param': c(v['L0_attn_D_param'].reshape(DC, P).T),
        'xproj': feat(v['L0_attn_x_proj_w'].T), 'dtproj': c(v['L0_attn_dt_proj_w'].T), 'dt_bias': c(v['L0_attn_dt_proj_b'].reshape(DC, P).T),
        'router0': feat(v['L0_ffn_router_w'].T), 'w13_0': w13_of(v['L0_ffn_gate_w'], v['L0_ffn_up_w']), 'w2_0': w2_of(v['L0_ffn_down_w']),
        'router1': feat(np.concatenate([v['L1_ffn_gate_w'], v['L1_ffn_shared_gate_w']]).T),
        'w13_1': w13_of(w13l1[:, :INNER], w13l1[:, INNER:]), 'w2_1': w2_of(w2l1),
        'wqkv': c(np.stack([q, k, wv], axis=2)), 'wo_h': c(v['L1_attn_wo'].reshape(HEADS, P, D)),
        'gate_logit': c(v['L1_attn_gate_logit'].reshape(1, HEADS)), 'rope': c(rope),
    }


ONLY0 = False


def kernel(**inputs):
    import concourse.bacc as _bacc
    from concourse.bass_utils import run_bass_kernel_spmd as _run

    nc = _bacc.Bacc("TRN2", target_bir_lowering=False, num_devices=1)
    arrays, args = {}, []
    for name, a in layouts({k: np.asarray(a) for k, a in inputs.items()}).items():
        arrays[f"in_{name}"] = a
        args.append(nc.dram_tensor(f"in_{name}", a.shape, mybir.dt.from_np(a.dtype), kind="ExternalInput").ap())
    args.append(nc.dram_tensor("out_0", (T, D), F32, kind="ExternalOutput").ap())
    build(nc, *args, only0=ONLY0)
    r = _run(nc, [arrays], core_ids=[0])
    return r.results[0]["out_0"].reshape(BATCH, SEQ, D)
```

```python
from contextlib import ExitStack

import numpy as np

import concourse.bass as bass
from concourse import mybir

F32 = mybir.dt.float32
F32R = mybir.dt.float32r
BF16 = mybir.dt.bfloat16
I32 = mybir.dt.int32
U32 = mybir.dt.uint32
ALU = mybir.AluOpType
ACT = mybir.ActivationFunctionType
AX = mybir.AxisListType

P = 128
BATCH, SEQ, D = 2, 1024, 256
T = BATCH * SEQ
NT = T // P
DC = D // P
NG = 4
GT = NT // NG
EPS = 1e-5

STATES, RANK = 16, 128
XD = RANK + 2 * STATES

INNER = 176
IC = INNER // 2
E0, E1 = 8, 60
K1 = 4
SHARED = 4
TILES0 = T // P + E0
TILES1 = T * K1 // P + E1
ALL1 = TILES1 + SHARED * NT
RING = 4
GU_BANK, DN_BANK = (5, 3), (7, 2)

HEADS, QK = 16, 64


class Route:
    def __init__(self, tiles_n, slots, result, etab_dram, w13_dram, w2_dram, routed, n_weights):
        self.tiles_n, self.routed, self.n_weights = tiles_n, routed, n_weights
        self.slots, self.result, self.etab_dram = slots, result, etab_dram
        self.w13_dram, self.w2_dram = w13_dram, w2_dram


def log1p_coefficients(n):
    z = (np.cos(np.pi * (np.arange(64) + 0.5) / 64) + 1) / 18
    s = np.sqrt(z)
    return [float(2 * c) for c in np.polynomial.chebyshev.Chebyshev.fit(z, np.arctanh(s) / s, n - 1, domain=[0, 1 / 9])
            .convert(kind=np.polynomial.Polynomial).coef]


def build(nc, x_in, a_log, d_param, xproj, dtproj, dt_bias, router0, w13_0, w2_0,
          router1, w13_1, w2_1, wqkv, wo_h, gate_logit, rope, out, only0=False):
    ctx = ExitStack()
    with ctx:
        def sb(name, shape, dt=F32):
            return ctx.enter_context(nc.sbuf_tensor(name, shape, dt))

        def sem(name):
            return ctx.enter_context(nc.semaphore(name))

        def dram(name, shape, dt=F32):
            return nc.dram_tensor(name, shape, dt).ap()

        ps = ctx.enter_context(nc.psum_tensor("ps", [P, 8, 512], F32))

        bc_rows = dram("bc_rows", [2 * STATES, T])
        sorted1 = dram("sorted1", [TILES1 * P, D])
        result1 = dram("result1", [TILES1 * P, D])
        etab1 = dram("etab1", [P, 1], I32)
        sorted0 = dram("sorted0", [TILES0 * P, D])
        result0 = dram("result0", [TILES0 * P, D])
        etab0 = dram("etab0", [P, 1], I32)
        xr = sb("xr", [P, NT, D])
        xn = sb("xn", [P, NT, D])
        ident = sb("ident", [P, P])
        ident_b = sb("ident_b", [P, P], BF16)
        before = sb("before", [P, P], BF16)
        ones_b = sb("ones_b", [P, P], BF16)
        zero_b = sb("zero_b", [P, P], BF16)
        iota_e = sb("iota_e", [P, E1])
        iota_p = sb("iota_p", [P, 1])
        neg_half = sb("neg_half", [P, NT])
        stat = sb("stat", [P, 4, NT])

        base0 = ExitStack()

        def sb0(name, shape, dt=F32):
            return base0.enter_context(nc.sbuf_tensor(name, shape, dt))

        zeros = sb0("zeros", [P, 2048])
        xnT = sb0("xnT", [P, DC, T])
        delta = sb0("delta", [P, DC, T])
        dx = sb0("dx", [P, DC, T])
        xpw = sb0("xpw", [P, DC, XD])
        dtw = sb0("dtw", [P, D])
        dtb = sb0("dtb", [P, DC])
        alog = sb0("alog", [P, DC, STATES])
        aneg = sb0("aneg", [P, DC, STATES])
        dpar = sb0("dpar", [P, DC])
        rw0 = sb0("rw0", [P, DC, E0])
        decay = sb0("decay", [P, 2, DC, SEQ])
        state = sb0("state", [P, 2, DC, SEQ])
        brow = sb0("brow", [P, 2, SEQ])
        crow = sb0("crow", [P, 2, SEQ])
        sq = state[:, 0].rearrange("p c t -> p (c t)")
        sp_x = decay[:, 0].rearrange("p c t -> p (c t)")
        sp_e = decay[:, 1].rearrange("p c t -> p (c t)")
        sp_s = state[:, 0].rearrange("p c t -> p (c t)")
        sp_z = state[:, 1].rearrange("p c t -> p (c t)")
        dtT = brow[:, :, :].rearrange("p a t -> p (a t)")
        bcT = crow[0:2 * STATES, :, :].rearrange("p a t -> p (a t)")

        def ring_buffers(r, n, alloc):
            r.w13 = alloc(f'w13r{n}', [P, RING, DC, 2 * INNER])
            r.w2 = alloc(f'w2r{n}', [IC, RING, 2, D])
            r.xs = alloc(f'xs{n}', [P, RING, D])
            r.xt = alloc(f'xt{n}', [P, 2, D])
            r.th = alloc(f'th{n}', [P, 2, INNER])
            r.ga = alloc(f'ga{n}', [P, 2, INNER])
            r.hh = alloc(f'hh{n}', [P, 2, INNER])
            r.ht = alloc(f'ht{n}', [IC, 2, 2, P])
            r.yy = alloc(f'yy{n}', [P, RING, D])
            r.got = alloc(f'got{n}', [P, 4, D])

        def route_buffers(r, n, e, k, alloc, el, keep_alloc):
            r.E = e
            r.K = k
            r.name = n
            r.EL = el
            r.logit = alloc(f'logit{n}', [P, NT, el])
            r.top = alloc(f'top{n}', [P, NT, 8])
            r.idx = alloc(f'idx{n}', [P, NT, 8], U32)
            r.idxf = alloc(f'idxf{n}', [P, NT, 8])
            r.hot = alloc(f'hot{n}', [P, k, e, NT], BF16)
            r.m = alloc(f'm{n}', [P, e, NT], BF16)
            r.keep = alloc(f'keep{n}', [P, e, NT], BF16)
            r.cum = alloc(f'cum{n}', [P, e, NT], BF16)
            r.cumx = alloc(f'cumx{n}', [P, e, NT], BF16)
            r.rank = alloc(f'rank{n}', [P, e, NT])
            r.prod = alloc(f'prod{n}', [P, e, NT])
            r.cnti = alloc(f'cnti{n}', [P, e], I32)
            r.tiles = alloc(f'tiles{n}', [P, e])
            r.upto = alloc(f'upto{n}', [P, e])
            r.base = alloc(f'base{n}', [P, e])
            r.slotf = alloc(f'slotf{n}', [P, k, NT])
            r.slot = keep_alloc(f'slot{n}', [P, k, NT], U32)
            r.weight = keep_alloc(f'weight{n}', [P, NT, 8])
            r.ecol = alloc(f'ecol{n}', [P, 2])
            r.ecoli = keep_alloc(f'ecoli{n}', [P, 1], I32)
            r.ecmp = alloc(f'ecmp{n}', [P, e])
            r.logits_ready = sem(f'logits_ready{n}')
            r.step = sem(f'route_step{n}')
            r.ranks_ready = sem(f'ranks_ready{n}')
            r.m_ready = sem(f'm_ready{n}')
            r.slots_ready = sem(f'slots_ready{n}')
            r.scattered = sem(f'scattered{n}')
            r.tiles_known = sem(f'tiles_known{n}')
            r.table_stored = sem(f'table_stored{n}')
            r.table_loaded = sem(f'table_loaded{n}')
            r.zeroed = sem(f'zeroed{n}')
            r.etab = keep_alloc(f'etabrow{n}', [1, 192], I32)
            r.x_loaded = [sem(f'tokens_loaded{n}_{q}') for q in range(RING)]
            r.w13_loaded = [sem(f'w13_loaded{n}_{q}') for q in range(RING)]
            r.w2_loaded = [sem(f'w2_loaded{n}_{q}') for q in range(RING)]
            r.shared_added = sem(f'shared_added{n}')
            r.xt_ready = sem(f'xt_ready{n}')
            r.xt_copied = sem(f'xt_copied{n}')
            r.gu_ready = sem(f'gu_ready{n}')
            r.tanh_ready = sem(f'tanh_ready{n}')
            r.act_step = sem(f'gated{n}')
            r.h_done = sem(f'h_done{n}')
            r.ht_ready = sem(f'ht_ready{n}')
            r.ht_copied = sem(f'ht_copied{n}')
            r.dn_done = sem(f'dn_done{n}')
            r.y_copied = sem(f'y_copied{n}')
            r.stored = [sem(f'y_stored{n}_{q}') for q in range(RING)]
            r.gathered = [sem(f'gathered{n}_{q}') for q in range(4)]
            r.added = sem(f'added{n}')

        R0 = Route(TILES0, sorted0, result0, etab0, w13_0, w2_0, TILES0, E0)
        route_buffers(R0, 0, E0, 1, sb0, E0, sb0)
        ring_buffers(R0, 0, sb0)

        base0.close()

        def sbk(name, shape, dt=F32):
            return ctx1.enter_context(nc.sbuf_tensor(name, shape, dt))
        ctx1 = ExitStack()
        xnr = sbk("xnr", [P, DC, T], F32R)
        xnl = sbk("xnl", [P, DC, T], F32R)
        xnT1 = sbk("xnT1", [P, DC, T])
        gsc = sbk("gsc", [P, 2, HEADS])
        rowsum = sbk("rowsum", [P, 2, 8])
        rinv = sbk("rinv", [P, 2, 8])
        negmax = sbk("negmax", [P, 2, 8])
        rw1 = sbk("rw1", [P, DC, E1 + 1])
        keep1 = {}

        def alloc_keep1(name, shape, dt=F32):
            return sbk(name, shape, dt)
        kslot = alloc_keep1

        att = ExitStack()

        def sba(name, shape, dt=F32):
            return att.enter_context(nc.sbuf_tensor(name, shape, dt))
        slot_w = kslot("slot1", [P, K1, NT], U32)
        weight_w = kslot("weight1", [P, NT, 8])
        ecoli_w = kslot("ecoli1", [P, 1], I32)
        etab_w = kslot("etabrow1", [1, 192], I32)
        kept = {"slot1": slot_w, "weight1": weight_w, "ecoli1": ecoli_w, "etabrow1": etab_w}
        wraw = sba("wraw", [P, 3, DC, P])
        wr = sba("wr", [P, 2, DC, P], F32R)
        wl = sba("wl", [P, 2, DC, P], F32R)
        wv = sba("wv", [P, DC, P])
        woraw = sba("woraw", [P, D])
        wo = sba("wo", [P, D])
        rope_t = sba("rope_t", [P, 2, SEQ])
        qkr = sba("qkr", [P, 2, 2, SEQ], F32R)
        qkl = sba("qkl", [P, 2, 2, SEQ], F32R)
        v = sba("v", [P, 2, 8, P])
        ot = sba("ot", [P, 512])
        t1 = sba("t1", [P, 2, 512])
        sw = sba("sw", [P, 2, 512])
        maskb = sba("maskb", [P, P], BF16)
        over = ExitStack()

        def sbo(name, shape, dt=F32):
            return over.enter_context(nc.sbuf_tensor(name, shape, dt))
        pb = sbo("pb", [P, 2, SEQ])
        pt = [sbo("pt0", [P, 4, 512]), sbo("pt1", [P, 8, 512])]
        over.close()
        over2 = ExitStack()
        R1 = Route(ALL1, sorted1, result1, etab1, w13_1, w2_1, TILES1, E1 + SHARED)
        route_buffers(R1, 1, E1, K1, lambda n, sh, dt=F32: over2.enter_context(nc.sbuf_tensor(n, sh, dt)), E1 + 1,
                            lambda n, sh, dt=F32: kept[n])
        over2.close()
        att.close()
        over3 = ExitStack()
        ring_buffers(R1, 1, lambda n, sh, dt=F32: over3.enter_context(nc.sbuf_tensor(n, sh, dt)))
        over3.close()
        ctx1.close()

        s_x = [sem(f"x_loaded{g}") for g in range(NG)]
        s_par = sem("params_loaded")
        s_const = sem("consts_made")
        s_ln = sem("ln_step")
        s_sq = sem("squares_ready")
        s_var = sem("variance_ready")
        s_rstd = sem("rstd_ready")
        s_cen = sem("centred")
        s_xn = sem("xn_ready")
        s_xnT_ps = sem("xnT_in_psum")
        s_xnT = sem("xnT_ready")
        s_xd = sem("xdbl_in_psum")
        s_xdc = sem("xdbl_copied")
        s_bc = sem("bc_rows_stored")
        s_dp = sem("dt_in_psum")
        s_dpc = sem("dt_biased")
        s_sp = sem("softplus_step")
        s_spa = sem("softplus_act_step")
        s_delta = sem("delta_ready")
        s_row = [sem(f"rows_loaded{r}") for r in range(2)]
        s_dec = sem("decay_ready")
        s_dbx = sem("input_term_ready")
        s_scan = sem("scanned")
        s_hc = sem("hc_ready")
        s_ysum = sem("y_summed")
        s_aneg = sem("a_ready")
        s_yT = sem("yT_ready")
        s_yT_ps = sem("y_rows_in_psum")
        s_yadd = sem("y_rows_added")
        s_out = sem("out_stored")

        s_mask = sem("mask_made")
        s_par1 = sem("params1_loaded")
        s_gate = sem("gate_step")
        s_gact = sem("gate_exp")
        s_xnT1_ps = sem("xn1T_in_psum")
        s_xnT1 = sem("xn1T_copied")
        s_split = sem("xn1_split")
        s_wraw = sem("head_weights_loaded")
        s_wsc = sem("head_weights_scaled")
        s_ws = sem("head_weights_split")
        s_wor = sem("wo_loaded")
        s_wos = sem("wo_split")
        s_rnd = sem("weights_rounded")
        s_S = sem("scores_ready")
        s_max = sem("max_ready")
        s_exp = sem("exp_ready")
        s_T = sem("probs_transposed")
        s_pr = sem("probs_rounded")
        s_pl = sem("probs_split")
        s_b6 = sem("bank6_filled")
        s_a6 = sem("bank6_rounded")
        s_e6 = sem("bank6_taken")
        s_b7 = sem("bank7_filled")
        s_a7 = sem("bank7_rounded")
        s_e7 = sem("bank7_taken")
        s_t2 = sem("rotated")
        s_rot = sem("rotation_added")
        s_qr = sem("qk_rounded")
        s_ql = sem("qk_split")
        s_rinv = sem("sums_inverted")
        s_w1 = sem("weights1_step")
        s_w1a = sem("weights1_exp")

        COEF = log1p_coefficients(5)

        def w(eng, s, value):
            if not isinstance(value, int) or value > 0:
                eng.wait_ge(s, value)

        def route_dve(v, r):
            n = [0]

            def step(ins):
                n[0] += 1
                ins.then_inc(r.step, 1)
                v.wait_ge(r.step, n[0])

            v.wait_ge(r.logits_ready, 1)
            for i in range(NT):
                last = v.tensor_copy(r.logit[:, i, :], ps[:, 4 + i // 8, (i % 8) * r.EL:(i % 8 + 1) * r.EL])
            step(last)
            for i in range(NT):
                last = v.max(r.top[:, i, :], r.logit[:, i, 0:r.E])
            step(last)
            for i in range(NT):
                last = v.max_index(r.idx[:, i, :], r.top[:, i, :], r.logit[:, i, 0:r.E])
            step(last)
            step(v.tensor_copy(r.idxf[:], r.idx[:]))
            for k in range(r.K):
                last = v.tensor_tensor(r.hot[:, k], iota_e[:, 0:r.E].unsqueeze(2).to_broadcast([P, r.E, NT]),
                                       r.idxf[:, :, k].unsqueeze(1).to_broadcast([P, r.E, NT]), ALU.is_equal)
            step(last)
            if r.K == 1:
                step(v.tensor_copy(r.m[:], r.hot[:, 0]))
            else:
                step(v.tensor_tensor(r.m[:], r.hot[:, 0], r.hot[:, 1], ALU.add))
                for k in range(2, r.K):
                    step(v.tensor_tensor(r.m[:], r.m[:], r.hot[:, k], ALU.add))
            step(v.memset(r.keep[:], 1.0))
            step(v.memset(r.keep[:, :, 0:1], 0.0))
            step(v.tensor_tensor_scan(r.cum[:].rearrange("p e i -> p (e i)"), r.keep[:].rearrange("p e i -> p (e i)"),
                                      r.m[:].rearrange("p e i -> p (e i)"), 0.0, ALU.mult, ALU.add))
            v.tensor_tensor(r.cumx[:], r.cum[:], r.m[:], ALU.subtract).then_inc(r.m_ready, 1)
            v.wait_ge(r.ranks_ready, 1)
            step(v.tensor_scalar(r.cnti[:], ps[:, 6, 0:r.E], float(P - 1), None, ALU.add))
            step(v.tensor_scalar(r.cnti[:], r.cnti[:], 7, None, ALU.arith_shift_right))
            step(v.tensor_copy(r.tiles[:], r.cnti[:]))
            step(v.tensor_tensor_scan(r.upto[:], r.ecmp[:], r.tiles[:], 0.0, ALU.mult, ALU.add))
            step(v.tensor_tensor(r.base[:], r.upto[:], r.tiles[:], ALU.subtract))
            step(v.tensor_scalar(r.base[:], r.base[:], float(P), None, ALU.mult))
            half = r.E // 2
            for c in range(2):
                last = v.tensor_tensor(r.rank[:, c * half:(c + 1) * half],
                                       ps[:, 4 + c, 0:half * NT].rearrange("p (e i) -> p e i", i=NT),
                                       r.base[:, c * half:(c + 1) * half].unsqueeze(2).to_broadcast([P, half, NT]), ALU.add)
            step(last)
            for k in range(r.K):
                step(v.tensor_tensor(r.prod[:], r.rank[:], r.hot[:, k], ALU.mult))
                step(v.tensor_reduce(r.slotf[:, k, :], r.prod[:].rearrange("p e i -> p i e"), AX.X, ALU.add))
            v.tensor_copy(r.slot[:], r.slotf[:]).then_inc(r.slots_ready, 1)
            step(v.tensor_scalar(r.ecmp[:], r.upto[:], iota_p[:, 0:1], None, ALU.is_le))
            step(v.tensor_reduce(r.ecol[:, 0:1], r.ecmp[:], AX.X, ALU.add))
            step(v.tensor_scalar(r.ecol[:, 1:2], r.ecol[:, 0:1], float(r.E - 1), None, ALU.min))
            v.tensor_copy(r.ecoli[:], r.ecol[:, 1:2]).then_inc(r.tiles_known, 1)
            return step

        def route_pe(pe, r):
            pe.wait_ge(r.m_ready, 1)
            half = r.E // 2
            for c in range(2):
                o = ps[:, 4 + c, 0:half * NT]
                mm = r.m[:, c * half:(c + 1) * half].rearrange("p e i -> p (e i)")
                cx = r.cumx[:, c * half:(c + 1) * half].rearrange("p e i -> p (e i)")
                pe.matmul(o, before[:], mm, start=True, stop=False)
                pe.matmul(o, ones_b[:], cx, start=False, stop=True)
            pe.matmul(ps[:, 6, 0:r.E], ones_b[:], r.cum[:, :, NT - 1], start=True, stop=True).then_inc(r.ranks_ready, 1)

        def route_pool(g, r):
            g.wait_ge(r.zeroed, 16 * r.zero_dmas)
            g.wait_ge(r.slots_ready, 1)
            for k in range(r.K):
                for i in range(NT):
                    g.indirect_dma_start(r.slots, bass.IndirectOffsetOnAxis(ap=r.slot[:, k, i:i + 1], axis=0),
                                         xn[:, i, :], None).then_inc(r.scattered, 16)

        def route_sp(sp, r):
            sp.wait_ge(r.tiles_known, 1)
            sp.dma_start(r.etab_dram, r.ecoli[:]).then_inc(r.table_stored, 16)
            sp.wait_ge(r.table_stored, 16)
            sp.dma_start(r.etab[0:1, 0:r.routed], r.etab_dram[0:r.routed, :].rearrange("p o -> o p")).then_inc(r.table_loaded, 16)
            sp.wait_ge(r.table_loaded, 16)
            sp.wait_ge(r.scattered, 16 * NT * r.K)

        def zero_fill(sp, r):
            rows = 1024
            total = r.routed * P
            r.zero_dmas = -(-total // rows)
            for q in range(r.zero_dmas):
                n = min(rows, total - q * rows)
                sp.dma_start(r.slots[q * rows:q * rows + n, :].rearrange("(p a) d -> p (a d)", p=P),
                             zeros[:, 0:n * D // P]).then_inc(r.zeroed, 16)

        def tile_steps(eng, r, fn):
            first_shared, end = r.routed // RING, r.tiles_n // RING

            def out(i):
                for q in range(RING):
                    def kind(a, s=i * RING + q):
                        return None if s < a or s - a >= r.tiles_n else 'routed' if s - a < r.routed else 'shared'
                    fn(i, q, kind)

            def loop(lo, hi, what):
                with eng.Fori(lo, hi) as i:
                    for q in range(RING):
                        fn(i, q, lambda a: what)
            out(0)
            out(1)
            loop(2, first_shared, 'routed')
            if end > first_shared:
                out(first_shared)
                out(first_shared + 1)
                loop(first_shared + 2, end, 'shared')
            out(end)
            out(end + 1)

        def experts_sp(sp, r):
            def fn(i, q, kind):
                s = i * RING + q
                if kind(0):
                    if kind(0) == 'routed':
                        e = sp.value_load(r.etab[0:1, bass.ds(s, 1)], min_val=0, max_val=r.n_weights - 1)
                    w(sp, r.gu_ready, s - 3)
                    if kind(0) == 'routed':
                        sp.dma_start(r.xs[:, q], r.slots[bass.ds(s * P, P), :]).then_inc(r.x_loaded[q], 16)
                        sp.dma_start(r.w13[:, q], r.w13_dram[bass.ds(e, 1)].rearrange("o p c n -> (o p) c n")).then_inc(r.w13_loaded[q], 16)
                    else:
                        token_tile = i - r.routed // RING
                        sp.dma_start(r.xs[:, q], xn[:, bass.ds(token_tile, 1), :].rearrange("p o d -> p (o d)")).then_inc(r.x_loaded[q], 16)
                        if isinstance(i, int) and s < r.routed + SHARED:
                            sp.dma_start(r.w13[:, q], r.w13_dram[r.E + q]).then_inc(r.w13_loaded[q], 16)
            tile_steps(sp, r, fn)

        def experts_pool(g, r):
            def load(i, q):
                s = i * RING + q
                e = g.value_load(r.etab[0:1, bass.ds(s, 1)], min_val=0, max_val=r.n_weights - 1)
                w(g, r.dn_done, s - 3)
                g.dma_start(r.w2[:, q], r.w2_dram[bass.ds(e, 1)].rearrange("o p c n -> (o p) c n")).then_inc(r.w2_loaded[q], 16)
            g.wait_ge(r.table_loaded, 16)
            for q in range(RING):
                load(0, q)
            with g.Fori(1, r.routed // RING) as i:
                for q in range(RING):
                    load(i, q)
            if r.tiles_n > r.routed:
                for q in range(SHARED):
                    g.wait_ge(r.dn_done, r.routed + q - 3)
                    g.dma_start(r.w2[:, q], r.w2_dram[r.E + q]).then_inc(r.w2_loaded[q], 16)

        def experts_pe(pe, r):
            uses = r.routed // RING

            def fn(i, q, kind):
                s = i * RING + q
                if kind(0):
                    pe.wait_ge(r.x_loaded[q], (i + 1) * 16)
                    w(pe, r.xt_copied, s)
                    for c in range(DC):
                        last = pe.transpose(ps[:, 4, c * P:(c + 1) * P], r.xs[:, q, c * P:(c + 1) * P], ident[:])
                    last.then_inc(r.xt_ready, 1)
                if kind(1):
                    b = (q - 1) % RING
                    turn = i + (q - 1) // RING
                    if kind(1) == 'routed' or isinstance(i, int) and turn == uses:
                        pe.wait_ge(r.w13_loaded[b], (turn + 1) * 16)
                    pe.wait_ge(r.xt_copied, s)
                    w(pe, r.h_done, s - 2)
                    for c in range(DC):
                        last = pe.matmul(ps[:, GU_BANK[b % 2], 0:2 * INNER], r.xt[:, b % 2, c * P:(c + 1) * P], r.w13[:, b, c],
                                         start=c == 0, stop=c == DC - 1)
                    last.then_inc(r.gu_ready, 1)
                if kind(2):
                    b = (q - 2) % RING
                    pe.wait_ge(r.h_done, s - 1)
                    w(pe, r.ht_copied, s - 2)
                    for c in range(2):
                        last = pe.transpose(ps[0:IC, 6, c * P:(c + 1) * P], r.hh[:, b % 2, c * IC:(c + 1) * IC], ident[:])
                    last.then_inc(r.ht_ready, 1)
                if kind(3):
                    b = (q - 3) % RING
                    turn = i + (q - 3) // RING
                    pe.wait_ge(r.ht_copied, s - 2)
                    if kind(3) == 'routed':
                        pe.wait_ge(r.w2_loaded[b], (turn + 1) * 16)
                        w(pe, r.y_copied, s - 4)
                        bank, begins, ends = DN_BANK[b % 2], True, True
                    else:
                        if isinstance(i, int) and turn == uses:
                            pe.wait_ge(r.w2_loaded[b], (turn + 1) * 16)
                        if b == 0:
                            if isinstance(i, int) and turn == uses:
                                pe.wait_ge(r.y_copied, r.routed)
                            else:
                                pe.wait_ge(r.shared_added, turn - uses)
                        bank, begins, ends = DN_BANK[0], b == 0, b == SHARED - 1
                    for c in range(2):
                        last = pe.matmul(ps[:, bank, 0:D], r.ht[:, b % 2, c], r.w2[:, b, c],
                                         start=begins and c == 0, stop=ends and c == 1)
                    last.then_inc(r.dn_done, 1)
            tile_steps(pe, r, fn)

        def experts_act(act, r):
            def fn(i, q, kind):
                s = i * RING + q
                if kind(0):
                    act.wait_ge(r.xt_ready, s + 1)
                    w(act, r.gu_ready, s - 1)
                    act.copy(r.xt[:, q % 2], ps[:, 4, 0:D]).then_inc(r.xt_copied, 1)
                if kind(1):
                    b = (q - 1) % 2
                    act.wait_ge(r.gu_ready, s)
                    w(act, r.act_step, s - 2)
                    act.activation(r.th[:, b], ps[:, GU_BANK[b], 0:INNER], ACT.Tanh, scale=0.5).then_inc(r.tanh_ready, 1)
                if kind(3) == 'routed':
                    b = (q - 3) % RING
                    act.wait_ge(r.dn_done, s - 2)
                    w(act, r.stored[b], (i + (q - 3) // RING) * 16)
                    act.copy(r.yy[:, b], ps[:, DN_BANK[b % 2], 0:D]).then_inc(r.y_copied, 1)
                if kind(4) == 'routed':
                    b = (q - 4) % RING
                    act.wait_ge(r.y_copied, s - 3)
                    act.dma_start(r.result[bass.ds((s - 4) * P, P), :], r.yy[:, b]).then_inc(r.stored[b], 16)
            tile_steps(act, r, fn)

        def experts_dve(v, r):
            def add_result(i, k):
                n = i * r.K + k
                v.wait_ge(r.gathered[k], 16 * (i + 1))
                w(v, r.added, n)
                if k == 0:
                    v.wait_ge(r.shared_added, i + 1)
                xi = xr[:, bass.ds(i, 1), :].rearrange("p o d -> p (o d)")
                v.scalar_tensor_tensor(xi, r.got[:, k, :], r.weight[:, bass.ds(i, 1), k], xi, ALU.mult, ALU.add).then_inc(r.added, 1)

            def fn(i, q, kind):
                s = i * RING + q
                if kind(1):
                    b = (q - 1) % 2
                    v.wait_ge(r.tanh_ready, s)
                    v.scalar_tensor_tensor(r.ga[:, b], r.th[:, b], 1.0, ps[:, GU_BANK[b], 0:INNER], ALU.add, ALU.mult).then_inc(r.act_step, 1)
                    v.wait_ge(r.act_step, s)
                    w(v, r.ht_ready, s - 2)
                    v.scalar_tensor_tensor(r.hh[:, b], r.ga[:, b], 0.5, ps[:, GU_BANK[b], INNER:2 * INNER], ALU.mult, ALU.mult).then_inc(r.h_done, 1)
                if kind(2):
                    b = (q - 2) % 2
                    v.wait_ge(r.ht_ready, s - 1)
                    w(v, r.dn_done, s - 3)
                    v.tensor_copy(r.ht[:, b].rearrange("p c t -> p (c t)"), ps[0:IC, 6, 0:2 * P]).then_inc(r.ht_copied, 1)
                if kind(3) == 'shared' and q == 2:
                    token_tile = i - 1 - r.routed // RING
                    v.wait_ge(r.dn_done, s - 2)
                    xi = xr[:, bass.ds(token_tile, 1), :].rearrange("p o d -> p (o d)")
                    v.scalar_tensor_tensor(xi, ps[:, DN_BANK[0], 0:D], r.weight[:, bass.ds(token_tile, 1), r.K], xi,
                                           ALU.mult, ALU.add).then_inc(r.shared_added, 1)
                if r.tiles_n > r.routed and (not isinstance(i, int) and kind(0) == 'shared' or isinstance(i, int) and i >= r.tiles_n // RING):
                    add_result(i - 2 - r.routed // RING, q)
            tile_steps(v, r, fn)

        def gather_pool(g, r):
            for q in range(RING):
                g.wait_ge(r.stored[q], 16 * r.routed // RING)
            n = 0
            for i in range(NT):
                for k in range(r.K):
                    if n >= 4:
                        g.wait_ge(r.added, n - 3)
                    g.indirect_dma_start(r.got[:, n % 4, :], None, r.result[:, :],
                                         bass.IndirectOffsetOnAxis(ap=r.slot[:, k, i:i + 1], axis=0)).then_inc(r.gathered[n % 4], 16)
                    n += 1

        def gather_dve(v, r):
            n = 0
            for i in range(NT):
                for k in range(r.K):
                    v.wait_ge(r.gathered[n % 4], 16 * (n // 4 + 1))
                    if k > 0:
                        v.wait_ge(r.added, n)
                    v.scalar_tensor_tensor(xr[:, i, :], r.got[:, n % 4, :], r.weight[:, i, k:k + 1], xr[:, i, :],
                                           ALU.mult, ALU.add).then_inc(r.added, 1)
                    n += 1

        ITS = BATCH * HEADS

        def chunk_of(qt):
            return qt if qt < 4 else 4 + 2 * (qt - 4)

        def chunks(qt):
            return [(chunk_of(qt) + j // 4, j, min(j + 4, qt + 1)) for j in range(0, qt + 1, 4)]
        CHUNKS = 12

        def use7(it, n):
            return 5 + 5 * it + n + 1

        OUT1, W2, W3, OUT0, W0, W1, VHALF = range(7)

        def use6(it, n):
            return 7 * it + n - 1 if not (isinstance(it, int) and it == ITS) else 7 * it + n - 2

        def heads_loop(eng, body):
            for b in range(BATCH):
                body(0, b, False)
            with eng.Fori(1, HEADS - 1) as h:
                for b in range(BATCH):
                    body(h, b, False)
            for b in range(BATCH):
                body(HEADS - 1, b, b == BATCH - 1)

        def first(it):
            return isinstance(it, int) and it == 0

        def three(pe, out_ap, a_r, a_l, b_r, b_l, start, stop):
            pe.matmul(out_ap, a_r, b_r, start=start, stop=False)
            pe.matmul(out_ap, a_l, b_r, start=False, stop=False)
            return pe.matmul(out_ap, a_r, b_l, start=False, stop=stop)

        def att_pe(pe):
            def scores(it, qt, buf):
                w(pe, s_exp, 8 * it + qt - 1)
                if qt == 4:
                    w(pe, s_ql, 4 * it + 4)
                if qt == 8:
                    w(pe, s_ql, 4 * it + 6)
                qn = qt % 8
                bank = 2 * (qt % 2)
                for c in range(0, qn + 1, 4):
                    cols = min(4, qn + 1 - c) * P
                    o = ps[:, bank + c // 4, 0:cols]
                    qs = slice(qn * P, (qn + 1) * P)
                    ks = slice(c * P, c * P + cols)
                    last = three(pe, o, qkr[:, buf, 0, qs], qkl[:, buf, 0, qs], qkr[:, buf, 1, ks], qkl[:, buf, 1, ks],
                                 True, qn // 4 != c // 4)
                    if qn // 4 == c // 4:
                        last = pe.matmul(ps[:, bank + c // 4, (qn - c) * P:(qn - c + 1) * P], ident_b[:], maskb[:], start=False, stop=True)
                last.then_inc(s_S, 1)

            def piece(p, target_b, count):
                w(pe, s_e7, count - 1)
                which, half = p % 2, p // 2
                sl = slice(target_b * SEQ + half * 512, target_b * SEQ + half * 512 + 512)
                for c in range(DC):
                    last = three(pe, ps[:, 7, :], wr[:, which, c], wl[:, which, c], xnr[:, c, sl], xnl[:, c, sl], c == 0, c == DC - 1)
                last.then_inc(s_b7, 1)

            def v_half(half, bank, target_b, s_fill):
                for i in range(4):
                    t0 = target_b * SEQ + (half * 4 + i) * P
                    for c in range(DC):
                        last = pe.matmul(ps[:, bank, i * P:(i + 1) * P], xnT1[:, c, t0:t0 + P], wv[:, c], start=c == 0, stop=c == DC - 1)
                last.then_inc(s_fill, 1)

            def transposes(it, qt):
                w(pe, s_exp, 8 * it + qt + 1)
                for ci, j0, j1 in chunks(qt):
                    if j0 == 4 and qt > 4:
                        pe.wait_ge(s_pl, 4 * it + qt - 4)
                    elif j0 == 4:
                        pe.wait_ge(s_pr, 8 * it + 4)
                    elif qt == 1:
                        w(pe, s_pl, 4 * it)
                    elif qt >= 5 or qt == 0:
                        w(pe, s_pr, 8 * it + qt)
                    else:
                        w(pe, s_pr, 8 * it + qt - 1)
                    for j in range(j0, j1):
                        last = pe.transpose(ps[:, 4 + ci % 2, (j - j0) * P:(j - j0 + 1) * P], pb[:, qt % 2, j * P:(j + 1) * P], ident[:])
                    last.then_inc(s_T, 1)

            def output(g, buf, keys):
                for j in keys:
                    c0 = max(0, j - 4 * g) * P
                    last = pe.matmul(ps[:, 6, c0:512], v[:, buf, j], pt[g][:, j, c0:512], start=j == 0, stop=j == 4 * g + 3)
                if keys[-1] == 4 * g + 3:
                    last.then_inc(s_b6, 1)

            def project_out(which, count):
                w(pe, s_e6, count - 1)
                for a in range(2):
                    sl = slice((2 * (which % 2) + a) * P, (2 * (which % 2) + a + 1) * P)
                    last = pe.matmul(ps[:, 6, a * D:(a + 1) * D], ot[:, sl], wo[:], start=True, stop=True)
                last.then_inc(s_b6, 1)

            def output1(it, b, part):
                if part == 0:
                    w(pe, s_e6, use6(it, OUT1) - 1)
                    pe.wait_ge(s_pr, 8 * it)
                    pe.wait_ge(s_pl, 4 * it)
                output(1, 1 - b, (range(0, 3), range(3, 8))[part])

            pe.wait_ge(s_split, 2 * NG)
            pe.wait_ge(s_ws, 1)
            for p in range(4):
                piece(p, 0, p + 1)
            pe.wait_ge(s_e7, 4)
            v_half(1, 6, 0, s_b6)
            v_half(0, 7, 0, s_b7)
            pe.wait_ge(s_mask, 1)
            pe.wait_ge(s_ql, 4)
            scores(0, 0, 0)
            scores(0, 1, 0)

            def body(h, b, last):
                it = 2 * h + b
                for qt in range(8):
                    transposes(it, qt)
                    if qt < 6:
                        scores(it, qt + 2, b)
                    elif not last:
                        scores(it, qt + 2, 1 - b)
                    if qt in (0, 1) and not first(it):
                        output1(it, b, qt)
                    if qt in (2, 3, 5, 6) and not last:
                        if qt == 2 and b == BATCH - 1:
                            pe.wait_ge(s_ws, h + 2)
                        p = {2: 0, 3: 1, 5: 2, 6: 3}[qt]
                        piece(p, 1 - b, use7(it, p))
                    if qt in (2, 3) and not first(it):
                        project_out(qt, use6(it, W2 if qt == 2 else W3))
                    if qt == 4:
                        w(pe, s_e7, use7(it - 1, 4))
                        w(pe, s_e6, use6(it, OUT0) - 1)
                        pe.wait_ge(s_pr, 8 * it + 4)
                        output(0, b, range(0, 4))
                    if qt in (5, 6):
                        if qt == 5 and b == 0:
                            pe.wait_ge(s_wos, h + 1)
                        project_out(qt - 5, use6(it, W0 if qt == 5 else W1))
                    if qt == 7 and not last:
                        pe.wait_ge(s_e6, use6(it, VHALF) - 1)
                        v_half(1, 6, 1 - b, s_b6)
                        pe.wait_ge(s_e7, use7(it, 4) - 1)
                        v_half(0, 7, 1 - b, s_b7)
            heads_loop(pe, body)
            for part in range(2):
                output1(ITS, 0, part)
            for which, n in ((2, W2), (3, W3)):
                project_out(which, use6(ITS, n))

        def att_act(act):
            def probs(it, qt):
                act.wait_ge(s_T, CHUNKS * it + chunk_of(qt) + 1)
                if qt == 0:
                    w(act, s_b6, use6(it - 1, OUT0))
                if qt == 4:
                    w(act, s_b6, use6(it, OUT1))
                g, j1 = qt // 4, min(4, qt + 1)
                cols = slice((qt % 4) * P, (qt % 4 + 1) * P)
                act.copy(pt[g][:, 0:j1, cols], ps[:, 4 + chunk_of(qt) % 2, 0:j1 * P].rearrange("p (j q) -> p j q", q=P)).then_inc(s_pr, 1)

            def exp_tile(it, qt, b):
                w(act, s_max, 8 * it + qt + 1)
                if qt >= 2:
                    act.wait_ge(s_T, CHUNKS * it + chunk_of(qt - 2) + len(chunks(qt - 2)))
                else:
                    w(act, s_T, CHUNKS * it - (2, 0)[qt])
                qn, par = qt % 8, b if qt < 8 else 1 - b
                cols = (qn + 1) * P
                bank = 2 * (qt % 2)
                act.activation(pb[:, qt % 2, 0:cols], ps[:, bank:bank + 2, :].rearrange("p a n -> p (a n)")[:, 0:cols], ACT.Exp,
                               bias=negmax[:, par, qn:qn + 1], accum_out=rowsum[:, par, qn:qn + 1]).then_inc(s_exp, 1)

            def swap(n, p, count):
                act.wait_ge(s_b7, count)
                w(act, s_rot, n - 1)
                act.copy(sw[64:96, p % 2, :], ps[96:128, 7, :])
                act.copy(sw[96:128, p % 2, :], ps[64:96, 7, :]).then_inc(s_a7, 1)

            def rounded(n, p, buf):
                act.wait_ge(s_rot, n + 1)
                act.copy(qkr[:, buf, p % 2, (p // 2) * 512:(p // 2 + 1) * 512], t1[:, p % 2, :]).then_inc(s_qr, 1)

            def v_first(buf, count):
                act.wait_ge(s_b7, count)
                act.copy(v[:, buf, 0:4, :].rearrange("p i d -> p (i d)"), ps[:, 7, :]).then_inc(s_e7, 1)

            def output1(it):
                act.wait_ge(s_b6, use6(it, OUT1))
                act.copy(ot[:], ps[:, 6, :]).then_inc(s_e6, 1)

            for p in range(4):
                swap(p, p, p + 1)
                rounded(p, p, 0)
            v_first(0, 5)
            exp_tile(0, 0, 0)

            def body(h, b, last):
                it = 2 * h + b
                n0 = 4 * (it + 1)
                for qt in range(8):
                    probs(it, qt)
                    if qt < 7 or not last:
                        exp_tile(it, qt + 1, b)
                    if qt == 1 and not first(it):
                        output1(it)
                    if qt in (2, 3, 5, 6) and not last:
                        p = {2: 0, 3: 1, 5: 2, 6: 3}[qt]
                        swap(n0 + p, p, use7(it, p))
                    if qt in (3, 4, 6, 7) and not last:
                        p = {3: 0, 4: 1, 6: 2, 7: 3}[qt]
                        rounded(n0 + p, p, 1 - b)
                    if qt == 7 and not last:
                        v_first(1 - b, use7(it, 4))
            heads_loop(act, body)
            output1(ITS)

        def att_dve(dve):
            def max_tile(it, qt, b):
                qn, par = qt % 8, b if qt < 8 else 1 - b
                cols = (qn + 1) * P
                bank = 2 * (qt % 2)
                dve.wait_ge(s_S, 8 * it + qt + 1)
                dve.tensor_reduce(negmax[:, par, qn:qn + 1], ps[:, bank:bank + 2, :].rearrange("p a n -> p (a n)")[:, 0:cols], AX.X, ALU.max,
                                  negate=True).then_inc(s_max, 1)

            def probs(it, qt):
                dve.wait_ge(s_T, CHUNKS * it + chunk_of(qt) + 2)
                cols = slice((qt % 4) * P, (qt % 4 + 1) * P)
                if qt == 4:
                    w(dve, s_b6, use6(it, OUT1))
                dve.tensor_copy(pt[1][:, 4:qt + 1, cols], ps[:, 5, 0:(qt - 3) * P].rearrange("p (j q) -> p j q", q=P)).then_inc(s_pl, 1)

            def turned(n, p):
                dve.wait_ge(s_a7, n + 1)
                w(dve, s_ql, n - 1)
                dve.tensor_tensor(t1[:, p % 2, :], ps[:, 7, :], rope_t[:, 0, (p // 2) * 512:(p // 2 + 1) * 512], ALU.mult).then_inc(s_e7, 1)

            def rest(n, p, buf):
                dve.wait_ge(s_qr, n + 1)
                o = (slice(None), buf, p % 2, slice((p // 2) * 512, (p // 2 + 1) * 512))
                dve.tensor_tensor(qkl[o], t1[:, p % 2, :], qkr[o].bitcast(F32), ALU.subtract).then_inc(s_ql, 1)

            def v_second(buf, count):
                dve.wait_ge(s_b6, count)
                dve.tensor_copy(v[:, buf, 4:8, :].rearrange("p i d -> p (i d)"), ps[:, 6, :]).then_inc(s_e6, 1)

            def add_out(which, b_out, count):
                dve.wait_ge(s_b6, count)
                for a in range(2):
                    qn = 2 * which + a
                    i = b_out * 8 + qn
                    last = dve.scalar_tensor_tensor(xr[:, i, :], ps[:, 6, a * D:(a + 1) * D], rinv[:, b_out, qn:qn + 1], xr[:, i, :], ALU.mult, ALU.add)
                last.then_inc(s_e6, 1)

            def invert(it, g, b):
                dve.wait_ge(s_exp, 8 * it + 4 * g + 4)
                dve.reciprocal(rinv[:, b, 4 * g:4 * g + 4], rowsum[:, b, 4 * g:4 * g + 4]).then_inc(s_rinv, 1)
                dve.wait_ge(s_rinv, 2 * it + g + 1)

            def split(h):
                dve.wait_ge(s_wraw, (h + 1) * 16)
                for part in range(2):
                    sl = slice(part * QK, (part + 1) * QK)
                    last = dve.tensor_scalar(wraw[:, 0, :, sl], wraw[:, 0, :, sl], gsc[:, part, bass.ds(h, 1)], None, ALU.mult)
                last.then_inc(s_wsc, 1)
                dve.tensor_copy(wv[:], wraw[:, 2])
                dve.wait_ge(s_wsc, h + 1)
                dve.tensor_copy(wr[:], wraw[:, 0:2]).then_inc(s_rnd, 1)
                dve.wait_ge(s_rnd, h + 1)
                dve.tensor_tensor(wl[:], wraw[:, 0:2], wr[:].bitcast(F32), ALU.subtract).then_inc(s_ws, 1)

            dve.wait_ge(s_par1, 64)
            split(0)
            for p in range(4):
                turned(p, p)
                rest(p, p, 0)
            v_second(0, 1)
            max_tile(0, 0, 0)

            def body(h, b, last):
                it = 2 * h + b
                n0 = 4 * (it + 1)
                for qt in range(8):
                    if qt < 7 or not last:
                        max_tile(it, qt + 1, b)
                    if qt >= 4:
                        probs(it, qt)
                    if qt in (3, 4) and not first(it):
                        add_out(qt - 1, 1 - b, use6(it, W2 if qt == 3 else W3))
                    if qt in (6, 7):
                        add_out(qt - 6, b, use6(it, W0 if qt == 6 else W1))
                    if qt == 0 and not first(it):
                        rest(n0 - 1, 3, b)
                    if qt in (4, 5, 7) and not last:
                        p = {4: 0, 5: 1, 7: 2}[qt]
                        rest(n0 + p, p, 1 - b)
                    if qt in (2, 3, 5, 6) and not last:
                        p = {2: 0, 3: 1, 5: 2, 6: 3}[qt]
                        turned(n0 + p, p)
                    if qt == 0 and b == 1 and not (isinstance(h, int) and h == HEADS - 1):
                        dve.wait_ge(s_b7, use7(it - 1, 4))
                        split(h + 1)
                    if qt in (4, 7):
                        invert(it, qt // 7, b)
                    if qt == 4 and b == 0:
                        dve.wait_ge(s_wor, (h + 1) * 16)
                        dve.tensor_copy(wo[:], woraw[:]).then_inc(s_wos, 1)
                    if qt == 4:
                        dve.wait_ge(s_b6, use6(it, OUT0))
                        dve.tensor_copy(ot[:], ps[:, 6, :]).then_inc(s_e6, 1)
                    if qt == 7 and not last:
                        v_second(1 - b, use6(it, VHALF))
            heads_loop(dve, body)
            for which, n in ((2, W2), (3, W3)):
                add_out(which, 1, use6(ITS, n))

        def att_pool(g):
            def rotate(n, p):
                g.wait_ge(s_a7, n + 1)
                g.tensor_tensor(sw[64:128, p % 2, :], sw[64:128, p % 2, :], rope_t[64:128, 1, (p // 2) * 512:(p // 2 + 1) * 512], ALU.mult).then_inc(s_t2, 1)
                g.wait_ge(s_t2, n + 1)
                g.wait_ge(s_e7, 5 * (n // 4) + p + 1 if isinstance(n, int) else 5 * n_it[0] + p + 1)
                g.tensor_tensor(t1[64:128, p % 2, :], t1[64:128, p % 2, :], sw[64:128, p % 2, :], ALU.add).then_inc(s_rot, 1)
            n_it = [0]
            g.wait_ge(s_par1, 64)
            for p in range(4):
                rotate(p, p)
            with g.Fori(1, ITS) as it:
                n_it[0] = it
                for p in range(4):
                    rotate(4 * it + p, p)

        def att_sp(sp):
            sp.dma_start(wraw[:], wqkv[0]).then_inc(s_wraw, 16)
            sp.dma_start(woraw[:], wo_h[0]).then_inc(s_wor, 16)
            with sp.Fori(1, HEADS) as h:
                sp.wait_ge(s_ws, h)
                sp.dma_start(wraw[:], wqkv[bass.ds(h, 1)].rearrange("o p a c n -> (o p) a c n")).then_inc(s_wraw, 16)
                sp.wait_ge(s_wos, h)
                sp.dma_start(woraw[:], wo_h[bass.ds(h, 1)].rearrange("o p n -> (o p) n")).then_inc(s_wor, 16)

        block = ctx.enter_context(nc.Block())

        @block.sync
        def _(sp):
            for g in range(NG):
                sp.dma_start(xr[:, g * GT:(g + 1) * GT, :],
                             x_in[g * GT * P:(g + 1) * GT * P, :].rearrange("(i p) d -> p i d", p=P)).then_inc(s_x[g], 16)
            sp.dma_start(xpw[:], xproj).then_inc(s_par, 16)
            sp.dma_start(dtw[:], dtproj).then_inc(s_par, 16)
            sp.dma_start(dtb[:], dt_bias).then_inc(s_par, 16)
            sp.dma_start(alog[:], a_log).then_inc(s_par, 16)
            sp.dma_start(dpar[:], d_param).then_inc(s_par, 16)
            sp.dma_start(rw0[:], router0).then_inc(s_par, 16)
            sp.wait_ge(s_const, 1)
            zero_fill(sp, R0)
            zero_fill(sp, R1)
            sp.wait_ge(s_xdc, 8)
            sp.dma_start(bc_rows, bcT).then_inc(s_bc, 16)
            route_sp(sp, R0)
            sp.wait_ge(s_bc, 16)
            sp.wait_ge(s_dp, 8)
            for b in range(BATCH):
                with sp.Fori(0, STATES // 2) as j:
                    for q in range(2):
                        it = b * STATES + j * 2 + q
                        sp.wait_ge(s_hc, it + 1)
                        for rows, off in ((brow, 0), (crow, STATES)):
                            sp.dma_start(rows[:, q, :], bc_rows[bass.ds(j * 2 + q + off, 1), b * SEQ:(b + 1) * SEQ]
                                         .to_broadcast([P, SEQ])).then_inc(s_row[q], 16)
            experts_sp(sp, R0)
            if not only0:
                sp.wait_ge(s_xn, 2 * NG)
                sp.dma_start(rw1[:], router1).then_inc(s_par1, 16)
                sp.dma_start(rope_t[:], rope).then_inc(s_par1, 16)
                sp.dma_start(gsc[:, 0, :], gate_logit.to_broadcast([P, HEADS])).then_inc(s_par1, 16)
                sp.dma_start(gsc[:, 1, :], gate_logit.to_broadcast([P, HEADS])).then_inc(s_par1, 16)
                att_sp(sp)
                route_sp(sp, R1)
                sp.wait_ge(s_e6, use6(ITS, W3))
                sp.wait_ge(s_e7, use7(ITS - 2, 4))
                experts_sp(sp, R1)
                for q in range(NG):
                    sp.wait_ge(R1.shared_added, (q + 1) * GT)
                    sp.wait_ge(R1.added, (q + 1) * GT * K1)
                    sp.dma_start(out[q * GT * P:(q + 1) * GT * P, :].rearrange("(i p) d -> p i d", p=P),
                                 xr[:, q * GT:(q + 1) * GT, :]).then_inc(s_out, 16)
                sp.wait_ge(s_out, 16 * NG)
                for q in range(RING):
                    sp.wait_ge(R1.stored[q], 16 * R1.routed // RING)
                sp.wait_ge(R1.zeroed, 16 * R1.zero_dmas)
            if only0:
                sp.wait_ge(R0.added, NT)
                sp.dma_start(out.rearrange("(i p) d -> p i d", p=P), xr[:]).then_inc(s_out, 16)
                sp.wait_ge(s_out, 16)
            for q in range(RING):
                sp.wait_ge(R0.stored[q], 16 * R0.tiles_n // RING)
            sp.wait_ge(R0.zeroed, 16 * R0.zero_dmas)

        @block.gpsimd
        def _(g):
            n = [0]

            def step(ins):
                n[0] += 1
                ins.then_inc(s_const, 1)
                g.wait_ge(s_const, n[0])
            step(g.memset(zeros[:], 0.0))
            step(g.memset(neg_half[:], -0.5))
            step(g.memset(zero_b[:], 0.0))
            step(g.memset(ones_b[:], 1.0))
            step(g.memset(ident[:], 0.0))
            step(g.affine_select(out=ident[:], in_=ident[:], compare_op=ALU.not_equal, fill=1.0, base=0,
                                 pattern=[[-1, P]], channel_multiplier=1))
            step(g.tensor_copy(ident_b[:], ident[:]))
            step(g.affine_select(out=before[:], in_=ones_b[:], compare_op=ALU.is_gt, fill=0.0, base=0,
                                 pattern=[[1, P]], channel_multiplier=-1))
            step(g.iota(iota_e[:], [[1, E1]], base=0, channel_multiplier=0, allow_small_or_imprecise_dtypes=True))
            step(g.iota(iota_p[:], [[1, 1]], base=0, channel_multiplier=1, allow_small_or_imprecise_dtypes=True))
            for q in range(NG):
                g.wait_ge(s_var, q + 1)
                g.tensor_tensor(stat[:, 3, q * GT:(q + 1) * GT], stat[:, 2, q * GT:(q + 1) * GT],
                                neg_half[:, q * GT:(q + 1) * GT], ALU.pow).then_inc(s_rstd, 1)
            route_pool(g, R0)
            experts_pool(g, R0)
            gather_pool(g, R0)
            if only0:
                return
            for q in range(NG):
                g.wait_ge(s_var, NG + q + 1)
                g.tensor_tensor(stat[:, 3, q * GT:(q + 1) * GT], stat[:, 2, q * GT:(q + 1) * GT],
                                neg_half[:, q * GT:(q + 1) * GT], ALU.pow).then_inc(s_rstd, 1)
            g.wait_ge(s_xn, 2 * NG)
            g.affine_select(out=maskb[:], in_=zero_b[:], compare_op=ALU.is_ge, fill=-1e9, base=0,
                            pattern=[[-1, P]], channel_multiplier=1).then_inc(s_mask, 1)
            g.wait_ge(s_mask, 1)
            route_pool(g, R1)
            g.wait_ge(R1.scattered, 16 * NT * K1)
            att_pool(g)
            g.wait_ge(s_e6, use6(ITS, W3))
            g.wait_ge(s_e7, use7(ITS - 2, 4))
            experts_pool(g, R1)
            gather_pool(g, R1)

        N_CONST = 10

        @block.vector
        def _(v):
            def ln(first):
                for q in range(NG):
                    sl = slice(q * GT, (q + 1) * GT)
                    st = first + 5 * q

                    def step(ins, m):
                        ins.then_inc(s_ln, 1)
                        v.wait_ge(s_ln, st + m)
                    if first == 0:
                        v.wait_ge(s_x[q], 16)
                    else:
                        v.wait_ge(R0.added, GT * (q + 1))
                    step(v.tensor_reduce(stat[:, 0, sl], xr[:, sl, :], AX.X, ALU.add), 1)
                    step(v.tensor_scalar(stat[:, 1, sl], stat[:, 0, sl], -1.0 / D, None, ALU.mult), 2)
                    step(v.tensor_tensor(xn[:, sl, :], xr[:, sl, :], stat[:, 1, sl].unsqueeze(2).to_broadcast([P, GT, D]), ALU.add), 3)
                    s3 = (sw[:].rearrange("p a n -> p (a n)") if first else sq[:, 0:GT * D]).rearrange("p (i d) -> p i d", d=D)
                    step(v.tensor_tensor(s3, xn[:, sl, :], xn[:, sl, :], ALU.mult), 4)
                    step(v.tensor_reduce(stat[:, 0, sl], s3, AX.X, ALU.add), 5)
                    v.tensor_scalar(stat[:, 2, sl], stat[:, 0, sl], 1.0 / D, EPS, ALU.mult, ALU.add).then_inc(s_var, 1)
                    v.wait_ge(s_rstd, first // (5 * NG) * NG + q + 1)
                    v.tensor_tensor(xn[:, sl, :], xn[:, sl, :], stat[:, 3, sl].unsqueeze(2).to_broadcast([P, GT, D]), ALU.mult)\
                        .then_inc(s_xn, 1)
            ln(0)
            for q in range(NG):
                v.wait_ge(s_xnT_ps, q + 1)
                for c in range(DC):
                    last = v.tensor_copy(xnT[:, c, q * 512:(q + 1) * 512], ps[:, (q % 2) * 2 + c, :])
                last.then_inc(s_xnT, 1)
            v.wait_ge(s_const, N_CONST)
            v.memset(R0.ecmp[:], 1.0)
            step = route_dve(v, R0)
            v.tensor_tensor(R0.weight[:, :, 0], R0.top[:, :, 1], R0.top[:, :, 0], ALU.subtract).then_inc(s_spa, 1)
            v.wait_ge(s_spa, 2)
            v.tensor_scalar(R0.weight[:, :, 0], R0.weight[:, :, 1], 1.0, None, ALU.add).then_inc(s_spa, 1)
            v.wait_ge(s_spa, 3)
            v.reciprocal(R0.weight[:, :, 0], R0.weight[:, :, 0]).then_inc(s_spa, 1)
            v.wait_ge(s_spa, 4)

            for b in range(BATCH):
                m = [10 * b]

                def sstep(ins):
                    m[0] += 1
                    ins.then_inc(s_sp, 1)
                    v.wait_ge(s_sp, m[0])
                dl = delta[:, :, b * SEQ:(b + 1) * SEQ]

                def two(a):
                    return a.rearrange("p (c t) -> p c t", c=DC)
                v.wait_ge(s_spa, 4 + b + 1)
                sstep(v.tensor_scalar(sp_z, sp_e, 2.0, None, ALU.add))
                sstep(v.reciprocal(sp_z, sp_z))
                sstep(v.tensor_tensor(sp_s, sp_e, sp_z, ALU.mult))
                sstep(v.tensor_tensor(sp_z, sp_s, sp_s, ALU.mult))
                sstep(v.tensor_scalar(sp_e, sp_z, COEF[4], COEF[3], ALU.mult, ALU.add))
                sstep(v.tensor_tensor(sp_e, sp_e, sp_z, ALU.mult))
                sstep(v.scalar_tensor_tensor(sp_e, sp_e, COEF[2], sp_z, ALU.add, ALU.mult))
                sstep(v.scalar_tensor_tensor(sp_e, sp_e, COEF[1], sp_z, ALU.add, ALU.mult))
                sstep(v.scalar_tensor_tensor(sp_e, sp_e, COEF[0], sp_s, ALU.add, ALU.mult))
                sstep(v.scalar_tensor_tensor(dl, two(sp_x), 0.0, two(sp_e), ALU.max, ALU.add))
                v.tensor_tensor(dx[:, :, b * SEQ:(b + 1) * SEQ], dl, xnT[:, :, b * SEQ:(b + 1) * SEQ], ALU.mult).then_inc(s_delta, 1)
            v.wait_ge(s_delta, 2)
            for q in range(2):
                last = v.memset(decay[:, q, :, 0:1], 0.0)
            last.then_inc(s_hc, 2)
            for b in range(BATCH):
                with v.Fori(0, STATES // 2) as j:
                    for q in range(2):
                        it = b * STATES + j * 2 + q
                        flat = state[:, q].rearrange("p c t -> p (c t)")
                        v.wait_ge(s_row[q], (b * (STATES // 2) + j + 1) * 32)
                        v.wait_ge(s_ysum, it + 1)
                        v.tensor_tensor(state[:, q], dx[:, :, b * SEQ:(b + 1) * SEQ],
                                        brow[:, q, :].unsqueeze(1).to_broadcast([P, DC, SEQ]), ALU.mult).then_inc(s_dbx, 1)
                        v.wait_ge(s_dbx, it + 1)
                        v.wait_ge(s_dec, it + 1)
                        v.tensor_tensor_scan(flat, decay[:, q].rearrange("p c t -> p (c t)"), flat, 0.0,
                                             ALU.mult, ALU.add).then_inc(s_scan, 1)
                        v.wait_ge(s_scan, it + 1)
                        v.tensor_tensor(state[:, q], state[:, q],
                                        crow[:, q, :].unsqueeze(1).to_broadcast([P, DC, SEQ]), ALU.mult).then_inc(s_hc, 1)
                v.wait_ge(s_ysum, 2 + (b + 1) * STATES)
                v.wait_ge(s_dec, (b + 1) * STATES)
                for c in range(DC):
                    last = v.scalar_tensor_tensor(delta[:, c, b * SEQ:(b + 1) * SEQ], xnT[:, c, b * SEQ:(b + 1) * SEQ],
                                                  dpar[:, c:c + 1], ps[:, 2 * c:2 * c + 2, :].rearrange("p a t -> p (a t)"), ALU.mult, ALU.add)
                last.then_inc(s_yT, 1)
            for i in range(NT // 2):
                v.wait_ge(s_yT_ps, i + 1)
                v.tensor_tensor(xr[:, 2 * i:2 * i + 2, :], xr[:, 2 * i:2 * i + 2, :],
                                ps[:, i % 2, :].rearrange("p (a d) -> p a d", a=2), ALU.add).then_inc(s_yadd, 1)
            experts_dve(v, R0)
            v.wait_ge(s_yadd, NT // 2)
            gather_dve(v, R0)
            if only0:
                return
            v.wait_ge(R1.zeroed, 16 * R1.zero_dmas)
            ln(5 * NG)
            for q in range(NG):
                sl = slice(q * 512, (q + 1) * 512)
                v.wait_ge(s_xnT1, q + 1)
                v.tensor_copy(xnr[:, :, sl], xnT1[:, :, sl]).then_inc(s_split, 1)
                v.wait_ge(s_split, 2 * q + 1)
                v.tensor_tensor(xnl[:, :, sl], xnT1[:, :, sl], xnr[:, :, sl].bitcast(F32), ALU.subtract).then_inc(s_split, 1)
            gs = [0]

            def gstep(ins):
                gs[0] += 1
                ins.then_inc(s_gate, 1)
                v.wait_ge(s_gate, gs[0])
            v.wait_ge(s_gact, 1)
            gstep(v.tensor_scalar(gsc[:], gsc[:], 1.0, None, ALU.add))
            gstep(v.reciprocal(gsc[:], gsc[:]))
            gstep(v.tensor_scalar(gsc[:, 1, :], gsc[:, 1, :], -1.0, 1.0, ALU.mult, ALU.add))
            gstep(v.tensor_scalar(gsc[:], gsc[:], QK ** -0.5, None, ALU.mult))
            v.memset(R1.ecmp[:], 1.0)
            step = route_dve(v, R1)
            soft = R1.rank[:].rearrange("p e i -> p (e i)").rearrange("p (i e) -> p i e", e=E1)
            top0 = R1.top[:, :, 0:1]
            v.tensor_tensor(soft, R1.logit[:, :, 0:E1], top0.to_broadcast([P, NT, E1]), ALU.subtract).then_inc(s_w1, 1)
            v.tensor_tensor(R1.weight[:, :, 0:K1], R1.top[:, :, 0:K1], top0.to_broadcast([P, NT, K1]), ALU.subtract).then_inc(s_w1, 1)
            v.memset(R1.weight[:, :, K1:], 0.0).then_inc(s_w1, 1)
            v.wait_ge(s_w1a, 3)
            v.tensor_reduce(R1.weight[:, :, 5], soft, AX.X, ALU.add).then_inc(s_w1, 1)
            v.tensor_scalar(R1.weight[:, :, K1], R1.weight[:, :, K1], 1.0, None, ALU.add).then_inc(s_w1, 1)
            v.wait_ge(s_w1, 5)
            v.reciprocal(R1.weight[:, :, K1:6], R1.weight[:, :, K1:6]).then_inc(s_w1, 1)
            v.wait_ge(s_w1, 6)
            v.tensor_tensor(R1.weight[:, :, 0:K1], R1.weight[:, :, 0:K1], R1.weight[:, :, 5:6].to_broadcast([P, NT, K1]), ALU.mult).then_inc(s_w1, 1)
            v.wait_ge(s_w1, 7)
            att_dve(v)
            v.wait_ge(s_e6, use6(ITS, W3))
            v.wait_ge(s_e7, use7(ITS - 2, 4))
            experts_dve(v, R1)

        @block.scalar
        def _(act):
            act.wait_ge(s_par, 96)
            act.activation(alog[:], alog[:], ACT.Exp).then_inc(s_aneg, 1)
            act.wait_ge(s_aneg, 1)
            act.mul(aneg[:], alog[:], -1.0).then_inc(s_aneg, 1)
            for q in range(4):
                act.wait_ge(s_xd, 2 * q + 1)
                act.copy(dtT[:, q * 512:(q + 1) * 512], ps[:, (2 * q) % 4, :]).then_inc(s_xdc, 1)
                act.wait_ge(s_xd, 2 * q + 2)
                act.copy(bcT[:, q * 512:(q + 1) * 512], ps[0:2 * STATES, (2 * q + 1) % 4, :]).then_inc(s_xdc, 1)
            act.wait_ge(s_spa, 1)
            act.activation(R0.weight[:, :, 1], R0.weight[:, :, 0], ACT.Exp).then_inc(s_spa, 1)
            for b in range(BATCH):
                if b:
                    act.wait_ge(s_sp, 10)
                for c in range(DC):
                    for q in range(2):
                        m = b * 4 + c * 2 + q
                        act.wait_ge(s_dp, m + 1)
                        act.activation(sp_x[:, c * SEQ + q * 512:c * SEQ + (q + 1) * 512], ps[:, m % 4, :], ACT.Identity,
                                       bias=dtb[:, c:c + 1]).then_inc(s_dpc, 1)
                act.wait_ge(s_dpc, 5 * (b + 1) - 1)
                act.activation(sp_e, sp_x, ACT.Abs).then_inc(s_dpc, 1)
                act.wait_ge(s_dpc, 5 * (b + 1))
                act.wait_ge(s_spa, 4 + b)
                act.activation(sp_e, sp_e, ACT.Exp, scale=-1.0).then_inc(s_spa, 1)
            act.wait_ge(s_delta, 2)
            act.wait_ge(s_aneg, 2)
            for b in range(BATCH):
                with act.Fori(0, STATES // 2) as j:
                    for q in range(2):
                        it = b * STATES + j * 2 + q
                        act.wait_ge(s_hc, it + 1)
                        for c in range(DC):
                            last = act.activation(decay[:, q, c, 1:SEQ], delta[:, c, b * SEQ + 1:(b + 1) * SEQ], ACT.Exp,
                                                  scale=aneg[:, c, bass.ds(j * 2 + q, 1)])
                        last.then_inc(s_dec, 1)
            experts_act(act, R0)
            if only0:
                return
            for q in range(NG):
                act.wait_ge(s_xnT1_ps, q + 1)
                for c in range(DC):
                    last = act.copy(xnT1[:, c, q * 512:(q + 1) * 512], ps[:, (q % 2) * 2 + c, :])
                last.then_inc(s_xnT1, 1)
            act.wait_ge(s_par1, 64)
            act.activation(gsc[:], gsc[:], ACT.Exp, scale=-1.0).then_inc(s_gact, 1)
            act.wait_ge(s_w1, 3)
            act.activation(R1.rank[:], R1.rank[:], ACT.Exp).then_inc(s_w1a, 1)
            act.activation(R1.weight[:, :, 0:K1], R1.weight[:, :, 0:K1], ACT.Exp).then_inc(s_w1a, 1)
            act.activation(R1.weight[:, :, K1], R1.logit[:, :, E1], ACT.Exp, scale=-1.0).then_inc(s_w1a, 1)
            att_act(act)
            experts_act(act, R1)

        @block.tensor
        def _(pe):
            pe.wait_ge(s_const, N_CONST)
            for q in range(NG):
                pe.wait_ge(s_xn, q + 1)
                if q >= 2:
                    pe.wait_ge(s_xnT, q - 1)
                for c in range(DC):
                    for i in range(GT):
                        last = pe.transpose(ps[:, (q % 2) * 2 + c, i * P:(i + 1) * P], xn[:, q * GT + i, c * P:(c + 1) * P], ident[:])
                last.then_inc(s_xnT_ps, 1)
            pe.wait_ge(s_xnT, NG)
            pe.wait_ge(s_par, 96)
            for i in range(NT):
                for c in range(DC):
                    last = pe.matmul(ps[:, 4 + i // 8, (i % 8) * E0:(i % 8 + 1) * E0], xnT[:, c, i * P:(i + 1) * P],
                                     rw0[:, c, :], start=c == 0, stop=c == DC - 1)
            last.then_inc(R0.logits_ready, 1)
            for q in range(4):
                for w in range(2):
                    n = 2 * q + w
                    if n >= 4:
                        pe.wait_ge(s_xdc, n - 3)
                    rows = P if w == 0 else 2 * STATES
                    for c in range(DC):
                        last = pe.matmul(ps[0:rows, n % 4, :], xpw[:, c, w * P:w * P + rows], xnT[:, c, q * 512:(q + 1) * 512],
                                         start=c == 0, stop=c == DC - 1)
                    last.then_inc(s_xd, 1)
            pe.wait_ge(s_xdc, 8)
            for b in range(BATCH):
                for c in range(DC):
                    for q in range(2):
                        m = b * 4 + c * 2 + q
                        if m >= 4:
                            pe.wait_ge(s_dpc, m - 3)
                        pe.matmul(ps[:, m % 4, :], dtw[:, c * P:(c + 1) * P], dtT[:, b * SEQ + q * 512:b * SEQ + (q + 1) * 512],
                                  start=True, stop=True).then_inc(s_dp, 1)
                if b == 0:
                    route_pe(pe, R0)
            pe.wait_ge(s_dpc, 10)
            for q in range(4):
                last = pe.matmul(ps[:, q, :], ident[:], zeros[:, 0:512], start=True, stop=False, skip_group_check=True)
            last.then_inc(s_ysum, 2)
            for b in range(BATCH):
                if b:
                    pe.wait_ge(s_yT, b)
                    for q in range(4):
                        last = pe.matmul(ps[:, q, :], ident[:], zeros[:, 0:512], start=True, stop=False, skip_group_check=True)
                with pe.Fori(0, STATES // 2) as j:
                    for q in range(2):
                        pe.wait_ge(s_hc, 2 + b * STATES + j * 2 + q + 1)
                        for c in range(DC):
                            for h in range(2):
                                last = pe.matmul(ps[:, 2 * c + h, :], ident[:], state[:, q, c, h * 512:(h + 1) * 512],
                                                 start=False, stop=True, skip_group_check=True)
                        last.then_inc(s_ysum, 1)
            pe.wait_ge(s_yT, 2)
            for i in range(NT // 2):
                if i >= 2:
                    pe.wait_ge(s_yadd, i - 1)
                for a in range(2):
                    for c in range(DC):
                        tt = 2 * i + a
                        last = pe.transpose(ps[:, i % 2, a * D + c * P:a * D + (c + 1) * P], delta[:, c, tt * P:(tt + 1) * P], ident[:])
                last.then_inc(s_yT_ps, 1)
            experts_pe(pe, R0)
            if only0:
                return
            for q in range(NG):
                pe.wait_ge(s_xn, NG + q + 1)
                if q >= 2:
                    pe.wait_ge(s_xnT1, q - 1)
                for c in range(DC):
                    for i in range(GT):
                        last = pe.transpose(ps[:, (q % 2) * 2 + c, i * P:(i + 1) * P], xn[:, q * GT + i, c * P:(c + 1) * P], ident[:])
                last.then_inc(s_xnT1_ps, 1)
            pe.wait_ge(s_xnT1, NG)
            pe.wait_ge(s_par1, 64)
            for i in range(NT):
                for c in range(DC):
                    last = pe.matmul(ps[:, 4 + i // 8, (i % 8) * (E1 + 1):(i % 8 + 1) * (E1 + 1)], xnT1[:, c, i * P:(i + 1) * P],
                                     rw1[:, c, :], start=c == 0, stop=c == DC - 1)
            last.then_inc(R1.logits_ready, 1)
            route_pe(pe, R1)
            att_pe(pe)
            experts_pe(pe, R1)


def layouts(v):
    c = np.ascontiguousarray

    def feat(w):
        return c(w.reshape(DC, P, -1).transpose(1, 0, 2))

    def w13_of(gate, up):
        w = np.concatenate([gate, up], axis=1).transpose(0, 2, 1)
        return c(w.reshape(-1, DC, P, 2 * INNER).transpose(0, 2, 1, 3))

    def w2_of(w):
        return c(w.transpose(0, 2, 1).reshape(-1, 2, IC, D).transpose(0, 2, 1, 3))

    se_g, se_u = v['L1_ffn_se_gate_up_w'][:SHARED * INNER], v['L1_ffn_se_gate_up_w'][SHARED * INNER:]
    w13l1 = np.concatenate([v['L1_ffn_w13'], np.concatenate([se_g.reshape(SHARED, INNER, D), se_u.reshape(SHARED, INNER, D)], axis=1)])
    w2l1 = np.concatenate([v['L1_ffn_w2'], v['L1_ffn_se_down_w'].reshape(D, SHARED, INNER).transpose(1, 0, 2)])

    def heads(w, n):
        return w.reshape(DC, P, HEADS, n).transpose(2, 1, 0, 3)
    q = np.concatenate([heads(v['L1_attn_wq_sem'], QK), heads(v['L1_attn_wq_geo'], QK)], axis=3)
    k = np.concatenate([heads(v['L1_attn_wk_sem'], QK), heads(v['L1_attn_wk_geo'], QK)], axis=3)
    wv = heads(v['L1_attn_wv'], P)
    half = QK // 2
    inv = (1.0 / 10000.0 ** (np.arange(half, dtype=np.float32) / np.float32(half))).astype(np.float32)
    ang = inv[:, None] * np.arange(SEQ, dtype=np.float32)[None]
    cos, sin = np.cos(ang).astype(np.float32), np.sin(ang).astype(np.float32)
    rope = np.stack([np.concatenate([np.ones((QK, SEQ), np.float32), cos, cos]),
                     np.concatenate([np.zeros((QK, SEQ), np.float32), -sin, sin])], axis=1)
    return {
        'x': c(v['L0_attn_x'].reshape(T, D)), 'a_log': feat(v['L0_attn_A_log']), 'd_param': c(v['L0_attn_D_param'].reshape(DC, P).T),
        'xproj': feat(v['L0_attn_x_proj_w'].T), 'dtproj': c(v['L0_attn_dt_proj_w'].T), 'dt_bias': c(v['L0_attn_dt_proj_b'].reshape(DC, P).T),
        'router0': feat(v['L0_ffn_router_w'].T), 'w13_0': w13_of(v['L0_ffn_gate_w'], v['L0_ffn_up_w']), 'w2_0': w2_of(v['L0_ffn_down_w']),
        'router1': feat(np.concatenate([v['L1_ffn_gate_w'], v['L1_ffn_shared_gate_w']]).T),
        'w13_1': w13_of(w13l1[:, :INNER], w13l1[:, INNER:]), 'w2_1': w2_of(w2l1),
        'wqkv': c(np.stack([q, k, wv], axis=2)), 'wo_h': c(v['L1_attn_wo'].reshape(HEADS, P, D)),
        'gate_logit': c(v['L1_attn_gate_logit'].reshape(1, HEADS)), 'rope': c(rope),
    }


ONLY0 = False


def kernel(**inputs):
    import concourse.bacc as _bacc
    from concourse.bass_utils import run_bass_kernel_spmd as _run

    nc = _bacc.Bacc("TRN2", target_bir_lowering=False, num_devices=1)
    arrays, args = {}, []
    for name, a in layouts({k: np.asarray(a) for k, a in inputs.items()}).items():
        arrays[f"in_{name}"] = a
        args.append(nc.dram_tensor(f"in_{name}", a.shape, mybir.dt.from_np(a.dtype), kind="ExternalInput").ap())
    args.append(nc.dram_tensor("out_0", (T, D), F32, kind="ExternalOutput").ap())
    build(nc, *args, only0=ONLY0)
    r = _run(nc, [arrays], core_ids=[0])
    return r.results[0]["out_0"].reshape(BATCH, SEQ, D)
```

```python
from contextlib import ExitStack

import numpy as np

import concourse.bass as bass
from concourse import mybir

F32 = mybir.dt.float32
F32R = mybir.dt.float32r
BF16 = mybir.dt.bfloat16
I32 = mybir.dt.int32
U32 = mybir.dt.uint32
ALU = mybir.AluOpType
ACT = mybir.ActivationFunctionType
AX = mybir.AxisListType

P = 128
BATCH, SEQ, D = 2, 1024, 256
T = BATCH * SEQ
NT = T // P
DC = D // P
NG = 4
GT = NT // NG
EPS = 1e-5

STATES, RANK = 16, 128
XD = RANK + 2 * STATES

INNER = 176
IC = INNER // 2
E0, E1 = 8, 60
K1 = 4
SHARED = 4
TILES0 = T // P + E0
TILES1 = T * K1 // P + E1
ALL1 = TILES1 + SHARED * NT
RING = 4
GU_BANK, DN_BANK = (5, 3), (7, 2)

HEADS, QK = 16, 64


class Route:
    def __init__(self, tiles_n, slots, result, etab_dram, w13_dram, w2_dram, routed, n_weights):
        self.tiles_n, self.routed, self.n_weights = tiles_n, routed, n_weights
        self.slots, self.result, self.etab_dram = slots, result, etab_dram
        self.w13_dram, self.w2_dram = w13_dram, w2_dram


def log1p_coefficients(n):
    z = (np.cos(np.pi * (np.arange(64) + 0.5) / 64) + 1) / 18
    s = np.sqrt(z)
    return [float(2 * c) for c in np.polynomial.chebyshev.Chebyshev.fit(z, np.arctanh(s) / s, n - 1, domain=[0, 1 / 9])
            .convert(kind=np.polynomial.Polynomial).coef]


def build(nc, x_in, a_log, d_param, xproj, dtproj, dt_bias, router0, w13_0, w2_0,
          router1, w13_1, w2_1, wqkv, wo_h, gate_logit, rope, out):
    ctx = ExitStack()
    with ctx:
        def sb(name, shape, dt=F32):
            return ctx.enter_context(nc.sbuf_tensor(name, shape, dt))

        def sem(name):
            return ctx.enter_context(nc.semaphore(name))

        def dram(name, shape, dt=F32):
            return nc.dram_tensor(name, shape, dt).ap()

        ps = ctx.enter_context(nc.psum_tensor("ps", [P, 8, 512], F32))

        bc_rows = dram("bc_rows", [2 * STATES, T])
        sorted1 = dram("sorted1", [TILES1 * P, D])
        result1 = dram("result1", [TILES1 * P, D])
        etab1 = dram("etab1", [P, 1], I32)
        sorted0 = dram("sorted0", [TILES0 * P, D])
        result0 = dram("result0", [TILES0 * P, D])
        etab0 = dram("etab0", [P, 1], I32)
        xr = sb("xr", [P, NT, D])
        xn = sb("xn", [P, NT, D])
        ident = sb("ident", [P, P])
        ident_b = sb("ident_b", [P, P], BF16)
        before = sb("before", [P, P], BF16)
        ones_b = sb("ones_b", [P, P], BF16)
        zero_b = sb("zero_b", [P, P], BF16)
        iota_e = sb("iota_e", [P, E1])
        iota_p = sb("iota_p", [P, 1])
        neg_half = sb("neg_half", [P, NT])
        bn = sb("bn", [P, NT, 6])
        mean_var = sb("mean_var", [P, NT, 2])
        stat = sb("stat", [P, 2, NT])

        base0 = ExitStack()

        def sb0(name, shape, dt=F32):
            return base0.enter_context(nc.sbuf_tensor(name, shape, dt))

        zeros = sb0("zeros", [P, 2048])
        xnT = sb0("xnT", [P, DC, T])
        delta = sb0("delta", [P, DC, T])
        dx = sb0("dx", [P, DC, T])
        xpw = sb0("xpw", [P, DC, XD])
        dtw = sb0("dtw", [P, D])
        dtb = sb0("dtb", [P, DC])
        alog = sb0("alog", [P, DC, STATES])
        aneg = sb0("aneg", [P, DC, STATES])
        dpar = sb0("dpar", [P, DC])
        rw0 = sb0("rw0", [P, DC, E0])
        decay = sb0("decay", [P, 2, DC, SEQ])
        state = sb0("state", [P, 2, DC, SEQ])
        brow = sb0("brow", [P, 2, SEQ])
        crow = sb0("crow", [P, 2, SEQ])
        sp_x = decay[:, 0].rearrange("p c t -> p (c t)")
        sp_e = decay[:, 1].rearrange("p c t -> p (c t)")
        sp_s = state[:, 0].rearrange("p c t -> p (c t)")
        sp_z = state[:, 1].rearrange("p c t -> p (c t)")
        dtT = brow[:, :, :].rearrange("p a t -> p (a t)")
        bcT = crow[0:2 * STATES, :, :].rearrange("p a t -> p (a t)")

        def ring_buffers(r, n, alloc):
            r.w13 = alloc(f'w13r{n}', [P, RING, DC, 2 * INNER])
            r.w2 = alloc(f'w2r{n}', [IC, RING, 2, D])
            r.xs = alloc(f'xs{n}', [P, RING, D])
            r.xt = alloc(f'xt{n}', [P, 2, D])
            r.th = alloc(f'th{n}', [P, 2, INNER])
            r.ga = alloc(f'ga{n}', [P, 2, INNER])
            r.hh = alloc(f'hh{n}', [P, 2, INNER])
            r.ht = alloc(f'ht{n}', [IC, 2, 2, P])
            r.yy = alloc(f'yy{n}', [P, RING, D])
            r.got = alloc(f'got{n}', [P, 4, D])

        def route_buffers(r, n, e, k, alloc, el, keep_alloc):
            r.E = e
            r.K = k
            r.EL = el
            r.logit = alloc(f'logit{n}', [P, NT, el])
            r.top = alloc(f'top{n}', [P, NT, 8])
            r.idx = alloc(f'idx{n}', [P, NT, 8], U32)
            r.idxf = alloc(f'idxf{n}', [P, NT, 8])
            r.hot = alloc(f'hot{n}', [P, k, e, NT], BF16)
            r.m = alloc(f'm{n}', [P, e, NT], BF16)
            r.keep = alloc(f'keep{n}', [P, e, NT], BF16)
            r.cum = alloc(f'cum{n}', [P, e, NT], BF16)
            r.cumx = alloc(f'cumx{n}', [P, e, NT], BF16)
            r.rank = alloc(f'rank{n}', [P, e, NT])
            r.prod = alloc(f'prod{n}', [P, e, NT])
            r.cnti = alloc(f'cnti{n}', [P, e], I32)
            r.tiles = alloc(f'tiles{n}', [P, e])
            r.upto = alloc(f'upto{n}', [P, e])
            r.base = alloc(f'base{n}', [P, e])
            r.slotf = alloc(f'slotf{n}', [P, k, NT])
            r.slot = keep_alloc(f'slot{n}', [P, k, NT], U32)
            r.weight = keep_alloc(f'weight{n}', [P, NT, 8])
            r.ecol = alloc(f'ecol{n}', [P, 2])
            r.ecoli = keep_alloc(f'ecoli{n}', [P, 1], I32)
            r.ecmp = alloc(f'ecmp{n}', [P, e])
            r.logits_ready = sem(f'logits_ready{n}')
            r.step = sem(f'route_step{n}')
            r.ranks_ready = sem(f'ranks_ready{n}')
            r.m_ready = sem(f'm_ready{n}')
            r.slots_ready = sem(f'slots_ready{n}')
            r.scattered = sem(f'scattered{n}')
            r.tiles_known = sem(f'tiles_known{n}')
            r.table_stored = sem(f'table_stored{n}')
            r.table_loaded = sem(f'table_loaded{n}')
            r.zeroed = sem(f'zeroed{n}')
            r.etab = keep_alloc(f'etabrow{n}', [1, 192], I32)
            r.x_loaded = [sem(f'tokens_loaded{n}_{q}') for q in range(RING)]
            r.w13_loaded = [sem(f'w13_loaded{n}_{q}') for q in range(RING)]
            r.w2_loaded = [sem(f'w2_loaded{n}_{q}') for q in range(RING)]
            r.shared_added = sem(f'shared_added{n}')
            r.xt_ready = sem(f'xt_ready{n}')
            r.xt_copied = sem(f'xt_copied{n}')
            r.gu_ready = sem(f'gu_ready{n}')
            r.tanh_ready = sem(f'tanh_ready{n}')
            r.act_step = sem(f'gated{n}')
            r.h_done = sem(f'h_done{n}')
            r.ht_ready = sem(f'ht_ready{n}')
            r.ht_copied = sem(f'ht_copied{n}')
            r.dn_done = sem(f'dn_done{n}')
            r.y_copied = sem(f'y_copied{n}')
            r.stored = [sem(f'y_stored{n}_{q}') for q in range(RING)]
            r.gathered = [sem(f'gathered{n}_{q}') for q in range(4)]
            r.added = sem(f'added{n}')

        R0 = Route(TILES0, sorted0, result0, etab0, w13_0, w2_0, TILES0, E0)
        route_buffers(R0, 0, E0, 1, sb0, E0, sb0)
        hc = sb0("hc", [P, 2, DC, SEQ])
        hc_flat = hc[:].rearrange("p q c t -> p (q c t)")
        w13_size = RING * DC * 2 * INNER
        shared_memory = {
            'w13r0': hc_flat[:, 0:w13_size].rearrange("p (r c n) -> p r c n", r=RING, c=DC),
            'xs0': hc_flat[:, w13_size:w13_size + RING * D].rearrange("p (r d) -> p r d", r=RING)}
        ring_buffers(R0, 0, lambda name, shape, dt=F32: shared_memory[name] if name in shared_memory else sb0(name, shape, dt))

        base0.close()

        def sbk(name, shape, dt=F32):
            return ctx1.enter_context(nc.sbuf_tensor(name, shape, dt))
        ctx1 = ExitStack()
        xnr = sbk("xnr", [P, DC, T], F32R)
        xnl = sbk("xnl", [P, DC, T], F32R)
        xnT1 = sbk("xnT1", [P, DC, T])
        gsc = sbk("gsc", [P, 2, HEADS])
        rowsum = sbk("rowsum", [P, 2, 8])
        rinv = sbk("rinv", [P, 2, 8])
        negmax = sbk("negmax", [P, 2, 8])
        rw1 = sbk("rw1", [P, DC, E1 + 1])
        att = ExitStack()

        def sba(name, shape, dt=F32):
            return att.enter_context(nc.sbuf_tensor(name, shape, dt))
        slot_w = sbk("slot1", [P, K1, NT], U32)
        weight_w = sbk("weight1", [P, NT, 8])
        ecoli_w = sbk("ecoli1", [P, 1], I32)
        etab_w = sbk("etabrow1", [1, 192], I32)
        kept = {"slot1": slot_w, "weight1": weight_w, "ecoli1": ecoli_w, "etabrow1": etab_w}
        wraw = sba("wraw", [P, 3, DC, P])
        wr = sba("wr", [P, 2, DC, P], F32R)
        wl = sba("wl", [P, 2, DC, P], F32R)
        wv = sba("wv", [P, DC, P])
        woraw = sba("woraw", [P, D])
        wo = sba("wo", [P, D])
        rope_t = sba("rope_t", [P, 2, SEQ])
        qkr = sba("qkr", [P, 2, 2, SEQ], F32R)
        qkl = sba("qkl", [P, 2, 2, SEQ], F32R)
        v = sba("v", [P, 2, 8, P])
        ot = sba("ot", [P, 512])
        t1 = sba("t1", [P, 2, 512])
        sw = sba("sw", [P, 2, 512])
        slot_cols = sba("slot_cols", [P, 2], U32)
        staged = sba("staged", [P, D])
        fence = sba("fence", [P, 1])
        maskb = sba("maskb", [P, P], BF16)
        over = ExitStack()

        def sbo(name, shape, dt=F32):
            return over.enter_context(nc.sbuf_tensor(name, shape, dt))
        pb = sbo("pb", [P, 2, SEQ])
        pt = [sbo("pt0", [P, 4, 512]), sbo("pt1", [P, 8, 512])]
        over.close()
        over2 = ExitStack()
        R1 = Route(ALL1, sorted1, result1, etab1, w13_1, w2_1, TILES1, E1 + SHARED)
        route_buffers(R1, 1, E1, K1, lambda n, sh, dt=F32: over2.enter_context(nc.sbuf_tensor(n, sh, dt)), E1 + 1,
                            lambda n, sh, dt=F32: kept[n])
        over2.close()
        att.close()
        over3 = ExitStack()
        ring_buffers(R1, 1, lambda n, sh, dt=F32: over3.enter_context(nc.sbuf_tensor(n, sh, dt)))
        over3.close()
        ctx1.close()

        s_x = [sem(f"x_loaded{g}") for g in range(NG)]
        s_par = sem("params_loaded")
        s_const = sem("consts_made")
        s_ln = sem("ln_step")
        s_var = sem("variance_ready")
        s_rstd = sem("rstd_ready")
        s_xn = sem("xn_ready")
        s_xnT_ps = sem("xnT_in_psum")
        s_xnT = sem("xnT_ready")
        s_xd = sem("xdbl_in_psum")
        s_xdc = sem("xdbl_copied")
        s_bc = sem("bc_rows_stored")
        s_dp = sem("dt_in_psum")
        s_dpc = sem("dt_biased")
        s_sp = sem("softplus_step")
        s_spa = sem("softplus_act_step")
        s_delta = sem("delta_ready")
        s_brow = [sem(f"b_row_loaded{r}") for r in range(2)]
        s_crow = [sem(f"c_row_loaded{r}") for r in range(2)]
        s_dec = sem("decay_ready")
        s_dbx = sem("input_term_ready")
        s_scan = sem("scanned")
        s_hc = sem("hc_ready")
        s_ysum = sem("y_summed")
        s_aneg = sem("a_ready")
        s_yT = sem("yT_ready")
        s_yT_ps = sem("y_rows_in_psum")
        s_yadd = sem("y_rows_added")
        s_out = sem("out_stored")

        s_mask = sem("mask_made")
        s_par1 = sem("params1_loaded")
        s_gate = sem("gate_step")
        s_gact = sem("gate_exp")
        s_xnT1_ps = sem("xn1T_in_psum")
        s_xnT1 = sem("xn1T_copied")
        s_split = sem("xn1_split")
        s_wraw = sem("head_weights_loaded")
        s_wsc = sem("head_weights_scaled")
        s_ws = sem("head_weights_split")
        s_wor = sem("wo_loaded")
        s_wos = sem("wo_copied")
        s_rnd = sem("weights_rounded")
        s_S = sem("scores_ready")
        s_max = sem("max_ready")
        s_exp = sem("exp_ready")
        s_T = sem("probs_transposed")
        s_pr = sem("probs_copied")
        s_pl = sem("second_probs_copied")
        s_b6 = sem("bank6_filled")
        s_e6 = sem("bank6_taken")
        s_b7 = sem("bank7_filled")
        s_a7 = sem("bank7_rounded")
        s_e7 = sem("bank7_taken")
        s_t2 = sem("rotated")
        s_cols = sem("slot_columns_copied")
        s_staged = sem("token_tile_staged")
        s_rot = sem("rotation_added")
        s_qr = sem("qk_rounded")
        s_ql = sem("qk_split")
        s_rinv = sem("sums_inverted")
        s_w0 = sem("weights0_step")
        s_w1 = sem("weights1_step")
        s_w1a = sem("weights1_exp")

        COEF = log1p_coefficients(5)

        def w(eng, s, value):
            if not isinstance(value, int) or value > 0:
                eng.wait_ge(s, value)

        def route_dve(v, r, meanwhile=lambda part: None):
            n = [0]

            def step(ins):
                n[0] += 1
                ins.then_inc(r.step, 1)
                v.wait_ge(r.step, n[0])

            v.wait_ge(r.logits_ready, 1)
            for c in range(NT // 8):
                last = v.tensor_copy(r.logit[:, 8 * c:8 * c + 8, :].rearrange("p i e -> p (i e)"), ps[:, 4 + c, 0:8 * r.EL])
            step(last)
            for i in range(NT):
                last = v.max(r.top[:, i, :], r.logit[:, i, 0:r.E])
            step(last)
            for i in range(NT):
                last = v.max_index(r.idx[:, i, :], r.top[:, i, :], r.logit[:, i, 0:r.E])
            step(last)
            step(v.tensor_copy(r.idxf[:], r.idx[:]))
            for k in range(r.K):
                last = v.tensor_tensor(r.hot[:, k], iota_e[:, 0:r.E].unsqueeze(2).to_broadcast([P, r.E, NT]),
                                       r.idxf[:, :, k].unsqueeze(1).to_broadcast([P, r.E, NT]), ALU.is_equal)
            step(last)
            meanwhile(0)
            if r.K == 1:
                step(v.tensor_copy(r.m[:], r.hot[:, 0]))
            else:
                step(v.tensor_tensor(r.m[:], r.hot[:, 0], r.hot[:, 1], ALU.add))
                for k in range(2, r.K):
                    step(v.tensor_tensor(r.m[:], r.m[:], r.hot[:, k], ALU.add))
            step(v.memset(r.keep[:], 1.0))
            step(v.memset(r.keep[:, :, 0:1], 0.0))
            step(v.tensor_tensor_scan(r.cum[:].rearrange("p e i -> p (e i)"), r.keep[:].rearrange("p e i -> p (e i)"),
                                      r.m[:].rearrange("p e i -> p (e i)"), 0.0, ALU.mult, ALU.add))
            v.tensor_tensor(r.cumx[:], r.cum[:], r.m[:], ALU.subtract).then_inc(r.m_ready, 1)
            meanwhile(1)
            v.wait_ge(r.ranks_ready, 1)
            step(v.tensor_scalar(r.cnti[:], ps[:, 6, 0:r.E], float(P - 1), None, ALU.add))
            step(v.tensor_scalar(r.cnti[:], r.cnti[:], 7, None, ALU.arith_shift_right))
            step(v.tensor_copy(r.tiles[:], r.cnti[:]))
            step(v.tensor_tensor_scan(r.upto[:], r.ecmp[:], r.tiles[:], 0.0, ALU.mult, ALU.add))
            step(v.tensor_tensor(r.base[:], r.upto[:], r.tiles[:], ALU.subtract))
            step(v.tensor_scalar(r.base[:], r.base[:], float(P), None, ALU.mult))
            half = r.E // 2
            for c in range(2):
                last = v.tensor_tensor(r.rank[:, c * half:(c + 1) * half],
                                       ps[:, 4 + c, 0:half * NT].rearrange("p (e i) -> p e i", i=NT),
                                       r.base[:, c * half:(c + 1) * half].unsqueeze(2).to_broadcast([P, half, NT]), ALU.add)
            step(last)
            for k in range(r.K):
                step(v.tensor_tensor(r.prod[:], r.rank[:], r.hot[:, k], ALU.mult))
                step(v.tensor_reduce(r.slotf[:, k, :], r.prod[:].rearrange("p e i -> p i e"), AX.X, ALU.add))
                meanwhile(2 + k)
            v.tensor_copy(r.slot[:], r.slotf[:]).then_inc(r.slots_ready, 1)
            step(v.tensor_scalar(r.ecmp[:], r.upto[:], iota_p[:, 0:1], None, ALU.is_le))
            step(v.tensor_reduce(r.ecol[:, 0:1], r.ecmp[:], AX.X, ALU.add))
            step(v.tensor_scalar(r.ecol[:, 1:2], r.ecol[:, 0:1], float(r.E - 1), None, ALU.min))
            v.tensor_copy(r.ecoli[:], r.ecol[:, 1:2]).then_inc(r.tiles_known, 1)

        def route_pe(pe, r):
            pe.wait_ge(r.m_ready, 1)
            half = r.E // 2
            for c in range(2):
                o = ps[:, 4 + c, 0:half * NT]
                mm = r.m[:, c * half:(c + 1) * half].rearrange("p e i -> p (e i)")
                cx = r.cumx[:, c * half:(c + 1) * half].rearrange("p e i -> p (e i)")
                pe.matmul(o, before[:], mm, start=True, stop=False)
                pe.matmul(o, ones_b[:], cx, start=False, stop=True)
            pe.matmul(ps[:, 6, 0:r.E], ones_b[:], r.cum[:, :, NT - 1], start=True, stop=True).then_inc(r.ranks_ready, 1)

        def route_pool(g, r):
            g.wait_ge(r.zeroed, 16 * r.zero_dmas)
            g.wait_ge(r.slots_ready, 1)
            for k in range(r.K):
                for i in range(NT):
                    g.indirect_dma_start(r.slots, bass.IndirectOffsetOnAxis(ap=r.slot[:, k, i:i + 1], axis=0),
                                         xn[:, i, :], None).then_inc(r.scattered, 16)

        def route_sp(sp, r):
            sp.wait_ge(r.tiles_known, 1)
            sp.dma_start(r.etab_dram, r.ecoli[:]).then_inc(r.table_stored, 16)
            sp.wait_ge(r.table_stored, 16)
            sp.dma_start(r.etab[0:1, 0:r.routed], r.etab_dram[0:r.routed, :].rearrange("p o -> o p")).then_inc(r.table_loaded, 16)
            sp.wait_ge(r.table_loaded, 16)
            sp.wait_ge(r.scattered, 16 * NT * r.K)

        def zero_fill(sp, r):
            rows = 1024
            total = r.routed * P
            r.zero_dmas = -(-total // rows)
            for q in range(r.zero_dmas):
                n = min(rows, total - q * rows)
                sp.dma_start(r.slots[q * rows:q * rows + n, :].rearrange("(p a) d -> p (a d)", p=P),
                             zeros[:, 0:n * D // P]).then_inc(r.zeroed, 16)

        def tile_steps(eng, r, fn):
            first_shared, end = r.routed // RING, r.tiles_n // RING

            def out(i):
                for q in range(RING):
                    def kind(a, s=i * RING + q):
                        return None if s < a or s - a >= r.tiles_n else 'routed' if s - a < r.routed else 'shared'
                    fn(i, q, kind)

            def loop(lo, hi, what):
                with eng.Fori(lo, hi) as i:
                    for q in range(RING):
                        fn(i, q, lambda a: what)
            out(0)
            out(1)
            loop(2, first_shared, 'routed')
            if end > first_shared:
                out(first_shared)
                out(first_shared + 1)
                loop(first_shared + 2, end, 'shared')
            out(end)
            out(end + 1)

        def experts_sp(sp, r):
            def fn(i, q, kind):
                s = i * RING + q
                if kind(0):
                    if kind(0) == 'routed':
                        e = sp.value_load(r.etab[0:1, bass.ds(s, 1)], min_val=0, max_val=r.n_weights - 1)
                    w(sp, r.gu_ready, s - 3)
                    if kind(0) == 'routed':
                        sp.dma_start(r.xs[:, q], r.slots[bass.ds(s * P, P), :]).then_inc(r.x_loaded[q], 16)
                        sp.dma_start(r.w13[:, q], r.w13_dram[bass.ds(e, 1)].rearrange("o p c n -> (o p) c n")).then_inc(r.w13_loaded[q], 16)
                    else:
                        token_tile = i - r.routed // RING
                        sp.dma_start(r.xs[:, q], xn[:, bass.ds(token_tile, 1), :].rearrange("p o d -> p (o d)")).then_inc(r.x_loaded[q], 16)
                        if isinstance(i, int) and s < r.routed + SHARED:
                            sp.dma_start(r.w13[:, q], r.w13_dram[r.E + q]).then_inc(r.w13_loaded[q], 16)
            tile_steps(sp, r, fn)

        def experts_pool(g, r):
            def load(i, q):
                s = i * RING + q
                e = g.value_load(r.etab[0:1, bass.ds(s, 1)], min_val=0, max_val=r.n_weights - 1)
                w(g, r.dn_done, s - 3)
                g.dma_start(r.w2[:, q], r.w2_dram[bass.ds(e, 1)].rearrange("o p c n -> (o p) c n")).then_inc(r.w2_loaded[q], 16)
            g.wait_ge(r.table_loaded, 16)
            for q in range(RING):
                load(0, q)
            with g.Fori(1, r.routed // RING) as i:
                for q in range(RING):
                    load(i, q)
            if r.tiles_n > r.routed:
                for q in range(SHARED):
                    g.wait_ge(r.dn_done, r.routed + q - 3)
                    g.dma_start(r.w2[:, q], r.w2_dram[r.E + q]).then_inc(r.w2_loaded[q], 16)

        def experts_pe(pe, r):
            uses = r.routed // RING

            def fn(i, q, kind):
                s = i * RING + q
                if kind(0):
                    pe.wait_ge(r.x_loaded[q], (i + 1) * 16)
                    w(pe, r.xt_copied, s)
                    for c in range(DC):
                        last = pe.transpose(ps[:, 4, c * P:(c + 1) * P], r.xs[:, q, c * P:(c + 1) * P], ident[:])
                    last.then_inc(r.xt_ready, 1)
                if kind(1):
                    b = (q - 1) % RING
                    turn = i + (q - 1) // RING
                    if kind(1) == 'routed' or isinstance(i, int) and turn == uses:
                        pe.wait_ge(r.w13_loaded[b], (turn + 1) * 16)
                    pe.wait_ge(r.xt_copied, s)
                    w(pe, r.h_done, s - 2)
                    for c in range(DC):
                        last = pe.matmul(ps[:, GU_BANK[b % 2], 0:2 * INNER], r.xt[:, b % 2, c * P:(c + 1) * P], r.w13[:, b, c],
                                         start=c == 0, stop=c == DC - 1)
                    last.then_inc(r.gu_ready, 1)
                if kind(2):
                    b = (q - 2) % RING
                    pe.wait_ge(r.h_done, s - 1)
                    w(pe, r.ht_copied, s - 2)
                    for c in range(2):
                        last = pe.transpose(ps[0:IC, 6, c * P:(c + 1) * P], r.hh[:, b % 2, c * IC:(c + 1) * IC], ident[:])
                    last.then_inc(r.ht_ready, 1)
                if kind(3):
                    b = (q - 3) % RING
                    turn = i + (q - 3) // RING
                    pe.wait_ge(r.ht_copied, s - 2)
                    if kind(3) == 'routed':
                        pe.wait_ge(r.w2_loaded[b], (turn + 1) * 16)
                        w(pe, r.y_copied, s - 4)
                        bank, begins, ends = DN_BANK[b % 2], True, True
                    else:
                        if isinstance(i, int) and turn == uses:
                            pe.wait_ge(r.w2_loaded[b], (turn + 1) * 16)
                        if b == 0:
                            if isinstance(i, int) and turn == uses:
                                pe.wait_ge(r.y_copied, r.routed)
                            else:
                                pe.wait_ge(r.shared_added, turn - uses)
                        bank, begins, ends = DN_BANK[0], b == 0, b == SHARED - 1
                    for c in range(2):
                        last = pe.matmul(ps[:, bank, 0:D], r.ht[:, b % 2, c], r.w2[:, b, c],
                                         start=begins and c == 0, stop=ends and c == 1)
                    last.then_inc(r.dn_done, 1)
            tile_steps(pe, r, fn)

        def experts_act(act, r):
            def fn(i, q, kind):
                s = i * RING + q
                if kind(0):
                    act.wait_ge(r.xt_ready, s + 1)
                    w(act, r.gu_ready, s - 1)
                    act.copy(r.xt[:, q % 2], ps[:, 4, 0:D]).then_inc(r.xt_copied, 1)
                if kind(1):
                    b = (q - 1) % 2
                    act.wait_ge(r.gu_ready, s)
                    w(act, r.act_step, s - 2)
                    act.activation(r.th[:, b], ps[:, GU_BANK[b], 0:INNER], ACT.Tanh, scale=0.5).then_inc(r.tanh_ready, 1)
                if kind(3) == 'routed':
                    b = (q - 3) % RING
                    act.wait_ge(r.dn_done, s - 2)
                    w(act, r.stored[b], (i + (q - 3) // RING) * 16)
                    act.copy(r.yy[:, b], ps[:, DN_BANK[b % 2], 0:D]).then_inc(r.y_copied, 1)
                if kind(4) == 'routed':
                    b = (q - 4) % RING
                    act.wait_ge(r.y_copied, s - 3)
                    act.dma_start(r.result[bass.ds((s - 4) * P, P), :], r.yy[:, b]).then_inc(r.stored[b], 16)
            tile_steps(act, r, fn)

        def experts_dve(v, r):
            def add_result(i, k):
                n = i * r.K + k
                v.wait_ge(r.gathered[k], 16 * (i + 1))
                w(v, r.added, n)
                if k == 0:
                    v.wait_ge(r.shared_added, i + 1)
                xi = xr[:, bass.ds(i, 1), :].rearrange("p o d -> p (o d)")
                v.scalar_tensor_tensor(xi, r.got[:, k, :], r.weight[:, bass.ds(i, 1), k], xi, ALU.mult, ALU.add).then_inc(r.added, 1)

            def fn(i, q, kind):
                s = i * RING + q
                if kind(1):
                    b = (q - 1) % 2
                    v.wait_ge(r.tanh_ready, s)
                    v.scalar_tensor_tensor(r.ga[:, b], r.th[:, b], 1.0, ps[:, GU_BANK[b], 0:INNER], ALU.add, ALU.mult).then_inc(r.act_step, 1)
                    v.wait_ge(r.act_step, s)
                    w(v, r.ht_ready, s - 2)
                    v.scalar_tensor_tensor(r.hh[:, b], r.ga[:, b], 0.5, ps[:, GU_BANK[b], INNER:2 * INNER], ALU.mult, ALU.mult).then_inc(r.h_done, 1)
                if kind(2):
                    b = (q - 2) % 2
                    v.wait_ge(r.ht_ready, s - 1)
                    w(v, r.dn_done, s - 3)
                    v.tensor_copy(r.ht[:, b].rearrange("p c t -> p (c t)"), ps[0:IC, 6, 0:2 * P]).then_inc(r.ht_copied, 1)
                if kind(3) == 'shared' and q == 2:
                    token_tile = i - 1 - r.routed // RING
                    v.wait_ge(r.dn_done, s - 2)
                    xi = xr[:, bass.ds(token_tile, 1), :].rearrange("p o d -> p (o d)")
                    v.scalar_tensor_tensor(xi, ps[:, DN_BANK[0], 0:D], r.weight[:, bass.ds(token_tile, 1), r.K], xi,
                                           ALU.mult, ALU.add).then_inc(r.shared_added, 1)
                if r.tiles_n > r.routed and (not isinstance(i, int) and kind(0) == 'shared' or isinstance(i, int) and i >= r.tiles_n // RING):
                    add_result(i - 2 - r.routed // RING, q)
            tile_steps(v, r, fn)

        def gather_pool(g, r, tiles):
            if tiles[0] == 0:
                for q in range(RING):
                    g.wait_ge(r.stored[q], 16 * r.routed // RING)
            for i in tiles:
                for k in range(r.K):
                    n = i * r.K + k
                    if n >= 4:
                        g.wait_ge(r.added, n - 3)
                    g.indirect_dma_start(r.got[:, n % 4, :], None, r.result[:, :],
                                         bass.IndirectOffsetOnAxis(ap=r.slot[:, k, i:i + 1], axis=0)).then_inc(r.gathered[n % 4], 16)

        def gather_dve(v, r, tiles):
            for i in tiles:
                for k in range(r.K):
                    n = i * r.K + k
                    v.wait_ge(r.gathered[n % 4], 16 * (n // 4 + 1))
                    if k > 0:
                        v.wait_ge(r.added, n)
                    v.scalar_tensor_tensor(xr[:, i, :], r.got[:, n % 4, :], r.weight[:, i, k:k + 1], xr[:, i, :],
                                           ALU.mult, ALU.add).then_inc(r.added, 1)

        ITS = BATCH * HEADS

        def chunk_of(qt):
            return qt if qt < 4 else 4 + 2 * (qt - 4)

        def chunks(qt):
            return [(chunk_of(qt) + j // 4, j, min(j + 4, qt + 1)) for j in range(0, qt + 1, 4)]
        CHUNKS = 12

        def use7(it, n):
            return 5 + 5 * it + n + 1

        OUT1, W2, W3, OUT0, W0, W1, VHALF = range(7)

        def use6(it, n):
            return 7 * it + n - 1 if not (isinstance(it, int) and it == ITS) else 7 * it + n - 2

        def heads_loop(eng, body):
            for b in range(BATCH):
                body(0, b, False)
            with eng.Fori(1, HEADS - 1) as h:
                for b in range(BATCH):
                    body(h, b, False)
            for b in range(BATCH):
                body(HEADS - 1, b, b == BATCH - 1)

        def first(it):
            return isinstance(it, int) and it == 0

        def three(pe, out_ap, a_r, a_l, b_r, b_l, start, stop):
            pe.matmul(out_ap, a_r, b_r, start=start, stop=False)
            pe.matmul(out_ap, a_l, b_r, start=False, stop=False)
            return pe.matmul(out_ap, a_r, b_l, start=False, stop=stop)

        def att_pe(pe):
            def scores(it, qt, buf):
                w(pe, s_exp, 8 * it + qt - 1)
                if qt == 4:
                    w(pe, s_ql, 4 * it + 4)
                if qt == 8:
                    w(pe, s_ql, 4 * it + 6)
                qn = qt % 8
                bank = 2 * (qt % 2)
                for c in range(0, qn + 1, 4):
                    cols = min(4, qn + 1 - c) * P
                    o = ps[:, bank + c // 4, 0:cols]
                    qs = slice(qn * P, (qn + 1) * P)
                    ks = slice(c * P, c * P + cols)
                    last = three(pe, o, qkr[:, buf, 0, qs], qkl[:, buf, 0, qs], qkr[:, buf, 1, ks], qkl[:, buf, 1, ks],
                                 True, qn // 4 != c // 4)
                    if qn // 4 == c // 4:
                        last = pe.matmul(ps[:, bank + c // 4, (qn - c) * P:(qn - c + 1) * P], ident_b[:], maskb[:], start=False, stop=True)
                last.then_inc(s_S, 1)

            def piece(p, target_b, count):
                w(pe, s_e7, count - 1)
                which, half = p % 2, p // 2
                sl = slice(target_b * SEQ + half * 512, target_b * SEQ + half * 512 + 512)
                for c in range(DC):
                    last = three(pe, ps[:, 7, :], wr[:, which, c], wl[:, which, c], xnr[:, c, sl], xnl[:, c, sl], c == 0, c == DC - 1)
                last.then_inc(s_b7, 1)

            def v_half(half, bank, target_b, s_fill):
                for i in range(4):
                    t0 = target_b * SEQ + (half * 4 + i) * P
                    for c in range(DC):
                        last = pe.matmul(ps[:, bank, i * P:(i + 1) * P], xnT1[:, c, t0:t0 + P], wv[:, c], start=c == 0, stop=c == DC - 1)
                last.then_inc(s_fill, 1)

            def transposes(it, qt):
                w(pe, s_exp, 8 * it + qt + 1)
                for ci, j0, j1 in chunks(qt):
                    if j0 == 4 and qt > 4:
                        pe.wait_ge(s_pl, 4 * it + qt - 4)
                    elif j0 == 4:
                        pe.wait_ge(s_pr, 8 * it + 4)
                    elif qt == 1:
                        w(pe, s_pl, 4 * it)
                    elif qt >= 5 or qt == 0:
                        w(pe, s_pr, 8 * it + qt)
                    else:
                        w(pe, s_pr, 8 * it + qt - 1)
                    for j in range(j0, j1):
                        last = pe.transpose(ps[:, 4 + ci % 2, (j - j0) * P:(j - j0 + 1) * P], pb[:, qt % 2, j * P:(j + 1) * P], ident[:])
                    last.then_inc(s_T, 1)

            def output(g, buf, keys):
                for j in keys:
                    c0 = max(0, j - 4 * g) * P
                    last = pe.matmul(ps[:, 6, c0:512], v[:, buf, j], pt[g][:, j, c0:512], start=j == 0, stop=j == 4 * g + 3)
                if keys[-1] == 4 * g + 3:
                    last.then_inc(s_b6, 1)

            def project_out(which, count):
                w(pe, s_e6, count - 1)
                for a in range(2):
                    sl = slice((2 * (which % 2) + a) * P, (2 * (which % 2) + a + 1) * P)
                    last = pe.matmul(ps[:, 6, a * D:(a + 1) * D], ot[:, sl], wo[:], start=True, stop=True)
                last.then_inc(s_b6, 1)

            def output1(it, b, part):
                if part == 0:
                    w(pe, s_e6, use6(it, OUT1) - 1)
                    pe.wait_ge(s_pr, 8 * it)
                    pe.wait_ge(s_pl, 4 * it)
                output(1, 1 - b, (range(0, 3), range(3, 8))[part])

            pe.wait_ge(s_split, 2 * NG)
            pe.wait_ge(s_ws, 1)
            for p in range(2):
                piece(p, 0, p + 1)
            route_pe(pe, R1)
            for p in range(2, 4):
                piece(p, 0, p + 1)
            pe.wait_ge(s_e7, 4)
            pe.wait_ge(R1.slots_ready, 1)
            v_half(1, 6, 0, s_b6)
            v_half(0, 7, 0, s_b7)
            pe.wait_ge(s_mask, 1)
            pe.wait_ge(s_ql, 4)
            scores(0, 0, 0)
            scores(0, 1, 0)

            def body(h, b, last):
                it = 2 * h + b
                for qt in range(8):
                    transposes(it, qt)
                    if qt < 6:
                        scores(it, qt + 2, b)
                    elif not last:
                        scores(it, qt + 2, 1 - b)
                    if qt in (0, 1) and not first(it):
                        output1(it, b, qt)
                    if qt in (2, 3, 5, 6) and not last:
                        if qt == 2 and b == BATCH - 1:
                            pe.wait_ge(s_ws, h + 2)
                        p = {2: 0, 3: 1, 5: 2, 6: 3}[qt]
                        piece(p, 1 - b, use7(it, p))
                    if qt in (2, 3) and not first(it):
                        project_out(qt, use6(it, W2 if qt == 2 else W3))
                    if qt == 4:
                        w(pe, s_e7, use7(it - 1, 4))
                        w(pe, s_e6, use6(it, OUT0) - 1)
                        pe.wait_ge(s_pr, 8 * it + 4)
                        output(0, b, range(0, 4))
                    if qt in (5, 6):
                        if qt == 5 and b == 0:
                            pe.wait_ge(s_wos, h + 1)
                        project_out(qt - 5, use6(it, W0 if qt == 5 else W1))
                    if qt == 7 and not last:
                        pe.wait_ge(s_e6, use6(it, VHALF) - 1)
                        v_half(1, 6, 1 - b, s_b6)
                        pe.wait_ge(s_e7, use7(it, 4) - 1)
                        v_half(0, 7, 1 - b, s_b7)
            heads_loop(pe, body)
            for part in range(2):
                output1(ITS, 0, part)
            for which, n in ((2, W2), (3, W3)):
                project_out(which, use6(ITS, n))

        def att_act(act):
            def probs(it, qt):
                act.wait_ge(s_T, CHUNKS * it + chunk_of(qt) + 1)
                if qt == 0:
                    w(act, s_b6, use6(it - 1, OUT0))
                if qt == 4:
                    w(act, s_b6, use6(it, OUT1))
                g, j1 = qt // 4, min(4, qt + 1)
                cols = slice((qt % 4) * P, (qt % 4 + 1) * P)
                act.copy(pt[g][:, 0:j1, cols], ps[:, 4 + chunk_of(qt) % 2, 0:j1 * P].rearrange("p (j q) -> p j q", q=P)).then_inc(s_pr, 1)

            def exp_tile(it, qt, b):
                w(act, s_max, 8 * it + qt + 1)
                if qt >= 2:
                    act.wait_ge(s_T, CHUNKS * it + chunk_of(qt - 2) + len(chunks(qt - 2)))
                else:
                    w(act, s_T, CHUNKS * it - (2, 0)[qt])
                qn, par = qt % 8, b if qt < 8 else 1 - b
                cols = (qn + 1) * P
                bank = 2 * (qt % 2)
                act.activation(pb[:, qt % 2, 0:cols], ps[:, bank:bank + 2, :].rearrange("p a n -> p (a n)")[:, 0:cols], ACT.Exp,
                               bias=negmax[:, par, qn:qn + 1], accum_out=rowsum[:, par, qn:qn + 1]).then_inc(s_exp, 1)

            def swap(n, p, count):
                act.wait_ge(s_b7, count)
                w(act, s_rot, n - 1)
                act.copy(sw[64:96, p % 2, :], ps[96:128, 7, :])
                act.copy(sw[96:128, p % 2, :], ps[64:96, 7, :]).then_inc(s_a7, 1)

            def rounded(n, p, buf):
                act.wait_ge(s_rot, n + 1)
                act.copy(qkr[:, buf, p % 2, (p // 2) * 512:(p // 2 + 1) * 512], t1[:, p % 2, :]).then_inc(s_qr, 1)

            def v_first(buf, count):
                act.wait_ge(s_b7, count)
                act.copy(v[:, buf, 0:4, :].rearrange("p i d -> p (i d)"), ps[:, 7, :]).then_inc(s_e7, 1)

            def output1(it):
                act.wait_ge(s_b6, use6(it, OUT1))
                act.copy(ot[:], ps[:, 6, :]).then_inc(s_e6, 1)

            for p in range(4):
                swap(p, p, p + 1)
                rounded(p, p, 0)
            act.wait_ge(s_w1, 3)
            act.activation(R1.rank[:], R1.rank[:], ACT.Exp).then_inc(s_w1a, 1)
            act.activation(R1.weight[:, :, 0:K1], R1.weight[:, :, 0:K1], ACT.Exp).then_inc(s_w1a, 1)
            act.activation(R1.weight[:, :, K1], R1.logit[:, :, E1], ACT.Exp, scale=-1.0).then_inc(s_w1a, 1)
            v_first(0, 5)
            exp_tile(0, 0, 0)

            def body(h, b, last):
                it = 2 * h + b
                n0 = 4 * (it + 1)
                for qt in range(8):
                    probs(it, qt)
                    if qt < 7 or not last:
                        exp_tile(it, qt + 1, b)
                    if qt == 1 and not first(it):
                        output1(it)
                    if qt in (2, 3, 5, 6) and not last:
                        p = {2: 0, 3: 1, 5: 2, 6: 3}[qt]
                        swap(n0 + p, p, use7(it, p))
                    if qt in (3, 4, 6, 7) and not last:
                        p = {3: 0, 4: 1, 6: 2, 7: 3}[qt]
                        rounded(n0 + p, p, 1 - b)
                    if qt == 7 and not last:
                        v_first(1 - b, use7(it, 4))
            heads_loop(act, body)
            output1(ITS)

        def weights1(v):
            soft = R1.rank[:].rearrange("p e i -> p (e i)").rearrange("p (i e) -> p i e", e=E1)
            top0 = R1.top[:, :, 0:1]
            v.tensor_tensor(soft, R1.logit[:, :, 0:E1], top0.to_broadcast([P, NT, E1]), ALU.subtract).then_inc(s_w1, 1)
            v.tensor_tensor(R1.weight[:, :, 0:K1], R1.top[:, :, 0:K1], top0.to_broadcast([P, NT, K1]), ALU.subtract).then_inc(s_w1, 1)
            v.memset(R1.weight[:, :, K1:], 0.0).then_inc(s_w1, 1)
            v.wait_ge(s_w1a, 3)
            v.tensor_reduce(R1.weight[:, :, 5], soft, AX.X, ALU.add).then_inc(s_w1, 1)
            v.tensor_scalar(R1.weight[:, :, K1], R1.weight[:, :, K1], 1.0, None, ALU.add).then_inc(s_w1, 1)
            v.wait_ge(s_w1, 5)
            v.reciprocal(R1.weight[:, :, K1:6], R1.weight[:, :, K1:6]).then_inc(s_w1, 1)
            v.wait_ge(s_w1, 6)
            v.tensor_tensor(R1.weight[:, :, 0:K1], R1.weight[:, :, 0:K1], R1.weight[:, :, 5:6].to_broadcast([P, NT, K1]), ALU.mult).then_inc(s_w1, 1)
            v.wait_ge(s_w1, 7)

        def att_dve(dve):
            def max_tile(it, qt, b):
                qn, par = qt % 8, b if qt < 8 else 1 - b
                cols = (qn + 1) * P
                bank = 2 * (qt % 2)
                dve.wait_ge(s_S, 8 * it + qt + 1)
                dve.tensor_reduce(negmax[:, par, qn:qn + 1], ps[:, bank:bank + 2, :].rearrange("p a n -> p (a n)")[:, 0:cols], AX.X, ALU.max,
                                  negate=True).then_inc(s_max, 1)

            def probs(it, qt):
                dve.wait_ge(s_T, CHUNKS * it + chunk_of(qt) + 2)
                cols = slice((qt % 4) * P, (qt % 4 + 1) * P)
                if qt == 4:
                    w(dve, s_b6, use6(it, OUT1))
                dve.tensor_copy(pt[1][:, 4:qt + 1, cols], ps[:, 5, 0:(qt - 3) * P].rearrange("p (j q) -> p j q", q=P)).then_inc(s_pl, 1)

            def turned(n, p):
                dve.wait_ge(s_a7, n + 1)
                w(dve, s_ql, n - 1)
                dve.tensor_tensor(t1[:, p % 2, :], ps[:, 7, :], rope_t[:, 0, (p // 2) * 512:(p // 2 + 1) * 512], ALU.mult).then_inc(s_e7, 1)

            def rest(n, p, buf):
                dve.wait_ge(s_qr, n + 1)
                o = (slice(None), buf, p % 2, slice((p // 2) * 512, (p // 2 + 1) * 512))
                dve.tensor_tensor(qkl[o], t1[:, p % 2, :], qkr[o].bitcast(F32), ALU.subtract).then_inc(s_ql, 1)

            def v_second(buf, count):
                dve.wait_ge(s_b6, count)
                dve.tensor_copy(v[:, buf, 4:8, :].rearrange("p i d -> p (i d)"), ps[:, 6, :]).then_inc(s_e6, 1)

            def add_out(which, b_out, count):
                dve.wait_ge(s_b6, count)
                for a in range(2):
                    qn = 2 * which + a
                    i = b_out * 8 + qn
                    last = dve.scalar_tensor_tensor(xr[:, i, :], ps[:, 6, a * D:(a + 1) * D], rinv[:, b_out, qn:qn + 1], xr[:, i, :], ALU.mult, ALU.add)
                last.then_inc(s_e6, 1)

            def invert(it, g, b):
                dve.wait_ge(s_exp, 8 * it + 4 * g + 4)
                dve.reciprocal(rinv[:, b, 4 * g:4 * g + 4], rowsum[:, b, 4 * g:4 * g + 4]).then_inc(s_rinv, 1)
                dve.wait_ge(s_rinv, 2 * it + g + 1)

            def split(h):
                dve.wait_ge(s_wraw, (h + 1) * 16)
                for part in range(2):
                    sl = slice(part * QK, (part + 1) * QK)
                    last = dve.tensor_scalar(wraw[:, 0, :, sl], wraw[:, 0, :, sl], gsc[:, part, bass.ds(h, 1)], None, ALU.mult)
                last.then_inc(s_wsc, 1)
                dve.tensor_copy(wv[:], wraw[:, 2])
                dve.wait_ge(s_wsc, h + 1)
                dve.tensor_copy(wr[:], wraw[:, 0:2]).then_inc(s_rnd, 1)
                dve.wait_ge(s_rnd, h + 1)
                dve.tensor_tensor(wl[:], wraw[:, 0:2], wr[:].bitcast(F32), ALU.subtract).then_inc(s_ws, 1)

            def meanwhile(part):
                if part < 4:
                    turned(part, part)
                if 0 < part < 5:
                    rest(part - 1, part - 1, 0)

            split(0)
            dve.memset(R1.ecmp[:], 1.0)
            route_dve(dve, R1, meanwhile)
            weights1(dve)
            v_second(0, 1)
            max_tile(0, 0, 0)

            def body(h, b, last):
                it = 2 * h + b
                n0 = 4 * (it + 1)
                for qt in range(8):
                    if qt < 7 or not last:
                        max_tile(it, qt + 1, b)
                    if qt >= 4:
                        probs(it, qt)
                    if qt == 0 and not first(it):
                        rest(n0 - 1, 3, b)
                    if qt in (4, 5, 7) and not last:
                        p = {4: 0, 5: 1, 7: 2}[qt]
                        rest(n0 + p, p, 1 - b)
                    if qt == 6:
                        add_out(1, b, use6(it, W1))
                    if qt in (2, 3, 5, 6) and not last:
                        p = {2: 0, 3: 1, 5: 2, 6: 3}[qt]
                        turned(n0 + p, p)
                    if qt in (2, 3) and not first(it):
                        add_out(qt, 1 - b, use6(it, W2 if qt == 2 else W3))
                    if qt == 5:
                        add_out(0, b, use6(it, W0))
                    if qt == 0 and b == 1 and not (isinstance(h, int) and h == HEADS - 1):
                        dve.wait_ge(s_b7, use7(it - 1, 4))
                        split(h + 1)
                    if qt in (4, 7):
                        invert(it, qt // 7, b)
                    if qt == 4 and b == 0:
                        dve.wait_ge(s_wor, (h + 1) * 16)
                        dve.tensor_copy(wo[:], woraw[:]).then_inc(s_wos, 1)
                    if qt == 4:
                        dve.wait_ge(s_b6, use6(it, OUT0))
                        dve.tensor_copy(ot[:], ps[:, 6, :]).then_inc(s_e6, 1)
                    if qt == 7 and not last:
                        v_second(1 - b, use6(it, VHALF))
            heads_loop(dve, body)
            for which, n in ((2, W2), (3, W3)):
                add_out(which, 1, use6(ITS, n))

        def att_pool(g):
            def rotate(it, p):
                n = 4 * it + p
                g.wait_ge(s_a7, n + 1)
                g.tensor_tensor(sw[64:128, p % 2, :], sw[64:128, p % 2, :], rope_t[64:128, 1, (p // 2) * 512:(p // 2 + 1) * 512], ALU.mult).then_inc(s_t2, 1)
                g.wait_ge(s_t2, n + 1)
                g.wait_ge(s_e7, 5 * it + p + 1)
                g.tensor_tensor(t1[64:128, p % 2, :], t1[64:128, p % 2, :], sw[64:128, p % 2, :], ALU.add).then_inc(s_rot, 1)
            g.wait_ge(s_par1, 64)
            for p in range(4):
                rotate(0, p)
            g.wait_ge(R1.zeroed, 16 * R1.zero_dmas)
            g.wait_ge(R1.slots_ready, 1)

            def body(h, b, last):
                it = 2 * h + b
                g.wait_ge(s_rot, 4 * it + 4)
                g.tensor_tensor(fence[:], iota_p[:], iota_p[:], ALU.add).then_inc(s_cols, 1)
                g.tensor_copy(slot_cols[:].unsqueeze(2), R1.slot[:, 2 * b:2 * b + 2, bass.ds(h, 1)]).then_inc(s_cols, 1)
                if b == 0:
                    g.tensor_copy(staged[:], xn[:, bass.ds(h, 1), :].rearrange("p o d -> p (o d)")).then_inc(s_staged, 1)
                    g.wait_ge(s_staged, h + 1)
                g.wait_ge(s_cols, 3 * it + 2)
                g.tensor_tensor(fence[:], iota_p[:], iota_p[:], ALU.add).then_inc(s_cols, 1)
                for k in range(2):
                    g.indirect_dma_start(R1.slots, bass.IndirectOffsetOnAxis(ap=slot_cols[:, k:k + 1], axis=0),
                                         staged[:], None).then_inc(R1.scattered, 16)
                g.wait_ge(R1.scattered, 32 * it + 32)
                g.wait_ge(s_cols, 3 * it + 3)
                if not last:
                    for p in range(4):
                        rotate(it + 1, p)
            heads_loop(g, body)

        def att_sp(sp):
            sp.dma_start(wraw[:], wqkv[0]).then_inc(s_wraw, 16)
            sp.dma_start(woraw[:], wo_h[0]).then_inc(s_wor, 16)
            with sp.Fori(1, HEADS) as h:
                sp.wait_ge(s_ws, h)
                sp.dma_start(wraw[:], wqkv[bass.ds(h, 1)].rearrange("o p a c n -> (o p) a c n")).then_inc(s_wraw, 16)
                sp.wait_ge(s_wos, h)
                sp.dma_start(woraw[:], wo_h[bass.ds(h, 1)].rearrange("o p n -> (o p) n")).then_inc(s_wor, 16)

        block = ctx.enter_context(nc.Block())

        @block.sync
        def _(sp):
            for g in range(NG):
                sp.dma_start(xr[:, g * GT:(g + 1) * GT, :],
                             x_in[g * GT * P:(g + 1) * GT * P, :].rearrange("(i p) d -> p i d", p=P)).then_inc(s_x[g], 16)
            sp.dma_start(xpw[:], xproj).then_inc(s_par, 16)
            sp.dma_start(dtw[:], dtproj).then_inc(s_par, 16)
            sp.dma_start(dtb[:], dt_bias).then_inc(s_par, 16)
            sp.dma_start(alog[:], a_log).then_inc(s_par, 16)
            sp.dma_start(dpar[:], d_param).then_inc(s_par, 16)
            sp.dma_start(rw0[:], router0).then_inc(s_par, 16)
            sp.wait_ge(s_const, 1)
            zero_fill(sp, R0)
            zero_fill(sp, R1)
            sp.wait_ge(s_xdc, 8)
            sp.dma_start(bc_rows, bcT).then_inc(s_bc, 16)
            route_sp(sp, R0)
            sp.wait_ge(s_bc, 16)
            sp.wait_ge(s_dp, 8)
            for b in range(BATCH):
                with sp.Fori(0, STATES // 2) as j:
                    for q in range(2):
                        it = b * STATES + j * 2 + q
                        for rows, off, used, loaded in ((brow, 0, s_dbx, s_brow), (crow, STATES, s_hc, s_crow)):
                            sp.wait_ge(used, it + 1)
                            sp.dma_start(rows[:, q, :], bc_rows[bass.ds(j * 2 + q + off, 1), b * SEQ:(b + 1) * SEQ]
                                         .to_broadcast([P, SEQ])).then_inc(loaded[q], 16)
            sp.wait_ge(s_ysum, 2 + BATCH * STATES)
            experts_sp(sp, R0)
            sp.wait_ge(s_xn, 2 * NG)
            sp.dma_start(rw1[:], router1).then_inc(s_par1, 16)
            sp.dma_start(rope_t[:], rope).then_inc(s_par1, 16)
            sp.dma_start(gsc[:, 0, :], gate_logit.to_broadcast([P, HEADS])).then_inc(s_par1, 16)
            sp.dma_start(gsc[:, 1, :], gate_logit.to_broadcast([P, HEADS])).then_inc(s_par1, 16)
            att_sp(sp)
            route_sp(sp, R1)
            sp.wait_ge(s_e6, use6(ITS, W3))
            sp.wait_ge(s_e7, use7(ITS - 2, 4))
            experts_sp(sp, R1)
            for q in range(NG):
                sp.wait_ge(R1.shared_added, (q + 1) * GT)
                sp.wait_ge(R1.added, (q + 1) * GT * K1)
                sp.dma_start(out[q * GT * P:(q + 1) * GT * P, :].rearrange("(i p) d -> p i d", p=P),
                             xr[:, q * GT:(q + 1) * GT, :]).then_inc(s_out, 16)
            sp.wait_ge(s_out, 16 * NG)
            for q in range(RING):
                sp.wait_ge(R1.stored[q], 16 * R1.routed // RING)
            sp.wait_ge(R1.zeroed, 16 * R1.zero_dmas)
            for q in range(RING):
                sp.wait_ge(R0.stored[q], 16 * R0.tiles_n // RING)
            sp.wait_ge(R0.zeroed, 16 * R0.zero_dmas)

        @block.gpsimd
        def _(g):
            n = [0]

            def step(ins):
                n[0] += 1
                ins.then_inc(s_const, 1)
                g.wait_ge(s_const, n[0])
            step(g.memset(zeros[:], 0.0))
            step(g.memset(neg_half[:], -0.5))
            step(g.memset(zero_b[:], 0.0))
            step(g.memset(ones_b[:], 1.0))
            step(g.memset(ident[:], 0.0))
            step(g.affine_select(out=ident[:], in_=ident[:], compare_op=ALU.not_equal, fill=1.0, base=0,
                                 pattern=[[-1, P]], channel_multiplier=1))
            step(g.tensor_copy(ident_b[:], ident[:]))
            step(g.affine_select(out=before[:], in_=ones_b[:], compare_op=ALU.is_gt, fill=0.0, base=0,
                                 pattern=[[1, P]], channel_multiplier=-1))
            step(g.iota(iota_e[:], [[1, E1]], base=0, channel_multiplier=0, allow_small_or_imprecise_dtypes=True))
            step(g.iota(iota_p[:], [[1, 1]], base=0, channel_multiplier=1, allow_small_or_imprecise_dtypes=True))
            for q in range(NG):
                g.wait_ge(s_var, q + 1)
                g.tensor_tensor(stat[:, 1, q * GT:(q + 1) * GT], stat[:, 0, q * GT:(q + 1) * GT],
                                neg_half[:, q * GT:(q + 1) * GT], ALU.pow).then_inc(s_rstd, 1)
            route_pool(g, R0)
            g.wait_ge(R0.scattered, 16 * NT)
            g.wait_ge(s_delta, 2)
            for b in range(BATCH):
                with g.Fori(0, STATES // 2) as j:
                    for q in range(2):
                        it = b * STATES + j * 2 + q
                        g.wait_ge(s_brow[q], (b * (STATES // 2) + j + 1) * 16)
                        g.wait_ge(s_hc, it + 1)
                        g.tensor_tensor(state[:, q], dx[:, :, b * SEQ:(b + 1) * SEQ],
                                        brow[:, q, :].unsqueeze(1).to_broadcast([P, DC, SEQ]), ALU.mult).then_inc(s_dbx, 1)
            experts_pool(g, R0)
            gather_pool(g, R0, range(GT))
            for q in range(NG):
                if q < NG - 1:
                    gather_pool(g, R0, range((q + 1) * GT, (q + 2) * GT))
                g.wait_ge(s_var, NG + q + 1)
                g.tensor_tensor(stat[:, 1, q * GT:(q + 1) * GT], stat[:, 0, q * GT:(q + 1) * GT],
                                neg_half[:, q * GT:(q + 1) * GT], ALU.pow).then_inc(s_rstd, 1)
            g.wait_ge(s_xn, 2 * NG)
            g.affine_select(out=maskb[:], in_=zero_b[:], compare_op=ALU.is_ge, fill=-1e9, base=0,
                            pattern=[[-1, P]], channel_multiplier=1).then_inc(s_mask, 1)
            g.wait_ge(s_mask, 1)
            att_pool(g)
            g.wait_ge(s_e6, use6(ITS, W3))
            g.wait_ge(s_e7, use7(ITS - 2, 4))
            experts_pool(g, R1)
            gather_pool(g, R1, range(NT))

        N_CONST = 10

        @block.vector
        def _(v):
            def ln(layer):
                def statistics(q):
                    sl = slice(q * GT, (q + 1) * GT)
                    n = 2 * (layer * NG + q)
                    if layer == 0:
                        v.wait_ge(s_x[q], 16)
                    else:
                        gather_dve(v, R0, range(q * GT, (q + 1) * GT))
                        v.wait_ge(R0.added, GT * (q + 1))
                    for i in range(q * GT, (q + 1) * GT):
                        last = v.bn_stats(bn[:, i, :], xr[:, i, :])
                    last.then_inc(s_ln, 1)
                    v.wait_ge(s_ln, n + 1)
                    for i in range(q * GT, (q + 1) * GT):
                        last = v.bn_aggr(mean_var[:, i, :], bn[:, i, :])
                    last.then_inc(s_ln, 1)
                    v.wait_ge(s_ln, n + 2)
                    v.tensor_scalar(stat[:, 0, sl], mean_var[:, sl, 1], EPS, None, ALU.add).then_inc(s_var, 1)

                def normalise(q):
                    v.wait_ge(s_rstd, layer * NG + q + 1)
                    for i in range(q * GT, (q + 1) * GT):
                        last = v.tensor_scalar(xn[:, i, :], xr[:, i, :], mean_var[:, i, 0:1], stat[:, 1, i:i + 1], ALU.subtract, ALU.mult)
                    last.then_inc(s_xn, 1)

                for q in range(NG):
                    statistics(q)
                    if q:
                        normalise(q - 1)
                normalise(NG - 1)
            ln(0)
            v.wait_ge(s_const, N_CONST)
            for b in range(BATCH):
                m = [10 * b]

                def sstep(ins):
                    m[0] += 1
                    ins.then_inc(s_sp, 1)
                    v.wait_ge(s_sp, m[0])
                dl = delta[:, :, b * SEQ:(b + 1) * SEQ]

                def two(a):
                    return a.rearrange("p (c t) -> p c t", c=DC)
                v.wait_ge(s_spa, b + 1)
                sstep(v.tensor_scalar(sp_z, sp_e, 2.0, None, ALU.add))
                sstep(v.reciprocal(sp_z, sp_z))
                sstep(v.tensor_tensor(sp_s, sp_e, sp_z, ALU.mult))
                sstep(v.tensor_tensor(sp_z, sp_s, sp_s, ALU.mult))
                sstep(v.tensor_scalar(sp_e, sp_z, COEF[4], COEF[3], ALU.mult, ALU.add))
                sstep(v.tensor_tensor(sp_e, sp_e, sp_z, ALU.mult))
                sstep(v.scalar_tensor_tensor(sp_e, sp_e, COEF[2], sp_z, ALU.add, ALU.mult))
                sstep(v.scalar_tensor_tensor(sp_e, sp_e, COEF[1], sp_z, ALU.add, ALU.mult))
                sstep(v.scalar_tensor_tensor(sp_e, sp_e, COEF[0], sp_s, ALU.add, ALU.mult))
                sstep(v.scalar_tensor_tensor(dl, two(sp_x), 0.0, two(sp_e), ALU.max, ALU.add))
                v.tensor_tensor(dx[:, :, b * SEQ:(b + 1) * SEQ], dl, xnT[:, :, b * SEQ:(b + 1) * SEQ], ALU.mult).then_inc(s_delta, 1)
                if b == 0:
                    v.memset(R0.ecmp[:], 1.0)
                    route_dve(v, R0)
                    v.tensor_tensor(R0.weight[:, :, 0], R0.top[:, :, 1], R0.top[:, :, 0], ALU.subtract).then_inc(s_w0, 1)
                    v.wait_ge(s_w0, 2)
                    v.tensor_scalar(R0.weight[:, :, 0], R0.weight[:, :, 1], 1.0, None, ALU.add).then_inc(s_w0, 1)
                    v.wait_ge(s_w0, 3)
                    v.reciprocal(R0.weight[:, :, 0], R0.weight[:, :, 0]).then_inc(s_w0, 1)
                    v.wait_ge(s_w0, 4)
            v.wait_ge(s_delta, 2)
            v.memset(decay[:, 0, :, 0:1], 0.0).then_inc(s_dbx, 2)
            v.memset(decay[:, 1, :, 0:1], 0.0).then_inc(s_hc, 2)
            for b in range(BATCH):
                with v.Fori(0, STATES // 2) as j:
                    for q in range(2):
                        it = b * STATES + j * 2 + q
                        flat = state[:, q].rearrange("p c t -> p (c t)")
                        v.wait_ge(s_dbx, it + 3)
                        v.wait_ge(s_dec, it + 1)
                        v.tensor_tensor_scan(flat, decay[:, q].rearrange("p c t -> p (c t)"), flat, 0.0,
                                             ALU.mult, ALU.add).then_inc(s_scan, 1)
                        v.wait_ge(s_scan, it + 1)
                        v.wait_ge(s_ysum, it + 1)
                        v.wait_ge(s_crow[q], (b * (STATES // 2) + j + 1) * 16)
                        v.tensor_tensor(hc[:, q], state[:, q],
                                        crow[:, q, :].unsqueeze(1).to_broadcast([P, DC, SEQ]), ALU.mult).then_inc(s_hc, 1)
                v.wait_ge(s_ysum, 2 + (b + 1) * STATES)
                v.wait_ge(s_dec, (b + 1) * STATES)
                for c in range(DC):
                    last = v.scalar_tensor_tensor(delta[:, c, b * SEQ:(b + 1) * SEQ], xnT[:, c, b * SEQ:(b + 1) * SEQ],
                                                  dpar[:, c:c + 1], ps[:, 2 * c:2 * c + 2, :].rearrange("p a t -> p (a t)"), ALU.mult, ALU.add)
                last.then_inc(s_yT, 1)
            for i in range(NT // 2):
                v.wait_ge(s_yT_ps, i + 1)
                v.tensor_tensor(xr[:, 2 * i:2 * i + 2, :], xr[:, 2 * i:2 * i + 2, :],
                                ps[:, i % 2, :].rearrange("p (a d) -> p a d", a=2), ALU.add).then_inc(s_yadd, 1)
            experts_dve(v, R0)
            v.wait_ge(s_yadd, NT // 2)
            v.wait_ge(R1.zeroed, 16 * R1.zero_dmas)
            ln(1)
            for q in range(NG):
                sl = slice(q * 512, (q + 1) * 512)
                v.wait_ge(s_xnT1, q + 1)
                v.tensor_copy(xnr[:, :, sl], xnT1[:, :, sl]).then_inc(s_split, 1)
                v.wait_ge(s_split, 2 * q + 1)
                v.tensor_tensor(xnl[:, :, sl], xnT1[:, :, sl], xnr[:, :, sl].bitcast(F32), ALU.subtract).then_inc(s_split, 1)
            gs = [0]

            def gstep(ins):
                gs[0] += 1
                ins.then_inc(s_gate, 1)
                v.wait_ge(s_gate, gs[0])
            v.wait_ge(s_gact, 1)
            gstep(v.tensor_scalar(gsc[:], gsc[:], 1.0, None, ALU.add))
            gstep(v.reciprocal(gsc[:], gsc[:]))
            gstep(v.tensor_scalar(gsc[:, 1, :], gsc[:, 1, :], -1.0, 1.0, ALU.mult, ALU.add))
            gstep(v.tensor_scalar(gsc[:], gsc[:], QK ** -0.5, None, ALU.mult))
            att_dve(v)
            v.wait_ge(s_e6, use6(ITS, W3))
            v.wait_ge(s_e7, use7(ITS - 2, 4))
            experts_dve(v, R1)

        @block.scalar
        def _(act):
            act.wait_ge(s_par, 96)
            act.activation(alog[:], alog[:], ACT.Exp).then_inc(s_aneg, 1)
            act.wait_ge(s_aneg, 1)
            act.mul(aneg[:], alog[:], -1.0).then_inc(s_aneg, 1)
            for q in range(NG):
                act.wait_ge(s_xnT_ps, q + 1)
                for c in range(DC):
                    last = act.copy(xnT[:, c, q * 512:(q + 1) * 512], ps[:, (q % 2) * 2 + c, :])
                last.then_inc(s_xnT, 1)
                act.wait_ge(s_xd, 2 * q + 1)
                act.copy(dtT[:, q * 512:(q + 1) * 512], ps[:, 4 + (2 * q) % 4, :]).then_inc(s_xdc, 1)
                act.wait_ge(s_xd, 2 * q + 2)
                act.copy(bcT[:, q * 512:(q + 1) * 512], ps[0:2 * STATES, 4 + (2 * q + 1) % 4, :]).then_inc(s_xdc, 1)
            for b in range(BATCH):
                if b:
                    act.wait_ge(s_w0, 1)
                    act.activation(R0.weight[:, :, 1], R0.weight[:, :, 0], ACT.Exp).then_inc(s_w0, 1)
                    act.wait_ge(s_sp, 10)
                for c in range(DC):
                    for q in range(2):
                        m = b * 4 + c * 2 + q
                        act.wait_ge(s_dp, m + 1)
                        act.activation(sp_x[:, c * SEQ + q * 512:c * SEQ + (q + 1) * 512], ps[:, m % 4, :], ACT.Identity,
                                       bias=dtb[:, c:c + 1]).then_inc(s_dpc, 1)
                act.wait_ge(s_dpc, 5 * (b + 1) - 1)
                act.activation(sp_e, sp_x, ACT.Abs).then_inc(s_dpc, 1)
                act.wait_ge(s_dpc, 5 * (b + 1))
                act.activation(sp_e, sp_e, ACT.Exp, scale=-1.0).then_inc(s_spa, 1)
            act.wait_ge(s_delta, 2)
            act.wait_ge(s_aneg, 2)
            for b in range(BATCH):
                with act.Fori(0, STATES // 2) as j:
                    for q in range(2):
                        it = b * STATES + j * 2 + q
                        act.wait_ge(s_hc, it + 1)
                        for c in range(DC):
                            last = act.activation(decay[:, q, c, 1:SEQ], delta[:, c, b * SEQ + 1:(b + 1) * SEQ], ACT.Exp,
                                                  scale=aneg[:, c, bass.ds(j * 2 + q, 1)])
                        last.then_inc(s_dec, 1)
            experts_act(act, R0)
            for q in range(NG):
                act.wait_ge(s_xnT1_ps, q + 1)
                for c in range(DC):
                    last = act.copy(xnT1[:, c, q * 512:(q + 1) * 512], ps[:, (q % 2) * 2 + c, :])
                last.then_inc(s_xnT1, 1)
            act.wait_ge(s_par1, 64)
            act.activation(gsc[:], gsc[:], ACT.Exp, scale=-1.0).then_inc(s_gact, 1)
            att_act(act)
            experts_act(act, R1)

        @block.tensor
        def _(pe):
            pe.wait_ge(s_const, N_CONST)
            for q in range(NG):
                pe.wait_ge(s_xn, q + 1)
                if q >= 2:
                    pe.wait_ge(s_xnT, q - 1)
                for c in range(DC):
                    for i in range(GT):
                        last = pe.transpose(ps[:, (q % 2) * 2 + c, i * P:(i + 1) * P], xn[:, q * GT + i, c * P:(c + 1) * P], ident[:])
                last.then_inc(s_xnT_ps, 1)
                if q == 0:
                    pe.wait_ge(s_par, 96)
                pe.wait_ge(s_xnT, q + 1)
                for w in range(2):
                    n = 2 * q + w
                    if n >= 4:
                        pe.wait_ge(s_xdc, n - 3)
                    rows = P if w == 0 else 2 * STATES
                    for c in range(DC):
                        last = pe.matmul(ps[0:rows, 4 + n % 4, :], xpw[:, c, w * P:w * P + rows], xnT[:, c, q * 512:(q + 1) * 512],
                                         start=c == 0, stop=c == DC - 1)
                    last.then_inc(s_xd, 1)
            pe.wait_ge(s_xdc, 8)
            for b in range(BATCH):
                for c in range(DC):
                    for q in range(2):
                        m = b * 4 + c * 2 + q
                        if m >= 4:
                            pe.wait_ge(s_dpc, m - 3)
                        pe.matmul(ps[:, m % 4, :], dtw[:, c * P:(c + 1) * P], dtT[:, b * SEQ + q * 512:b * SEQ + (q + 1) * 512],
                                  start=True, stop=True).then_inc(s_dp, 1)
                if b == 0:
                    for i in range(NT):
                        for c in range(DC):
                            last = pe.matmul(ps[:, 4 + i // 8, (i % 8) * E0:(i % 8 + 1) * E0], xnT[:, c, i * P:(i + 1) * P],
                                             rw0[:, c, :], start=c == 0, stop=c == DC - 1)
                    last.then_inc(R0.logits_ready, 1)
            route_pe(pe, R0)
            pe.wait_ge(s_dpc, 10)
            for q in range(4):
                last = pe.matmul(ps[:, q, :], ident[:], zeros[:, 0:512], start=True, stop=False, skip_group_check=True)
            last.then_inc(s_ysum, 2)
            for b in range(BATCH):
                if b:
                    pe.wait_ge(s_yT, b)
                    for q in range(4):
                        last = pe.matmul(ps[:, q, :], ident[:], zeros[:, 0:512], start=True, stop=False, skip_group_check=True)
                with pe.Fori(0, STATES // 2) as j:
                    for q in range(2):
                        pe.wait_ge(s_hc, 2 + b * STATES + j * 2 + q + 1)
                        for c in range(DC):
                            for h in range(2):
                                last = pe.matmul(ps[:, 2 * c + h, :], ident[:], hc[:, q, c, h * 512:(h + 1) * 512],
                                                 start=False, stop=True, skip_group_check=True)
                        last.then_inc(s_ysum, 1)
            pe.wait_ge(s_yT, 2)
            for i in range(NT // 2):
                if i >= 2:
                    pe.wait_ge(s_yadd, i - 1)
                for a in range(2):
                    for c in range(DC):
                        tt = 2 * i + a
                        last = pe.transpose(ps[:, i % 2, a * D + c * P:a * D + (c + 1) * P], delta[:, c, tt * P:(tt + 1) * P], ident[:])
                last.then_inc(s_yT_ps, 1)
            experts_pe(pe, R0)
            for q in range(NG):
                pe.wait_ge(s_xn, NG + q + 1)
                if q >= 2:
                    pe.wait_ge(s_xnT1, q - 1)
                for c in range(DC):
                    for i in range(GT):
                        last = pe.transpose(ps[:, (q % 2) * 2 + c, i * P:(i + 1) * P], xn[:, q * GT + i, c * P:(c + 1) * P], ident[:])
                last.then_inc(s_xnT1_ps, 1)
            pe.wait_ge(s_xnT1, NG)
            pe.wait_ge(s_par1, 64)
            for i in range(NT):
                for c in range(DC):
                    last = pe.matmul(ps[:, 4 + i // 8, (i % 8) * (E1 + 1):(i % 8 + 1) * (E1 + 1)], xnT1[:, c, i * P:(i + 1) * P],
                                     rw1[:, c, :], start=c == 0, stop=c == DC - 1)
            last.then_inc(R1.logits_ready, 1)
            att_pe(pe)
            experts_pe(pe, R1)


def layouts(v):
    c = np.ascontiguousarray

    def feat(w):
        return c(w.reshape(DC, P, -1).transpose(1, 0, 2))

    def w13_of(gate, up):
        w = np.concatenate([gate, up], axis=1).transpose(0, 2, 1)
        return c(w.reshape(-1, DC, P, 2 * INNER).transpose(0, 2, 1, 3))

    def w2_of(w):
        return c(w.transpose(0, 2, 1).reshape(-1, 2, IC, D).transpose(0, 2, 1, 3))

    se_g, se_u = v['L1_ffn_se_gate_up_w'][:SHARED * INNER], v['L1_ffn_se_gate_up_w'][SHARED * INNER:]
    w13l1 = np.concatenate([v['L1_ffn_w13'], np.concatenate([se_g.reshape(SHARED, INNER, D), se_u.reshape(SHARED, INNER, D)], axis=1)])
    w2l1 = np.concatenate([v['L1_ffn_w2'], v['L1_ffn_se_down_w'].reshape(D, SHARED, INNER).transpose(1, 0, 2)])

    def heads(w, n):
        return w.reshape(DC, P, HEADS, n).transpose(2, 1, 0, 3)
    q = np.concatenate([heads(v['L1_attn_wq_sem'], QK), heads(v['L1_attn_wq_geo'], QK)], axis=3)
    k = np.concatenate([heads(v['L1_attn_wk_sem'], QK), heads(v['L1_attn_wk_geo'], QK)], axis=3)
    wv = heads(v['L1_attn_wv'], P)
    half = QK // 2
    inv = (1.0 / 10000.0 ** (np.arange(half, dtype=np.float32) / np.float32(half))).astype(np.float32)
    ang = inv[:, None] * np.arange(SEQ, dtype=np.float32)[None]
    cos, sin = np.cos(ang).astype(np.float32), np.sin(ang).astype(np.float32)
    rope = np.stack([np.concatenate([np.ones((QK, SEQ), np.float32), cos, cos]),
                     np.concatenate([np.zeros((QK, SEQ), np.float32), -sin, sin])], axis=1)
    return {
        'x': c(v['L0_attn_x'].reshape(T, D)), 'a_log': feat(v['L0_attn_A_log']), 'd_param': c(v['L0_attn_D_param'].reshape(DC, P).T),
        'xproj': feat(v['L0_attn_x_proj_w'].T), 'dtproj': c(v['L0_attn_dt_proj_w'].T), 'dt_bias': c(v['L0_attn_dt_proj_b'].reshape(DC, P).T),
        'router0': feat(v['L0_ffn_router_w'].T), 'w13_0': w13_of(v['L0_ffn_gate_w'], v['L0_ffn_up_w']), 'w2_0': w2_of(v['L0_ffn_down_w']),
        'router1': feat(np.concatenate([v['L1_ffn_gate_w'], v['L1_ffn_shared_gate_w']]).T),
        'w13_1': w13_of(w13l1[:, :INNER], w13l1[:, INNER:]), 'w2_1': w2_of(w2l1),
        'wqkv': c(np.stack([q, k, wv], axis=2)), 'wo_h': c(v['L1_attn_wo'].reshape(HEADS, P, D)),
        'gate_logit': c(v['L1_attn_gate_logit'].reshape(1, HEADS)), 'rope': c(rope),
    }


def kernel(**inputs):
    import concourse.bacc as _bacc
    from concourse.bass_utils import run_bass_kernel_spmd as _run

    nc = _bacc.Bacc("TRN2", target_bir_lowering=False, num_devices=1)
    arrays, args = {}, []
    for name, a in layouts({k: np.asarray(a) for k, a in inputs.items()}).items():
        arrays[f"in_{name}"] = a
        args.append(nc.dram_tensor(f"in_{name}", a.shape, mybir.dt.from_np(a.dtype), kind="ExternalInput").ap())
    args.append(nc.dram_tensor("out_0", (T, D), F32, kind="ExternalOutput").ap())
    build(nc, *args)
    r = _run(nc, [arrays], core_ids=[0])
    return r.results[0]["out_0"].reshape(BATCH, SEQ, D)
```
